# Optimizing a Trainium2 kernel written in Bass

```python
import numpy as np
import jax
import jax.numpy as jnp

def _softmax(x, axis=-1):
    return jax.nn.softmax(x, axis=axis)

def _gelu(x):
    return jax.nn.gelu(x, approximate=True)

def _silu(x):
    return jax.nn.silu(x)

def _sigmoid(x):
    return jax.nn.sigmoid(x)

def _layernorm(x, axis=-1, eps=1e-05):
    m = jnp.mean(x, axis=axis, keepdims=True)
    v = jnp.var(x, axis=axis, keepdims=True)
    return (x - m) / jnp.sqrt(v + eps)

def _scatter_add(tgt, idx, src, axis=0):
    return tgt.at[idx].add(src)

def _segment_sum(src, seg, n):
    return jax.ops.segment_sum(src, seg, n)
kernel_name = 'mk_gnn_resnorm_d2_gnn_r8_9c9253'

def setup_inputs(seed: int=0):
    np.random.seed(seed)
    _w = jnp.asarray

    def _rec_inputs():
        import jax
        import jax.numpy as jnp
        _gk = jax.random.key(seed)
        x = -8.776e-05 + 1 * jax.random.normal(jax.random.fold_in(_gk, 1), (2500, 256), jnp.float32)
        _s = jax.random.randint(jax.random.fold_in(_gk, 2), (40000,), 0, 2500, jnp.int32)
        _d = jax.random.randint(jax.random.fold_in(_gk, 3), (40000,), 0, 2500, jnp.int32)
        _loop = jnp.arange(2500, dtype=jnp.int32)
        src = jnp.concatenate([_s, _d, _loop])
        dst = jnp.concatenate([_d, _s, _loop])
        _o = jnp.argsort(dst, stable=True)
        src = src[_o]
        dst = dst[_o]
        edge_attr_3 = 0.00047201 + 1.00023 * jax.random.normal(jax.random.fold_in(_gk, 11), (82500, 3), jnp.float32)
        edge_attr_64 = 1.36993e-05 + 0.999972 * jax.random.normal(jax.random.fold_in(_gk, 12), (82500, 64), jnp.float32)
        edge_attr_8 = jax.random.uniform(jax.random.fold_in(_gk, 13), (82500, 8), jnp.float32, 0.0, 0.999999)
        edge_weight = jax.random.uniform(jax.random.fold_in(_gk, 15), (82500,), jnp.float32, 0.0, 0.999998)
        return (x, src, dst, edge_attr_3, edge_attr_64, edge_attr_8, edge_weight)
    x, src, dst, edge_attr_3, edge_attr_64, edge_attr_8, edge_weight = _rec_inputs()

    def _L0_gnn_setup():
        import jax, jax.numpy as jnp
        import numpy as np
        MUL = 64
        NN = 2500
        NE = 40000
        NB = 8
        NH = 64
        NPATH = 5
        AVG_NEIGH = 16.0
        key = jax.random.key(seed)
        ks = jax.random.split(key, 8)
        return {'node_features': jax.random.normal(ks[0], (NN, 4 * MUL), jnp.float32), 'edge_vectors': jax.random.normal(ks[1], (NE, 3), jnp.float32), 'edge_lengths_embedding': jax.random.uniform(ks[2], (NE, NB), dtype=jnp.float32), 'fc_w1': jax.random.normal(ks[3], (NB, NH), jnp.float32), 'fc_w2': jax.random.normal(ks[4], (NH, NPATH * MUL), jnp.float32), 'lin_w0': jax.random.normal(ks[5], (MUL, MUL), jnp.float32), 'lin_w1': jax.random.normal(ks[6], (MUL, MUL), jnp.float32), 'edge_index': jax.random.randint(ks[7], (2, NE), 0, NN, dtype=jnp.int32)}
    _L0_gnn_all = _L0_gnn_setup()
    _L0_gnn_in = {k: v for k, v in _L0_gnn_all.items() if k in ('fc_w1', 'fc_w2', 'lin_w0', 'lin_w1')}
    del _L0_gnn_all

    def _L1_gnn_setup():
        import jax, jax.numpy as jnp
        import numpy as np
        N = 2500
        E = 40000
        D = 256
        H = 8
        DH = D // H
        ED = 64
        FF = 4 * D
        EPS = 1e-05

        def _layernorm(x, g, b):
            m = jnp.mean(x, axis=-1, keepdims=True)
            v = jnp.var(x, axis=-1, keepdims=True)
            return (x - m) * jax.lax.rsqrt(v + EPS) * g + b

        def _edge_attention(xn, edge_index, ef, ew, Wq, bq, Wk, bk, Wv, bv, We, be, Wo, bo):
            n = xn.shape[0]
            scale = DH ** (-0.5)
            q = (xn @ Wq + bq).reshape(n, H, DH)
            k = (xn @ Wk + bk).reshape(n, H, DH)
            v = (xn @ Wv + bv).reshape(n, H, DH)
            src, dst = (edge_index[0], edge_index[1])
            ep = ef @ We + be
            scores = jnp.einsum('ehd,ehd->eh', q[dst], k[src] + ep[:, None, :]) * scale
            scores = scores * ew[:, None]
            m = jax.ops.segment_max(scores, dst, num_segments=n)
            m = jnp.where(jnp.isfinite(m), m, 0.0)
            ex = jnp.exp(scores - m[dst])
            s = jax.ops.segment_sum(ex, dst, num_segments=n)
            attn = ex / s[dst]
            out = jax.ops.segment_sum(attn[:, :, None] * v[src], dst, num_segments=n)
            out = out.reshape(n, D) @ Wo + bo
            return out
        key = jax.random.key(seed)
        ks = jax.random.split(key, 32)

        def lin_w(k, i, o):
            return (jax.random.normal(k, (i, o), jnp.float32) / np.sqrt(i)).astype(jnp.float32)
        return {'x': jax.random.normal(ks[0], (N, D), jnp.float32), 'edge_features': jax.random.normal(ks[1], (E, ED), jnp.float32), 'edge_weights': jax.random.uniform(ks[2], (E,), jnp.float32), 'edge_index': jax.random.randint(ks[3], (2, E), 0, N, dtype=jnp.int32), 'Wq': lin_w(ks[4], D, D), 'bq': jnp.zeros((D,), jnp.float32), 'Wk': lin_w(ks[5], D, D), 'bk': jnp.zeros((D,), jnp.float32), 'Wv': lin_w(ks[6], D, D), 'bv': jnp.zeros((D,), jnp.float32), 'We': lin_w(ks[7], ED, DH), 'be': jnp.zeros((DH,), jnp.float32), 'Wo': lin_w(ks[8], D, D), 'bo': jnp.zeros((D,), jnp.float32), 'ln1_g': jnp.ones((D,), jnp.float32), 'ln1_b': jnp.zeros((D,), jnp.float32), 'ln2_g': jnp.ones((D,), jnp.float32), 'ln2_b': jnp.zeros((D,), jnp.float32), 'W1': lin_w(ks[9], D, FF), 'b1': jnp.zeros((FF,), jnp.float32), 'W2': lin_w(ks[10], FF, D), 'b2': jnp.zeros((D,), jnp.float32), 'alpha': jnp.ones((1,), jnp.float32), 'beta': jnp.ones((1,), jnp.float32)}
    _L1_gnn_all = _L1_gnn_setup()
    _L1_gnn_in = {k: v for k, v in _L1_gnn_all.items() if k in ('Wq', 'bq', 'Wk', 'bk', 'Wv', 'bv', 'We', 'be', 'Wo', 'bo', 'ln1_g', 'ln1_b', 'ln2_g', 'ln2_b', 'W1', 'b1', 'W2', 'b2', 'alpha', 'beta')}
    del _L1_gnn_all
    return {'x': x, 'src': src, 'dst': dst, 'edge_attr_3': edge_attr_3, 'edge_attr_64': edge_attr_64, 'edge_attr_8': edge_attr_8, 'edge_weight': edge_weight, 'L0_gnn_fc_w1': _L0_gnn_in['fc_w1'], 'L0_gnn_fc_w2': _L0_gnn_in['fc_w2'], 'L0_gnn_lin_w0': _L0_gnn_in['lin_w0'], 'L0_gnn_lin_w1': _L0_gnn_in['lin_w1'], 'L1_gnn_Wq': _L1_gnn_in['Wq'], 'L1_gnn_bq': _L1_gnn_in['bq'], 'L1_gnn_Wk': _L1_gnn_in['Wk'], 'L1_gnn_bk': _L1_gnn_in['bk'], 'L1_gnn_Wv': _L1_gnn_in['Wv'], 'L1_gnn_bv': _L1_gnn_in['bv'], 'L1_gnn_We': _L1_gnn_in['We'], 'L1_gnn_be': _L1_gnn_in['be'], 'L1_gnn_Wo': _L1_gnn_in['Wo'], 'L1_gnn_bo': _L1_gnn_in['bo'], 'L1_gnn_ln1_g': _L1_gnn_in['ln1_g'], 'L1_gnn_ln1_b': _L1_gnn_in['ln1_b'], 'L1_gnn_ln2_g': _L1_gnn_in['ln2_g'], 'L1_gnn_ln2_b': _L1_gnn_in['ln2_b'], 'L1_gnn_W1': _L1_gnn_in['W1'], 'L1_gnn_b1': _L1_gnn_in['b1'], 'L1_gnn_W2': _L1_gnn_in['W2'], 'L1_gnn_b2': _L1_gnn_in['b2'], 'L1_gnn_alpha': _L1_gnn_in['alpha'], 'L1_gnn_beta': _L1_gnn_in['beta']}

def reference(x, src, dst, edge_attr_3, edge_attr_64, edge_attr_8, edge_weight, L0_gnn_fc_w1, L0_gnn_fc_w2, L0_gnn_lin_w0, L0_gnn_lin_w1, L1_gnn_Wq, L1_gnn_bq, L1_gnn_Wk, L1_gnn_bk, L1_gnn_Wv, L1_gnn_bv, L1_gnn_We, L1_gnn_be, L1_gnn_Wo, L1_gnn_bo, L1_gnn_ln1_g, L1_gnn_ln1_b, L1_gnn_ln2_g, L1_gnn_ln2_b, L1_gnn_W1, L1_gnn_b1, L1_gnn_W2, L1_gnn_b2, L1_gnn_alpha, L1_gnn_beta):
    import jax
    import jax.numpy as jnp

    def _L0_gnn_ref(node_features, edge_vectors, edge_lengths_embedding, fc_w1, fc_w2, lin_w0, lin_w1, edge_index):
        import jax, jax.numpy as jnp
        import numpy as np
        MUL = 64
        NN = 2500
        NE = 40000
        NB = 8
        NH = 64
        NPATH = 5
        AVG_NEIGH = 16.0
        sender, receiver = (edge_index[0], edge_index[1])
        r = jnp.linalg.norm(edge_vectors, axis=-1, keepdims=True)
        sh1 = jnp.sqrt(jnp.asarray(3.0, edge_vectors.dtype)) * edge_vectors / (r + 1e-09)
        h = jax.nn.silu(edge_lengths_embedding @ fc_w1 / np.sqrt(NB))
        w = (h @ fc_w2 / np.sqrt(NH)).reshape(-1, NPATH, MUL)
        s = node_features[:, :MUL][sender]
        v = node_features[:, MUL:].reshape(-1, MUL, 3)[sender]
        dot = jnp.einsum('eui,ei->eu', v, sh1)
        crs = jnp.cross(v, sh1[:, None, :])
        inv_sqrt2 = 1.0 / np.sqrt(2.0)
        inv_sqrt3 = 1.0 / np.sqrt(3.0)
        m0 = (w[:, 0] * s + w[:, 3] * dot * inv_sqrt3) * inv_sqrt2
        m1 = (w[:, 1, :, None] * s[:, :, None] * sh1[:, None, :] + w[:, 2, :, None] * v + w[:, 4, :, None] * crs * inv_sqrt2) * inv_sqrt3
        agg0 = jax.ops.segment_sum(m0, receiver, num_segments=NN) / AVG_NEIGH
        agg1 = jax.ops.segment_sum(m1.reshape(-1, MUL * 3), receiver, num_segments=NN).reshape(-1, MUL, 3) / AVG_NEIGH
        out0 = agg0 @ lin_w0 / np.sqrt(MUL)
        out1 = jnp.einsum('nui,uv->nvi', agg1, lin_w1) / np.sqrt(MUL)
        upd = jnp.concatenate([out0, out1.reshape(-1, MUL * 3)], axis=-1)
        return upd + node_features

    def _L1_gnn_ref(x, edge_features, edge_weights, edge_index, Wq, bq, Wk, bk, Wv, bv, We, be, Wo, bo, ln1_g, ln1_b, ln2_g, ln2_b, W1, b1, W2, b2, alpha, beta):
        import jax, jax.numpy as jnp
        import numpy as np
        N = 2500
        E = 40000
        D = 256
        H = 8
        DH = D // H
        ED = 64
        FF = 4 * D
        EPS = 1e-05

        def _layernorm(x, g, b):
            m = jnp.mean(x, axis=-1, keepdims=True)
            v = jnp.var(x, axis=-1, keepdims=True)
            return (x - m) * jax.lax.rsqrt(v + EPS) * g + b

        def _edge_attention(xn, edge_index, ef, ew, Wq, bq, Wk, bk, Wv, bv, We, be, Wo, bo):
            n = xn.shape[0]
            scale = DH ** (-0.5)
            q = (xn @ Wq + bq).reshape(n, H, DH)
            k = (xn @ Wk + bk).reshape(n, H, DH)
            v = (xn @ Wv + bv).reshape(n, H, DH)
            src, dst = (edge_index[0], edge_index[1])
            ep = ef @ We + be
            scores = jnp.einsum('ehd,ehd->eh', q[dst], k[src] + ep[:, None, :]) * scale
            scores = scores * ew[:, None]
            m = jax.ops.segment_max(scores, dst, num_segments=n)
            m = jnp.where(jnp.isfinite(m), m, 0.0)
            ex = jnp.exp(scores - m[dst])
            s = jax.ops.segment_sum(ex, dst, num_segments=n)
            attn = ex / s[dst]
            out = jax.ops.segment_sum(attn[:, :, None] * v[src], dst, num_segments=n)
            out = out.reshape(n, D) @ Wo + bo
            return out
        xn = _layernorm(x, ln1_g, ln1_b)
        attn_out = _edge_attention(xn, edge_index, edge_features, edge_weights, Wq, bq, Wk, bk, Wv, bv, We, be, Wo, bo)
        x = x + alpha * attn_out
        xn = _layernorm(x, ln2_g, ln2_b)
        ff = jax.nn.gelu(xn @ W1 + b1, approximate=False) @ W2 + b2
        x = x + beta * ff
        return x
    edge_index = jnp.stack([src, dst])
    x = _layernorm(x + _L0_gnn_ref(x, edge_attr_3, edge_attr_8, L0_gnn_fc_w1, L0_gnn_fc_w2, L0_gnn_lin_w0, L0_gnn_lin_w1, edge_index), axis=-1)
    x = _layernorm(x + _L1_gnn_ref(x, edge_attr_64, edge_weight, edge_index, L1_gnn_Wq, L1_gnn_bq, L1_gnn_Wk, L1_gnn_bk, L1_gnn_Wv, L1_gnn_bv, L1_gnn_We, L1_gnn_be, L1_gnn_Wo, L1_gnn_bo, L1_gnn_ln1_g, L1_gnn_ln1_b, L1_gnn_ln2_g, L1_gnn_ln2_b, L1_gnn_W1, L1_gnn_b1, L1_gnn_W2, L1_gnn_b2, L1_gnn_alpha, L1_gnn_beta), axis=-1)
    return x

_drawn_inputs = setup_inputs


def setup_inputs(seed=0):
    import zlib

    import numpy as np

    out = dict(_drawn_inputs(seed))
    spreads = {'L1_gnn_bq': (0.0, 0.55),
     'L1_gnn_bk': (0.0, 0.8),
     'L1_gnn_bv': (0.0, 0.1),
     'L1_gnn_be': (0.0, 0.8),
     'L1_gnn_bo': (0.0, 0.1),
     'L1_gnn_ln1_g': (1.0, 0.2),
     'L1_gnn_ln1_b': (0.0, 0.1),
     'L1_gnn_ln2_g': (1.0, 0.2),
     'L1_gnn_ln2_b': (0.0, 0.1),
     'L1_gnn_b1': (0.0, 0.1),
     'L1_gnn_b2': (0.0, 0.1)}
    factors = {}
    for name, (base, spread) in spreads.items():
        noise = np.random.default_rng([zlib.crc32(name.encode()), seed]).standard_normal(out[name].shape)
        drawn = base * np.exp(spread * noise) if base else spread * noise
        out[name] = jnp.asarray(drawn.astype(out[name].dtype))
    for name, factor in factors.items():
        out[name] = (out[name] * factor).astype(out[name].dtype)
    return out
```

```python
from contextlib import ExitStack

import numpy as np

import concourse.bass as bass
from concourse import mybir

F32 = mybir.dt.float32
BF16 = mybir.dt.bfloat16
I32 = mybir.dt.int32
ALU = mybir.AluOpType
ACT = mybir.ActivationFunctionType
AX = mybir.AxisListType

P = 128
NODES = 2500
EDGES = 82500
MUL = 64
D = 4 * MUL
HEADS = 8
DH = D // HEADS
ED = 64
NB = 8
NH = 64
NPATH = 5
FF = 4 * D
EPS = 1e-5
AVG_NEIGH = 16.0

WINDOWS = -(-NODES // P)
CHUNKS = 4
SUPER = CHUNKS * P
BLOCKS = P // HEADS
COLS = -(-(-(-EDGES // P)) // BLOCKS) * BLOCKS
GROUPS = COLS // BLOCKS
BLOCK_EDGES = GROUPS * P
SUPERS = COLS // CHUNKS
EDGES_PAD = COLS * P
NODES_PAD = WINDOWS * P
SPAN = 32
IDLE = WINDOWS
TABLE = -(-(SUPERS * WINDOWS + 4) // 512) * 512
FAR = 4096.0
NEG = -1.0e30
TINY = 1.0e-30


class Held:
    pass


def semaphores(nc, ctx, names):
    return [ctx.enter_context(nc.semaphore(n)) for n in names.split()]


def step_of(nc, eng, code_row, i):
    code = eng.value_load(code_row[0:1, bass.ds(i, 1)], min_val=0, max_val=(SUPERS - 1) * SPAN + IDLE)
    sc = nc.s_assert_within(eng.snap(code // SPAN), 0, SUPERS - 1,
                            skip_runtime_bounds_check_because="a step's code holds a super-chunk's number")
    w = nc.s_assert_within(eng.snap(code % SPAN), 0, IDLE,
                           skip_runtime_bounds_check_because="a step's code holds a window's number")
    return sc, w


def stage_tables(nc, g):
    with ExitStack() as ctx:
        def sb(name, shape, dt=F32):
            return ctx.enter_context(nc.sbuf_tensor(name, shape, dt))

        dst_i = sb("dst_i", [P, COLS], I32)
        win_i = sb("win_i", [P, COLS], I32)
        win_f = sb("win_f", [P, COLS])
        pad_far = sb("pad_far", [P, COLS])
        vec = sb("vec", [P, COLS, 3])
        vec2 = sb("vec2", [P, COLS, 3])
        length = sb("length", [P, COLS])
        inv_len = sb("inv_len", [P, COLS])
        win_hi = sb("win_hi", [P, SUPERS])
        win_lo = sb("win_lo", [P, SUPERS])
        hi = sb("hi", [P, 2])
        lo = sb("lo", [P, 2])
        count = sb("count", [P, 2])
        count0 = sb("count0", [P, 2])
        has = sb("has", [P, 2])
        first = sb("first", [P, 2])
        after = sb("after", [P, 2])
        code_of = sb("code_of", [P, 2])
        upper = sb("upper", [P, P])
        iota_step = sb("iota_step", [P, TABLE])
        from_first = sb("from_first", [P, 2, 512])
        member = sb("member", [P, 2, 512])
        code_t = sb("code_t", [1, 512])
        total = sb("total", [1, 2])
        total1 = sb("total1", [1, 1])
        total_i = sb("total_i", [1, 1], I32)
        ps_t = ctx.enter_context(nc.psum_tensor("ps_t", [P, 2, 512], F32))
        ps_n = ctx.enter_context(nc.psum_tensor("ps_n", [P, 512], F32))
        ps_c = ctx.enter_context(nc.psum_tensor("ps_c", [1, 2, 2, 512], F32))
        (t_dst, t_vec, t_ew, t_x, t_w, t_const, t_turn, t_dve, t_len, t_act, t_pe, t_mem, t_code, t_lin) = semaphores(nc, ctx, "t_dst t_vec t_ew t_x t_w t_const t_turn t_dve t_len t_act t_pe t_mem t_code t_lin")
        block = ctx.enter_context(nc.Block())

        @block.sync
        def _(sp):
            sp.dma_start(dst_i[:], g.dst_t).then_inc(t_dst, 16)
            sp.dma_start(vec[:], g.vec_t).then_inc(t_vec, 16)
            sp.dma_start(g.src_i[:], g.src_t).then_inc(t_x, 16)
            sp.dma_start(g.ew[:], g.ew_t).then_inc(t_ew, 16)
            sp.dma_start(g.w1[:], g.fc_w1).then_inc(t_w, 16)
            for path, place in enumerate((0, 4, 2, 1, 3)):
                sp.dma_start(g.w2[:, place * MUL:(place + 1) * MUL],
                             g.fc_w2[:, path * MUL:(path + 1) * MUL]).then_inc(t_w, 16)
            sp.wait_ge(t_x, 16)
            sp.wait_ge(t_ew, 16)

        @block.gpsimd
        def _(pool):
            pool.iota(iota_step[:], [[1, TABLE]], base=0, channel_multiplier=0,
                      allow_small_or_imprecise_dtypes=True).then_inc(t_const, 1)
            pool.iota(g.iota_node[:], [[1, (WINDOWS + 1) * P]], base=0, channel_multiplier=0,
                      allow_small_or_imprecise_dtypes=True).then_inc(t_const, 1)
            pool.iota(first[:], [[P, 2]], base=0, channel_multiplier=1,
                      allow_small_or_imprecise_dtypes=True).then_inc(t_const, 1)
            pool.memset(g.ident[:], 0.0).then_inc(t_const, 1)
            pool.memset(upper[:], 1.0).then_inc(t_const, 1)
            pool.memset(g.ones[:], 1.0).then_inc(t_const, 1)
            pool.memset(g.acc[:], 0.0).then_inc(t_const, 1)
            pool.memset(g.lin[:], 0.0).then_inc(t_const, 1)
            pool.wait_ge(t_const, 8)
            pool.affine_select(out=g.ident[:], in_=g.ident[:], compare_op=ALU.not_equal, fill=1.0, base=0,
                               pattern=[[-1, P]], channel_multiplier=1).then_inc(t_const, 1)
            pool.affine_select(out=upper[:], in_=upper[:], compare_op=ALU.is_ge, fill=0.0, base=0,
                               pattern=[[1, P]], channel_multiplier=-1).then_inc(t_const, 1)
            pool.dma_start(g.lin[0:64, 0, 0:64], g.lin_w0).then_inc(t_lin, 16)
            pool.dma_start(g.lin[64:128, 0, 64:128], g.lin_w1).then_inc(t_lin, 16)
            pool.dma_start(g.lin[0:64, 1, 0:64], g.lin_w1).then_inc(t_lin, 16)
            pool.dma_start(g.lin[64:128, 1, 64:128], g.lin_w1).then_inc(t_lin, 16)
            pool.wait_ge(t_lin, 64)

        @block.scalar
        def _(act):
            act.wait_ge(t_len, 1)
            act.activation(length[:], length[:], ACT.Sqrt).then_inc(t_act, 1)

        @block.tensor
        def _(pe):
            pe.wait_ge(t_const, 10)
            pe.wait_ge(t_turn, 2)
            pe.transpose(ps_t[:, 0, 0:128], win_hi[:, 0:128], g.ident[:])
            pe.transpose(ps_t[0:SUPERS - 128, 0, 128:256], win_hi[:, 128:SUPERS], g.ident[:])
            pe.transpose(ps_t[:, 1, 0:128], win_lo[:, 0:128], g.ident[:])
            pe.transpose(ps_t[0:SUPERS - 128, 1, 128:256], win_lo[:, 128:SUPERS], g.ident[:]).then_inc(t_pe, 1)
            pe.wait_ge(t_turn, 3)
            pe.matmul(ps_n[:, 0:2], upper[:], count[:], start=True, stop=False)
            pe.matmul(ps_n[:, 0:2], g.ones[:], count0[:], start=False, stop=True)
            pe.matmul(ps_n[0:1, 4:6], g.ones[:, 0:1], count[:], start=True, stop=True,
                      skip_group_check=True).then_inc(t_pe, 1)
            for b in range(TABLE // 512):
                pe.wait_ge(t_mem, b + 1)
                if b >= 2:
                    pe.wait_ge(t_code, b - 1)
                for row, lhs in ((0, code_of), (1, g.ones)):
                    for c in range(2):
                        mm = pe.matmul(ps_c[:, b % 2, row, :], lhs[:, c:c + 1], member[:, c, :],
                                       start=(c == 0), stop=(c == 1))
                mm.then_inc(t_pe, 1)

        @block.vector
        def _(dve):
            done = [0]

            def then(ins):
                done[0] += 1
                ins.then_inc(t_dve, 1)
                dve.wait_ge(t_dve, done[0])

            dve.wait_ge(t_dst, 16)
            then(dve.tensor_scalar(win_i[:], dst_i[:], 7, None, ALU.arith_shift_right))
            then(dve.tensor_copy(win_f[:], win_i[:]))
            then(dve.tensor_scalar(pad_far[:], win_f[:], 0.0, -FAR, ALU.is_lt, ALU.mult))
            then(dve.scalar_tensor_tensor(pad_far[:], win_f[:], -1.0, pad_far[:], ALU.mult, ALU.add))
            dve.tensor_reduce(win_hi[:], win_f[:].rearrange("p (s c) -> p s c", c=CHUNKS), AX.X,
                              ALU.max).then_inc(t_turn, 1)
            dve.tensor_reduce(win_lo[:], pad_far[:].rearrange("p (s c) -> p s c", c=CHUNKS), AX.X,
                              ALU.max).then_inc(t_turn, 1)
            dve.tensor_copy(g.rec[:, :, 0], dst_i[:])
            dve.wait_ge(t_vec, 16)
            then(dve.tensor_tensor(vec2[:], vec[:], vec[:], ALU.mult))
            dve.tensor_reduce(length[:], vec2[:], AX.X, ALU.add).then_inc(t_len, 1)
            dve.memset(g.code_before[:, 0:1], IDLE)
            dve.memset(hi[:], -1.0)
            dve.memset(count0[:], 0.0)
            then(dve.memset(lo[:], -FAR))
            dve.wait_ge(t_pe, 1)
            rest = SUPERS - 128
            dve.tensor_reduce(hi[:, 0:1], ps_t[:, 0, 0:128], AX.X, ALU.max)
            dve.tensor_reduce(hi[0:rest, 1:2], ps_t[0:rest, 0, 128:256], AX.X, ALU.max)
            dve.tensor_reduce(lo[:, 0:1], ps_t[:, 1, 0:128], AX.X, ALU.max)
            then(dve.tensor_reduce(lo[0:rest, 1:2], ps_t[0:rest, 1, 128:256], AX.X, ALU.max))
            then(dve.tensor_tensor(count[:], hi[:], lo[:], ALU.add))
            then(dve.tensor_scalar(count[:], count[:], 1.0, 0.0, ALU.add, ALU.max))
            then(dve.tensor_scalar(has[:], count[:], 0.0, None, ALU.is_gt))
            dve.tensor_copy(count0[:, 1:2], count[:, 0:1]).then_inc(t_turn, 1)
            then(dve.tensor_tensor(lo[:], lo[:], has[:], ALU.mult))
            dve.wait_ge(t_const, 10)
            then(dve.tensor_scalar(code_of[:], first[:], float(SPAN), -float(IDLE), ALU.mult, ALU.add))
            then(dve.tensor_tensor(code_of[:], code_of[:], lo[:], ALU.subtract))
            dve.wait_ge(t_pe, 2)
            then(dve.tensor_copy(after[:], ps_n[:, 0:2]))
            then(dve.tensor_tensor(first[:], after[:], count[:], ALU.subtract))
            then(dve.tensor_tensor(code_of[:], code_of[:], first[:], ALU.subtract))
            then(dve.tensor_copy(total[:], ps_n[0:1, 4:6]))
            then(dve.tensor_tensor(total1[:], total[:, 0:1], total[:, 1:2], ALU.add))
            then(dve.tensor_scalar(total1[:], total1[:], 1.0, None, ALU.add))
            then(dve.tensor_copy(total_i[:], total1[:]))
            then(dve.tensor_scalar(g.pairs[:], total_i[:], 1, None, ALU.arith_shift_right))
            for b in range(TABLE // 512):
                cut = slice(b * 512, (b + 1) * 512)
                if b >= 1:
                    dve.wait_ge(t_pe, 2 + b)
                for c in range(2):
                    then(dve.tensor_scalar(from_first[:, c, :], iota_step[:, cut], first[:, c:c + 1], None,
                                           ALU.is_ge))
                    ins = dve.scalar_tensor_tensor(member[:, c, :], iota_step[:, cut], after[:, c:c + 1],
                                                   from_first[:, c, :], ALU.is_lt, ALU.mult)
                    if c == 1:
                        ins.then_inc(t_mem, 1)
                dve.wait_ge(t_pe, 3 + b)
                then(dve.tensor_tensor(code_t[:], ps_c[:, b % 2, 1, :], iota_step[0:1, cut], ALU.mult))
                done[0] += 1
                dve.scalar_tensor_tensor(code_t[:], ps_c[:, b % 2, 0, :], float(IDLE), code_t[:],
                                         ALU.add, ALU.add).then_inc(t_dve, 1)
                dve.wait_ge(t_dve, done[0])
                dve.tensor_copy(g.code[:, cut], code_t[:]).then_inc(t_code, 1)
                dve.wait_ge(t_code, b + 1)
            dve.wait_ge(t_act, 1)
            then(dve.tensor_scalar(length[:], length[:], 1e-9, None, ALU.add))
            then(dve.reciprocal(inv_len[:], length[:]))
            for j in range(3):
                dve.scalar_tensor_tensor(g.rec[:, :, 1 + j], vec[:, :, j], float(np.sqrt(3.0)), inv_len[:],
                                         ALU.mult, ALU.mult)
            dve.wait_ge(t_w, 16 * (1 + NPATH))
            dve.tensor_scalar(g.w1[:], g.w1[:], 1.0 / float(np.sqrt(NB)), None, ALU.mult)
            out = 1.0 / (np.sqrt(NH) * AVG_NEIGH * np.sqrt(MUL))
            r2, r3 = 1.0 / np.sqrt(2.0), 1.0 / np.sqrt(3.0)
            for path, scale in enumerate((r2, r3 * r2, r3, r3 * r2, r3)):
                cols = g.w2[:, path * MUL:(path + 1) * MUL]
                dve.tensor_scalar(cols, cols, float(out * scale), None, ALU.mult)


def stage_messages(nc, g):
    with ExitStack() as ctx:
        def sb(name, shape, dt=F32):
            return ctx.enter_context(nc.sbuf_tensor(name, shape, dt))

        emb = sb("emb", [NB, 2, SUPER])
        hid = sb("hid", [NH, 2, SUPER])
        idx = sb("idx", [P, 2, CHUNKS], I32)
        feat = sb("feat", [P, 2, CHUNKS, 2, 4, MUL])
        rec_a = sb("rec_a", [P, 2, CHUNKS, 4])
        rec_v = sb("rec_v", [P, 2, CHUNKS, 4])
        iota_w = sb("iota_w", [P, 2, P])
        vsh = sb("vsh", [P, 2, CHUNKS, 3, 4, MUL])
        hot = sb("hot", [P, 2, P])
        msg = sb("msg", [P, 2, 3, 4, MUL])
        ps_h = ctx.enter_context(nc.psum_tensor("ps_h", [NH, SUPER], F32))
        ps_w = ctx.enter_context(nc.psum_tensor("ps_w", [P, CHUNKS, 512], F32))
        ps_a = ctx.enter_context(nc.psum_tensor("ps_a", [P, 2, 512], F32))
        (m_emb0, m_emb1, m_emb_used, m_hps, m_hid, m_w, m_idx, m_ask, m_snd0, m_snd1, m_snd_used, m_reca,
         m_vsh, m_vsh_used, m_rec, m_dot, m_msg, m_used, m_clear, m_acc) = semaphores(nc, ctx, "m_emb0 m_emb1 m_emb_used m_hps m_hid m_w m_idx m_ask m_snd0 m_snd1 m_snd_used "
                                "m_reca m_vsh m_vsh_used m_rec m_dot m_msg m_used m_clear m_acc")
        emb_landed = (m_emb0, m_emb1)
        snd_landed = (m_snd0, m_snd1)
        block = ctx.enter_context(nc.Block())

        @block.sync
        def _(sp):
            sp.sem_inc(m_emb_used, 2)
            pairs = sp.value_load(g.pairs[0:1, 0:1], min_val=0, max_val=TABLE // 2 - 2)

            def load(i, u):
                sc, _w = step_of(nc, sp, g.code, i)
                sp.wait_ge(m_emb_used, i + 1)
                sp.dma_start(emb[:, u, :], g.emb_t[:, bass.ds(sc * SUPER, SUPER)]).then_inc(emb_landed[u], 16)

            load(0, 0)
            with sp.Fori(0, pairs) as t:
                load(t * 2 + 1, 1)
                load(t * 2 + 2, 0)

        @block.gpsimd
        def _(pool):
            pool.sem_inc(m_snd_used, 2)
            pairs = pool.value_load(g.pairs[0:1, 0:1], min_val=0, max_val=TABLE // 2 - 2)

            def gather(i, u):
                sc, _w = step_of(nc, pool, g.code, i)
                pool.wait_ge(m_snd_used, i + 1)
                pool.tensor_copy(idx[:, u, :], g.src_i[:, bass.ds(sc * CHUNKS, CHUNKS)]).then_inc(m_idx, 1)
                pool.wait_ge(m_idx, i + 1)
                pool.sem_inc(m_ask, 1)
                for c in range(CHUNKS):
                    pool.indirect_dma_start(
                        out=feat[:, u, c, 0, :, :].rearrange("p a b -> p (a b)"), out_offset=None, in_=g.x_rows,
                        in_offset=bass.IndirectOffsetOnAxis(ap=idx[:, u, c:c + 1], axis=0),
                    ).then_inc(snd_landed[u], 16)

            gather(0, 0)
            with pool.Fori(0, pairs) as t:
                gather(t * 2 + 1, 1)
                gather(t * 2 + 2, 0)

        @block.scalar
        def _(act):
            act.sem_inc(m_vsh_used, 2)
            pairs = act.value_load(g.pairs[0:1, 0:1], min_val=0, max_val=TABLE // 2 - 2)

            def prepare(i, u, landed):
                sc, _w = step_of(nc, act, g.code, i)
                act.activation(rec_a[:, u, :, :], g.rec[:, bass.ds(sc * CHUNKS, CHUNKS), :],
                               ACT.Copy).then_inc(m_reca, 1)
                act.wait_ge(m_hps, i + 1)
                act.activation(hid[:, u, :], ps_h[:], ACT.Silu).then_inc(m_hid, 1)
                act.wait_ge(m_reca, i + 1)
                act.wait_ge(snd_landed[u], landed)
                act.wait_ge(m_vsh_used, i + 1)
                for c in range(CHUNKS):
                    for j in range(3):
                        ins = act.activation(vsh[:, u, c, j, :, :], feat[:, u, c, 0, :, :], ACT.Copy,
                                             scale=rec_a[:, u, c, 1 + j:2 + j])
                ins.then_inc(m_vsh, 1)

            prepare(0, 0, 16 * CHUNKS)
            with act.Fori(0, pairs) as t:
                prepare(t * 2 + 1, 1, (t + 1) * (16 * CHUNKS))
                prepare(t * 2 + 2, 0, (t + 2) * (16 * CHUNKS))

        @block.tensor
        def _(pe):
            pairs = pe.value_load(g.pairs[0:1, 0:1], min_val=0, max_val=TABLE // 2 - 2)

            def hidden(i, u, landed):
                pe.wait_ge(emb_landed[u], landed)
                pe.matmul(ps_h[:], g.w1[:], emb[:, u, :], start=True, stop=True).then_inc(m_hps, 1)

            def weights(i, u, c):
                pe.matmul(ps_w[:, c, 0:NPATH * MUL], hid[:, u, c * P:(c + 1) * P], g.w2[:], start=True,
                          stop=True).then_inc(m_w, 1)

            hidden(0, 0, 16)
            pe.wait_ge(m_hid, 1)
            pe.sem_inc(m_emb_used, 1)
            for c in range(CHUNKS):
                weights(0, 0, c)
            pe.wait_ge(m_clear, 1)
            with pe.Fori(0, pairs) as t:
                for u in range(2):
                    i = t * 2 + u
                    hidden(i + 1, 1 - u, (t + 1) * 16 + 16 * u)
                    pe.wait_ge(m_hid, i + 2)
                    pe.sem_inc(m_emb_used, 1)
                    pe.wait_ge(m_acc, i + 1)
                    for c in range(CHUNKS):
                        pe.wait_ge(m_msg, i * CHUNKS + c + 1)
                        q = c % 2
                        out = ps_a[:, u, :]
                        rows = msg[:, q].rearrange("p a b c -> p a (b c)")
                        pe.matmul(out[:, 0:D], hot[:, q, :], rows[:, 0, :], start=(c == 0), stop=False,
                                  skip_group_check=True)
                        pe.matmul(out[:, 0:D], hot[:, q, :], rows[:, 1, :], start=False, stop=False,
                                  skip_group_check=True)
                        pe.matmul(out[:, MUL:D], hot[:, q, :], rows[:, 2, MUL:D], start=False,
                                  stop=(c == CHUNKS - 1), skip_group_check=True).then_inc(m_used, 1)
                        weights(i + 1, 1 - u, c)

        @block.vector
        def _(dve):
            dve.sem_inc(m_used, 2)
            dve.sem_inc(m_acc, 1)
            dve.memset(ps_a[:], 0.0).then_inc(m_clear, 1)
            dve.wait_ge(m_clear, 1)
            pairs = dve.value_load(g.pairs[0:1, 0:1], min_val=0, max_val=TABLE // 2 - 2)

            def add_sums(i, u):
                _sc, w = step_of(nc, dve, g.code_before, i)
                dve.wait_ge(m_used, i * CHUNKS + 2)
                dve.wait_ge(m_acc, i + 1)
                dve.tensor_tensor(g.acc[:, bass.ds(w, 1), 0:D], g.acc[:, bass.ds(w, 1), 0:D],
                                  ps_a[:, 1 - u:2 - u, 0:D], ALU.add).then_inc(m_acc, 1)

            with dve.Fori(0, pairs) as t:
                for u in range(2):
                    i = t * 2 + u
                    sc, w = step_of(nc, dve, g.code, i)
                    dve.tensor_copy(rec_v[:, u], g.rec[:, bass.ds(sc * CHUNKS, CHUNKS), :])
                    dve.tensor_copy(iota_w[:, u], g.iota_node[:, bass.ds(w * P, P)]).then_inc(m_rec, 1)
                    dve.wait_ge(m_vsh, i + 1)
                    v, f = vsh[:, u], feat[:, u]
                    dve.tensor_tensor(f[:, :, 1, 0, :], v[:, :, 0, 1, :], v[:, :, 1, 2, :],
                                      ALU.add).then_inc(m_dot, 1)
                    for k in range(3):
                        a, b = (k + 1) % 3, (k + 2) % 3
                        dve.tensor_tensor(f[:, :, 1, 1 + k, :], v[:, :, b, 1 + a, :], v[:, :, a, 1 + b, :],
                                          ALU.subtract)
                    dve.wait_ge(m_dot, i * 2 + 1)
                    dve.tensor_tensor(f[:, :, 1, 0, :], f[:, :, 1, 0, :], v[:, :, 2, 3, :],
                                      ALU.add).then_inc(m_dot, 1)
                    dve.wait_ge(m_rec, i + 1)
                    dve.wait_ge(m_dot, i * 2 + 2)
                    for c in range(CHUNKS):
                        q = c % 2
                        last = c == CHUNKS - 1
                        dve.wait_ge(m_used, i * CHUNKS + c + 1)
                        dve.tensor_scalar(hot[:, q, :], iota_w[:, u], rec_v[:, u, c, 0:1], None, ALU.is_equal)
                        dve.wait_ge(m_w, i * CHUNKS + c + 1)
                        wt = ps_w[:, c, 0:NPATH * MUL].rearrange("p (a b) -> p a b", a=NPATH)
                        ins = dve.tensor_tensor(msg[:, q, 2, 1:4, :], wt[:, 4:5, :].broadcast_to([P, 3, MUL]),
                                                v[:, c, :, 0, :], ALU.mult)
                        if last:
                            ins.then_inc(m_vsh_used, 1)
                        dve.tensor_tensor(msg[:, q, 0:2, 0, :], wt[:, 0:2, :], f[:, c, :, 0, :], ALU.mult)
                        ins = dve.tensor_tensor(
                            msg[:, q, 0:2, 1:4, :],
                            wt[:, 2:4, :].rearrange("p a (k b) -> p a k b", k=1).broadcast_to([P, 2, 3, MUL]),
                            f[:, c, :, 1:4, :], ALU.mult).then_inc(m_msg, 1)
                        if last:
                            pass
                        if c == 1:
                            add_sums(i, u)
                    dve.wait_ge(m_msg, i * CHUNKS + CHUNKS)
                    dve.sem_inc(m_snd_used, 1)
            add_sums(pairs * 2, 0)


def stage_project(nc, g):
    with ExitStack() as ctx:
        def sb(name, shape, dt=F32):
            return ctx.enter_context(nc.sbuf_tensor(name, shape, dt))

        w_qkv = sb("w_qkv", [P, 2, 3 * D])
        b_qkv = sb("b_qkv", [P, 3 * D])
        gain = sb("gain", [P, 2])
        shift = sb("shift", [P, 2])
        xw = sb("xw", [P, 2, D])
        agg = sb("agg", [P, D])
        agg_t = sb("agg_t", [P, 2, P])
        y = sb("y", [P, D])
        stats = sb("stats", [P, 2, 6])
        mv = sb("mv", [P, 2, 2])
        dev = sb("dev", [P, 2])
        rstd = sb("rstd", [P, 2])
        xn = sb("xn", [P, D])
        xn_t = sb("xn_t", [P, 2, P])
        qkv = sb("qkv", [P, 2, 3 * D])
        left = sb("left", [P, D])
        eps = sb("eps", [P, 1])
        x1 = sb("x1_w", [P, D])
        spare = sb("spare", [P, 1])
        ps_1 = ctx.enter_context(nc.psum_tensor("ps_1", [P, 2, 2 * P], F32))
        ps_2 = ctx.enter_context(nc.psum_tensor("ps_2", [P, 2, 2 * P], F32))
        ps_q = ctx.enter_context(nc.psum_tensor("ps_q", [P, 2, 512], F32))
        (p_w, p_x0, p_x1, p_agg, p_turn, p_aggt, p_upd, p_y, p_stat, p_dev, p_x1done, p_xn, p_turn2, p_xnt,
         p_qkv, p_bias, p_split, p_kv0, p_kv1, p_eps, p_clear, p_chain, p_free) = semaphores(nc, ctx, "p_w p_x0 p_x1 p_agg p_turn p_aggt p_upd p_y p_stat p_dev p_x1done p_xn p_turn2 p_xnt "
                                "p_qkv p_bias p_split p_kv0 p_kv1 p_eps p_clear p_chain p_free")
        x_landed = (p_x0, p_x1)
        kv_stored = (p_kv0, p_kv1)
        block = ctx.enter_context(nc.Block())

        @block.sync
        def _(sp):
            for n, w in enumerate(g.w_qkv):
                sp.dma_start(w_qkv[:, :, n * D:(n + 1) * D], w.rearrange("(k p) n -> p k n", p=P)).then_inc(p_w, 16)
            for n, b in enumerate(g.b_qkv):
                sp.dma_start(b_qkv[:, n * D:(n + 1) * D],
                             b.rearrange("(a d) -> a d", a=1).broadcast_to([P, D])).then_inc(p_w, 16)
            sp.dma_start(gain[:], g.ln1_g).then_inc(p_w, 16)
            sp.dma_start(shift[:], g.ln1_b).then_inc(p_w, 16)
            for u in range(2):
                sp.dma_start(xw[:, u, :], g.x_rows[u * P:(u + 1) * P, :]).then_inc(x_landed[u], 16)
            with sp.Fori(0, WINDOWS // 2) as t:
                for u in range(2):
                    w = t * 2 + u
                    sp.wait_ge(p_bias, w + 2)
                    rows = bass.ds(w * P, P)
                    sp.dma_start(g.k_rows[rows, :], qkv[:, u, D:2 * D]).then_inc(kv_stored[u], 16)
                    sp.dma_start(g.v_rows[rows, :], qkv[:, u, 2 * D:3 * D]).then_inc(kv_stored[u], 16)
                    sp.wait_ge(kv_stored[u], t * 32 + 32)
                    sp.sem_inc(p_free, 1)
                    sp.dma_start(xw[:, u, :], g.x_rows[bass.ds(w * P + 2 * P, P), :]).then_inc(x_landed[u], 16)
            for u in range(2):
                sp.wait_ge(x_landed[u], 16 * (WINDOWS // 2 + 1))

        @block.scalar
        def _(act):
            act.wait_ge(p_eps, 1)
            act.sem_inc(p_turn, 1)
            with act.Fori(0, WINDOWS) as w:
                act.wait_ge(p_turn, w + 1)
                act.activation(agg[:], g.acc[:, bass.ds(w, 1), 0:D].rearrange("p a d -> p (a d)"),
                               ACT.Copy).then_inc(p_agg, 1)
                act.wait_ge(p_turn, w + 2)
                act.activation(agg_t[:].rearrange("p a b -> p (a b)"), ps_1[:, 0, :], ACT.Copy).then_inc(p_aggt, 1)
                for n in range(2):
                    act.wait_ge(p_stat, w * 2 + n + 1)
                    act.activation(dev[:, n:n + 1], mv[:, n, 1:2], ACT.Sqrt, bias=eps[:]).then_inc(p_dev, 1)
                act.wait_ge(p_turn2, w + 1)
                for k in range(2):
                    ins = act.activation(xn_t[:, k, :], ps_2[:, 0, k * P:(k + 1) * P], ACT.Identity,
                                         bias=shift[:, k:k + 1], scale=gain[:, k:k + 1])
                ins.then_inc(p_xnt, 1)

        @block.tensor
        def _(pe):
            pe.wait_ge(p_w, 16 * 8)
            with pe.Fori(0, WINDOWS) as w:
                pe.wait_ge(p_agg, w + 1)
                for k in range(2):
                    mm = pe.transpose(ps_1[:, 0, k * P:(k + 1) * P], agg[:, k * P:(k + 1) * P], g.ident[:])
                mm.then_inc(p_turn, 1)
                pe.wait_ge(p_aggt, w + 1)
                for k in range(2):
                    mm = pe.matmul(ps_1[:, 1, k * P:(k + 1) * P], agg_t[:, k, :], g.lin[:, k, :], start=True,
                                   stop=True, skip_group_check=True)
                mm.then_inc(p_upd, 1)
                pe.wait_ge(p_xn, w + 1)
                for k in range(2):
                    mm = pe.transpose(ps_2[:, 0, k * P:(k + 1) * P], xn[:, k * P:(k + 1) * P], g.ident[:])
                mm.then_inc(p_turn2, 1)
                pe.wait_ge(p_xnt, w + 1)
                pe.wait_ge(p_bias, w + 1)
                for k in range(2):
                    pe.matmul(ps_q[:, 0, :], xn_t[:, k, :], w_qkv[:, k, 0:512], start=(k == 0), stop=(k == 1))
                for k in range(2):
                    mm = pe.matmul(ps_q[:, 1, 0:256], xn_t[:, k, :], w_qkv[:, k, 512:768], start=(k == 0),
                                   stop=(k == 1))
                mm.then_inc(p_qkv, 1)

        @block.vector
        def _(dve):
            dve.sem_inc(p_bias, 1)
            dve.sem_inc(p_free, 2)
            dve.memset(eps[:], EPS).then_inc(p_eps, 1)
            dve.memset(g.q3[:, IDLE, :, :], 0.0)
            dve.wait_ge(p_w, 16 * 8)
            with dve.Fori(0, WINDOWS // 2) as t:
                for u in range(2):
                    w = t * 2 + u
                    chain = [w * 9]

                    def then(ins):
                        chain[0] = chain[0] + 1
                        ins.then_inc(p_chain, 1)
                        dve.wait_ge(p_chain, chain[0])

                    dve.wait_ge(p_upd, w + 1)
                    dve.wait_ge(x_landed[u], t * 16 + 16)
                    then(dve.scalar_tensor_tensor(y[:], xw[:, u, :], 2.0, ps_1[:, 1, :], ALU.mult, ALU.add))
                    then(dve.bn_stats(stats[:, 0, :], y[:]))
                    dve.memset(spare[:], 0.0)
                    dve.bn_aggr(mv[:, 0, :], stats[:, 0, :]).then_inc(p_stat, 1)
                    dve.wait_ge(p_dev, w * 2 + 1)
                    then(dve.reciprocal(rstd[:, 0:1], dev[:, 0:1]))
                    then(dve.tensor_scalar(x1[:], y[:], mv[:, 0, 0:1], rstd[:, 0:1], ALU.subtract, ALU.mult))
                    then(dve.bn_stats(stats[:, 1, :], x1[:]))
                    dve.memset(spare[:], 0.0)
                    dve.bn_aggr(mv[:, 1, :], stats[:, 1, :]).then_inc(p_stat, 1)
                    dve.wait_ge(p_dev, w * 2 + 2)
                    then(dve.reciprocal(rstd[:, 1:2], dev[:, 1:2]))
                    dve.tensor_scalar(xn[:], x1[:], mv[:, 1, 0:1], rstd[:, 1:2], ALU.subtract,
                                      ALU.mult).then_inc(p_xn, 1)
                    dve.tensor_copy(g.x1[:, bass.ds(w, 1), :].rearrange("p a d -> p (a d)"), x1[:])
                    dve.wait_ge(p_qkv, w + 1)
                    dve.wait_ge(p_free, w + 1)
                    dve.tensor_tensor(qkv[:, u, 0:512], ps_q[:, 0, :], b_qkv[:, 0:512], ALU.add)
                    dve.tensor_tensor(qkv[:, u, 512:768], ps_q[:, 1, 0:256], b_qkv[:, 512:768],
                                      ALU.add).then_inc(p_bias, 1)
                    dve.wait_ge(p_bias, w + 2)
                    q = qkv[:, u, 0:D]
                    q3 = [g.q3[:, bass.ds(w, 1), n, :].rearrange("p a d -> p (a d)") for n in range(3)]
                    then(dve.tensor_scalar(q, q, float(DH) ** -0.5, None, ALU.mult))
                    dve.tensor_copy(q3[0], q).then_inc(p_split, 1)
                    dve.wait_ge(p_split, w * 3 + 1)
                    then(dve.tensor_tensor(left[:], q, q3[0], ALU.subtract))
                    dve.tensor_copy(q3[1], left[:]).then_inc(p_split, 1)
                    dve.wait_ge(p_split, w * 3 + 2)
                    dve.tensor_tensor(q3[2], left[:], q3[1], ALU.subtract).then_inc(p_split, 1)
                    dve.wait_ge(p_split, w * 3 + 3)
                    then(dve.memset(y[:, 0:1], 0.0))

        @block.gpsimd
        def _(pool):
            pool.wait_ge(p_turn, WINDOWS + 1)
            pool.memset(g.acc[:], 0.0).then_inc(p_clear, 1)


def stage_scores(nc, g):
    with ExitStack() as ctx:
        def sb(name, shape, dt=F32):
            return ctx.enter_context(nc.sbuf_tensor(name, shape, dt))

        ef = sb("ef", [ED, 2, SUPER])
        w_e = sb("w_e", [ED, DH])
        b_e = sb("b_e", [P, DH])
        idx = sb("idx3", [P, 2, CHUNKS], I32)
        key = sb("key", [P, 2, CHUNKS, HEADS, DH])
        rec_v = sb("rec_v3", [P, 2, CHUNKS, 4])
        iota_w = sb("iota_w3", [P, 2, P])
        hot = sb("hot3", [P, 2, CHUNKS, P], BF16)
        hot_t = sb("hot_t", [P, 2, SUPER], BF16)
        ident_b = sb("ident_b", [P, P], BF16)
        ep = sb("ep", [P, 2, CHUNKS, DH])
        part = sb("part", [P, CHUNKS, HEADS])
        ps_t = ctx.enter_context(nc.psum_tensor("ps_t3", [P, 2, 2, SUPER], BF16))
        ps_e = ctx.enter_context(nc.psum_tensor("ps_e", [P, 2, 512], F32))
        ps_x = ctx.enter_context(nc.psum_tensor("ps_x", [P, 2, CHUNKS, D], F32))
        (c_w, c_ef0, c_ef1, c_ef_used, c_idx, c_ask, c_key0, c_key1, c_key_used, c_rec, c_hot, c_turn, c_hott,
         c_eps, c_ep, c_qx, c_sum, c_mul, c_red, c_add, c_id, c_zero) = semaphores(nc, ctx, "c_w c_ef0 c_ef1 c_ef_used c_idx c_ask c_key0 c_key1 c_key_used c_rec c_hot c_turn c_hott "
                                "c_eps c_ep c_qx c_sum c_mul c_red c_add c_id c_zero")
        ef_landed = (c_ef0, c_ef1)
        key_landed = (c_key0, c_key1)
        block = ctx.enter_context(nc.Block())

        @block.sync
        def _(sp):
            sp.dma_start(w_e[:], g.We).then_inc(c_w, 16)
            sp.dma_start(b_e[:], g.be.rearrange("(a d) -> a d", a=1).broadcast_to([P, DH])).then_inc(c_w, 16)
            sp.sem_inc(c_ef_used, 2)
            pairs = sp.value_load(g.pairs[0:1, 0:1], min_val=0, max_val=TABLE // 2 - 2)
            with sp.Fori(0, pairs) as t:
                for u in range(2):
                    i = t * 2 + u
                    sc, _w = step_of(nc, sp, g.code, i)
                    sp.wait_ge(c_ef_used, i + 1)
                    sp.dma_start(ef[:, u, :], g.ef_t[:, bass.ds(sc * SUPER, SUPER)]).then_inc(ef_landed[u], 16)

        @block.gpsimd
        def _(pool):
            pool.memset(g.score[:], 0.0).then_inc(c_zero, 1)
            pool.sem_inc(c_key_used, 2)
            pairs = pool.value_load(g.pairs[0:1, 0:1], min_val=0, max_val=TABLE // 2 - 2)
            with pool.Fori(0, pairs) as t:
                for u in range(2):
                    i = t * 2 + u
                    sc, _w = step_of(nc, pool, g.code, i)
                    pool.wait_ge(c_key_used, i + 1)
                    pool.tensor_copy(idx[:, u, :], g.src_i[:, bass.ds(sc * CHUNKS, CHUNKS)]).then_inc(c_idx, 1)
                    pool.wait_ge(c_idx, i + 1)
                    pool.sem_inc(c_ask, 1)
                    for c in range(CHUNKS):
                            pool.indirect_dma_start(
                            out=key[:, u, c, :, :].rearrange("p a b -> p (a b)"), out_offset=None, in_=g.k_rows,
                            in_offset=bass.IndirectOffsetOnAxis(ap=idx[:, u, c:c + 1], axis=0),
                        ).then_inc(key_landed[u], 16)

        @block.scalar
        def _(act):
            pairs = act.value_load(g.pairs[0:1, 0:1], min_val=0, max_val=TABLE // 2 - 2)
            act.sem_inc(c_mul, 2)
            with act.Fori(0, pairs) as t:
                for u in range(2):
                    i = t * 2 + u
                    act.wait_ge(c_turn, i + 1)
                    act.wait_ge(c_mul, i + 1)
                    act.activation(hot_t[:, u, :], ps_t[:, u, 0, :], ACT.Copy).then_inc(c_hott, 1)

        @block.tensor
        def _(pe):
            pe.wait_ge(c_w, 32)
            pe.wait_ge(c_id, 1)
            pairs = pe.value_load(g.pairs[0:1, 0:1], min_val=0, max_val=TABLE // 2 - 2)
            with pe.Fori(0, pairs) as t:
                for u in range(2):
                    i = t * 2 + u
                    _sc, w = step_of(nc, pe, g.code, i)
                    pe.wait_ge(c_hot, i + 1)
                    for c in range(CHUNKS):
                        mm = pe.transpose(ps_t[:, u, 0, c * P:(c + 1) * P], hot[:, u, c, :], ident_b[:])
                    mm.then_inc(c_turn, 1)
                    pe.wait_ge(ef_landed[u], t * 16 + 16)
                    pe.wait_ge(c_mul, i + 1)
                    for c in range(CHUNKS):
                        mm = pe.matmul(ps_e[:, u, c * DH:(c + 1) * DH], ef[:, u, c * P:(c + 1) * P], w_e[:],
                                       start=True, stop=True, skip_group_check=True)
                    mm.then_inc(c_eps, 1)
                    pe.wait_ge(c_hott, i + 1)
                    for c in range(CHUNKS):
                        for n in range(3):
                            mm = pe.matmul(ps_x[:, u, c, :], hot_t[:, u, c * P:(c + 1) * P],
                                           g.q3[:, bass.ds(w, 1), n, :].rearrange("p a d -> p (a d)"),
                                           start=(n == 0), stop=(n == 2), skip_group_check=True)
                    mm.then_inc(c_qx, 1)

        @block.vector
        def _(dve):
            dve.sem_inc(c_add, 1)
            dve.tensor_copy(ident_b[:], g.ident[:]).then_inc(c_id, 1)
            dve.wait_ge(c_w, 32)
            dve.wait_ge(c_zero, 1)
            pairs = dve.value_load(g.pairs[0:1, 0:1], min_val=0, max_val=TABLE // 2 - 2)

            def one_hots(i, u):
                sc, w = step_of(nc, dve, g.code, i)
                dve.tensor_copy(rec_v[:, u], g.rec[:, bass.ds(sc * CHUNKS, CHUNKS), :])
                dve.tensor_copy(iota_w[:, u], g.iota_node[:, bass.ds(w * P, P)]).then_inc(c_rec, 1)
                dve.wait_ge(c_rec, i + 1)
                for c in range(CHUNKS):
                    ins = dve.tensor_scalar(hot[:, u, c, :], iota_w[:, u], rec_v[:, u, c, 0:1], None, ALU.is_equal)
                ins.then_inc(c_hot, 1)

            one_hots(0, 0)
            with dve.Fori(0, pairs) as t:
                for u in range(2):
                    i = t * 2 + u
                    sc, _w = step_of(nc, dve, g.code, i)
                    one_hots(i + 1, 1 - u)
                    dve.wait_ge(key_landed[u], (t + 1) * (16 * CHUNKS))
                    dve.wait_ge(c_eps, i + 1)
                    dve.tensor_tensor(ep[:, u], ps_e[:, u, 0:CHUNKS * DH].rearrange("p (c d) -> p c d", c=CHUNKS),
                                      b_e[:].rearrange("p (a d) -> p a d", a=1).broadcast_to([P, CHUNKS, DH]),
                                      ALU.add).then_inc(c_ep, 1)
                    dve.wait_ge(c_ep, i + 1)
                    k = key[:, u]
                    dve.tensor_tensor(k, k, ep[:, u].rearrange("p c (h d) -> p c h d", h=1)
                                      .broadcast_to([P, CHUNKS, HEADS, DH]), ALU.add).then_inc(c_sum, 1)
                    dve.wait_ge(c_sum, i + 1)
                    dve.wait_ge(c_qx, i + 1)
                    flat = k.rearrange("p c h d -> p (c h d)")
                    dve.tensor_tensor(flat, flat, ps_x[:, u].rearrange("p c d -> p (c d)"),
                                      ALU.mult).then_inc(c_mul, 1)
                    dve.wait_ge(c_mul, i + 3)
                    dve.tensor_reduce(part[:], k, AX.X, ALU.add).then_inc(c_red, 1)
                    dve.wait_ge(c_red, i + 1)
                    dve.sem_inc(c_key_used, 1)
                    dve.sem_inc(c_ef_used, 1)
                    mine = g.score[:, bass.ds(sc * CHUNKS, CHUNKS), :]
                    dve.wait_ge(c_add, i + 1)
                    dve.tensor_tensor(mine, mine, part[:], ALU.add).then_inc(c_add, 1)


def stage_softmax(nc, g):
    with ExitStack() as ctx:
        def sb(name, shape, dt=F32):
            return ctx.enter_context(nc.sbuf_tensor(name, shape, dt))

        row = sb("row", [P, BLOCK_EDGES])
        top = sb("top", [P, BLOCK_EDGES])
        dst_r = sb("dst_r", [P, BLOCK_EDGES + 2], I32)
        new = sb("new", [P, BLOCK_EDGES + 1])
        ends = sb("ends", [P, 2])
        ends_r = sb("ends_r", [1, 2, P])
        carry_r = sb("carry_r", [1, P])
        carry_c = sb("carry_c", [P, 1])
        edge_t = sb("edge_t", [P, COLS])
        one = sb("one", [1, 1])
        ps_r = ctx.enter_context(nc.psum_tensor("ps_r", [P, 4, 512], F32))
        ps_e = ctx.enter_context(nc.psum_tensor("ps_e4", [P, 512], F32))
        (x_dst, x_ew, x_turn, x_row, x_dve, x_pe, x_exp, x_back, x_out) = semaphores(nc, ctx, "x_dst x_ew x_turn x_row x_dve x_pe x_exp x_back x_out")
        block = ctx.enter_context(nc.Block())
        GB = 4
        NG = -(-GROUPS // GB)

        def blocks(c):
            return top[:, c * P:(c + 1) * P]

        @block.sync
        def _(sp):
            sp.dma_start(dst_r[:], bass.AP(g.dst_row.tensor, 0, [[BLOCK_EDGES, BLOCKS], [0, HEADS],
                                                                  [1, BLOCK_EDGES + 2]])).then_inc(x_dst, 16)

        @block.tensor
        def _(pe):
            pe.wait_ge(x_ew, 1)
            for n in range(NG):
                if n >= 4:
                    pe.wait_ge(x_row, n - 3)
                for m in range(min(GB, GROUPS - n * GB)):
                    mm = pe.transpose(ps_r[:, n % 4, m * P:(m + 1) * P], blocks(n * GB + m), g.ident[:])
                mm.then_inc(x_turn, 1)
            for k in range(2):
                pe.wait_ge(x_pe, 2 * k + 1)
                pe.transpose(ps_e[0:1, 0:P], ends[:, 0:1], g.ident[:])
                pe.transpose(ps_e[0:1, P:2 * P], ends[:, 1:2], g.ident[:]).then_inc(x_turn, 1)
                pe.wait_ge(x_pe, 2 * k + 2)
                pe.matmul(ps_e[:, 256 + k:257 + k], carry_r[:], one[:], start=True, stop=True,
                          skip_group_check=True).then_inc(x_turn, 1)
            for n in range(NG):
                pe.wait_ge(x_exp, n + 1)
                if n >= 4:
                    pe.wait_ge(x_out, n - 3)
                for m in range(min(GB, GROUPS - n * GB)):
                    c = n * GB + m
                    mm = pe.transpose(ps_r[:, n % 4, m * P:(m + 1) * P], row[:, c * P:(c + 1) * P], g.ident[:])
                mm.then_inc(x_back, 1)

        @block.scalar
        def _(act):
            for n in range(NG):
                w = min(GB, GROUPS - n * GB) * P
                act.wait_ge(x_turn, n + 1)
                act.activation(row[:, n * GB * P:n * GB * P + w], ps_r[:, n % 4, 0:w],
                               ACT.Copy).then_inc(x_row, 1)
            act.wait_ge(x_dve, 1)
            for n in range(NG):
                w = min(GB, GROUPS - n * GB) * P
                cut = row[:, n * GB * P:n * GB * P + w]
                act.activation(cut, cut, ACT.Exp).then_inc(x_exp, 1)

        @block.vector
        def _(dve):
            chain = [0]
            link = ctx.enter_context(nc.semaphore("x_link"))

            def then(ins):
                chain[0] += 1
                ins.then_inc(link, 1)
                dve.wait_ge(link, chain[0])

            dve.memset(one[:], 1.0)
            dve.tensor_tensor(top[:].rearrange("p (c b h) -> p b c h", b=BLOCKS, h=HEADS),
                              g.score[:].rearrange("p (b c) h -> p b c h", b=BLOCKS),
                              g.ew[:].rearrange("p (b c h) -> p b c h", b=BLOCKS, h=1)
                              .broadcast_to([P, BLOCKS, GROUPS, HEADS]), ALU.mult).then_inc(x_ew, 1)
            dve.wait_ge(x_dst, 16)
            then(dve.tensor_tensor(new[:], dst_r[:, 1:], dst_r[:, :-1], ALU.not_equal))
            then(dve.tensor_scalar(new[:], new[:], NEG, None, ALU.mult))
            dve.wait_ge(x_row, NG)
            start, nxt = new[:, 0:BLOCK_EDGES], new[:, 1:BLOCK_EDGES + 1]

            def sweep(k, data, pen, initial, out):
                then(dve.tensor_tensor_scan(out, pen, data, initial, ALU.add, ALU.max))

            for k, (data, pen, out) in enumerate(((row[:], start, top[:]),
                                                  (top[:][:, ::-1], nxt[:, ::-1], top[:][:, ::-1]))):
                if k == 0:
                    sweep(k, data, pen, NEG, out)
                else:
                    sweep(k, data, pen, NEG, out)
                at = BLOCK_EDGES - 1 if k == 0 else 0
                then(dve.tensor_copy(ends[:, 0:1], top[:, at:at + 1]))
                dve.tensor_reduce(ends[:, 1:2], pen if k == 0 else nxt, AX.X, ALU.min).then_inc(x_pe, 1)
                dve.wait_ge(x_turn, NG + 2 * k + 1)
                then(dve.tensor_copy(ends_r[:], ps_e[0:1, 0:2 * P].rearrange("p (a b) -> p a b", a=2)))
                then(dve.memset(carry_r[:], NEG))
                for h in range(HEADS):
                    last = ends_r[:, 0, h::HEADS]
                    keep = ends_r[:, 1, h::HEADS]
                    take = carry_r[:, h::HEADS]
                    n = BLOCKS - 1
                    if k == 0:
                        last, keep, take = last[:, 0:n], keep[:, 0:n], take[:, 1:]
                    else:
                        last, keep, take = last[:, 1:][:, ::-1], keep[:, 1:][:, ::-1], take[:, 0:n][:, ::-1]
                    ins = dve.tensor_tensor_scan(take, keep, last, NEG, ALU.add, ALU.max)
                ins.then_inc(x_pe, 1)
                dve.wait_ge(x_turn, NG + 2 * k + 2)
                then(dve.tensor_copy(carry_c[:], ps_e[:, 256 + k:257 + k]))
                sweep(k, data, pen, carry_c[:], out)
            dve.tensor_tensor(row[:], row[:], top[:], ALU.subtract).then_inc(x_dve, 1)
            for n in range(NG):
                m = min(GB, GROUPS - n * GB)
                dve.wait_ge(x_back, n + 1)
                where = g.score[:].rearrange("p (b c) h -> p c b h", b=BLOCKS)[:, n * GB:n * GB + m]
                dve.tensor_copy(where, ps_r[:, n % 4, 0:m * P].rearrange("p (c b h) -> p c b h", c=m, b=BLOCKS)
                                ).then_inc(x_out, 1)


def stage_values(nc, g):
    with ExitStack() as ctx:
        def sb(name, shape, dt=F32):
            return ctx.enter_context(nc.sbuf_tensor(name, shape, dt))

        idx = sb("idx5", [P, 2, CHUNKS], I32)
        val = sb("val", [P, 2, CHUNKS, HEADS, DH])
        rec_v = sb("rec_v5", [P, 2, CHUNKS, 4])
        iota_w = sb("iota_w5", [P, 2, P])
        hot = sb("hot5", [P, 2, CHUNKS, P])
        msg = sb("msg5", [P, 2, CHUNKS, D + HEADS])
        ps_a = ctx.enter_context(nc.psum_tensor("ps_a5", [P, 2, 512], F32))
        (v_idx, v_ask, v_val0, v_val1, v_used, v_rec, v_p, v_msg, v_sum, v_acc) = semaphores(nc, ctx, "v_idx v_ask v_val0 v_val1 v_used v_rec v_p v_msg v_sum v_acc")
        val_landed = (v_val0, v_val1)
        block = ctx.enter_context(nc.Block())

        @block.gpsimd
        def _(pool):
            pool.sem_inc(v_used, 2)
            pairs = pool.value_load(g.pairs[0:1, 0:1], min_val=0, max_val=TABLE // 2 - 2)
            with pool.Fori(0, pairs) as t:
                for u in range(2):
                    i = t * 2 + u
                    sc, _w = step_of(nc, pool, g.code, i)
                    pool.wait_ge(v_used, i + 1)
                    pool.tensor_copy(idx[:, u, :], g.src_i[:, bass.ds(sc * CHUNKS, CHUNKS)]).then_inc(v_idx, 1)
                    pool.wait_ge(v_idx, i + 1)
                    pool.sem_inc(v_ask, 1)
                    for c in range(CHUNKS):
                            pool.indirect_dma_start(
                            out=val[:, u, c, :, :].rearrange("p a b -> p (a b)"), out_offset=None, in_=g.v_rows,
                            in_offset=bass.IndirectOffsetOnAxis(ap=idx[:, u, c:c + 1], axis=0),
                        ).then_inc(val_landed[u], 16)

        @block.tensor
        def _(pe):
            pairs = pe.value_load(g.pairs[0:1, 0:1], min_val=0, max_val=TABLE // 2 - 2)
            with pe.Fori(0, pairs) as t:
                for u in range(2):
                    i = t * 2 + u
                    pe.wait_ge(v_msg, i + 1)
                    pe.wait_ge(v_acc, i + 1)
                    for c in range(CHUNKS):
                        mm = pe.matmul(ps_a[:, u, 0:D + HEADS], hot[:, u, c, :], msg[:, u, c, :],
                                       start=(c == 0), stop=(c == CHUNKS - 1))
                    mm.then_inc(v_sum, 1)

        @block.vector
        def _(dve):
            dve.sem_inc(v_sum, 2)
            dve.sem_inc(v_acc, 2)
            pairs = dve.value_load(g.pairs[0:1, 0:1], min_val=0, max_val=TABLE // 2 - 2)

            def prepare(i, u, landed):
                sc, w = step_of(nc, dve, g.code, i)
                dve.tensor_copy(rec_v[:, u], g.rec[:, bass.ds(sc * CHUNKS, CHUNKS), :])
                dve.tensor_copy(msg[:, u, :, D:], g.score[:, bass.ds(sc * CHUNKS, CHUNKS), :])
                dve.tensor_copy(iota_w[:, u], g.iota_node[:, bass.ds(w * P, P)]).then_inc(v_rec, 1)
                dve.wait_ge(v_rec, i + 1)
                for c in range(CHUNKS):
                    dve.tensor_scalar(hot[:, u, c, :], iota_w[:, u], rec_v[:, u, c, 0:1], None, ALU.is_equal)
                dve.wait_ge(val_landed[u], landed)
                p = msg[:, u, :, D:].rearrange("p c (h d) -> p c h d", d=1).broadcast_to([P, CHUNKS, HEADS, DH])
                dve.tensor_tensor(msg[:, u, :, 0:D].rearrange("p c (h d) -> p c h d", h=HEADS), val[:, u], p,
                                  ALU.mult).then_inc(v_msg, 1)
                dve.wait_ge(v_msg, i + 1)
                dve.sem_inc(v_used, 1)

            with dve.Fori(0, pairs) as t:
                for u in range(2):
                    i = t * 2 + u
                    dve.wait_ge(v_sum, i + 1)
                    prepare(i, u, (t + 1) * (16 * CHUNKS))
                    _sc, w = step_of(nc, dve, g.code, i)
                    dve.wait_ge(v_sum, i + 3)
                    dve.wait_ge(v_acc, i + 2)
                    dve.tensor_tensor(g.acc[:, bass.ds(w, 1), :], g.acc[:, bass.ds(w, 1), :],
                                      ps_a[:, u:u + 1, 0:D + HEADS], ALU.add).then_inc(v_acc, 1)


def stage_output(nc, g):
    FT = FF // P
    with ExitStack() as ctx:
        def sb(name, shape, dt=F32):
            return ctx.enter_context(nc.sbuf_tensor(name, shape, dt))

        w_o = sb("w_o", [P, 2, D])
        w_1 = sb("w_1", [P, 2, FF])
        w_2 = sb("w_2", [P, FT, D])
        b_o = sb("b_o", [P, D])
        b_2 = sb("b_2", [P, D])
        b_1 = sb("b_1", [P, FT])
        gain = sb("gain6", [P, 2])
        shift = sb("shift6", [P, 2])
        alpha = sb("alpha", [P, 1])
        beta = sb("beta", [P, 1])
        eps = sb("eps6", [P, 1])
        den = sb("den", [P, HEADS])
        att = sb("att", [P, D])
        att_t = sb("att_t", [P, 2, P])
        t_o = sb("t_o", [P, D])
        x2 = sb("x2", [P, D])
        stats = sb("stats6", [P, 2, 6])
        mv = sb("mv6", [P, 2, 2])
        dev = sb("dev6", [P, 2])
        rstd = sb("rstd6", [P, 2])
        xn = sb("xn6", [P, D])
        xn_t = sb("xn_t6", [P, 2, P])
        gel = sb("gel", [P, FT, P])
        y = sb("y6", [P, D])
        res = sb("res", [P, 2, D])
        spare = sb("spare6", [P, 1])
        ps_1 = ctx.enter_context(nc.psum_tensor("ps_16", [P, 2, 2 * P], F32))
        ps_2 = ctx.enter_context(nc.psum_tensor("ps_26", [P, 2 * P], F32))
        ps_f = ctx.enter_context(nc.psum_tensor("ps_f", [P, FT, P], F32))
        ps_y = ctx.enter_context(nc.psum_tensor("ps_y", [P, D], F32))
        (o_w, o_eps, o_att, o_turn, o_attt, o_o, o_stat, o_dev, o_xn, o_turn2, o_xnt, o_ff, o_gel, o_y, o_res,
         o_st0, o_st1, o_chain, o_free) = semaphores(nc, ctx, "o_w o_eps o_att o_turn o_attt o_o o_stat o_dev o_xn o_turn2 o_xnt o_ff o_gel o_y "
                                "o_res o_st0 o_st1 o_chain o_free")
        stored = (o_st0, o_st1)
        block = ctx.enter_context(nc.Block())

        @block.sync
        def _(sp):
            sp.dma_start(w_o[:], g.Wo.rearrange("(k p) n -> p k n", p=P)).then_inc(o_w, 16)
            sp.dma_start(w_1[:], g.W1.rearrange("(k p) n -> p k n", p=P)).then_inc(o_w, 16)
            sp.dma_start(w_2[:], g.W2.rearrange("(k p) n -> p k n", p=P)).then_inc(o_w, 16)
            for tile, b in ((b_o, g.bo), (b_2, g.b2)):
                sp.dma_start(tile[:], b.rearrange("(a d) -> a d", a=1).broadcast_to([P, D])).then_inc(o_w, 16)
            for tile, b in ((alpha, g.alpha), (beta, g.beta)):
                sp.dma_start(tile[:], b.rearrange("(a d) -> a d", a=1).broadcast_to([P, 1])).then_inc(o_w, 16)
            sp.dma_start(gain[:], g.ln2_g).then_inc(o_w, 16)
            sp.dma_start(shift[:], g.ln2_b).then_inc(o_w, 16)
            sp.dma_start(b_1[:], g.b1).then_inc(o_w, 16)
            with sp.Fori(0, WINDOWS // 2) as t:
                for u in range(2):
                    w = t * 2 + u
                    sp.wait_ge(o_res, w + 1)
                    sp.dma_start(g.out[bass.ds(w * P, P), :], res[:, u, :]).then_inc(stored[u], 16)
                    sp.wait_ge(stored[u], t * 16 + 16)
                    sp.sem_inc(o_free, 1)

        @block.scalar
        def _(act):
            act.wait_ge(o_eps, 1)
            act.wait_ge(o_w, 16 * 10)
            with act.Fori(0, WINDOWS) as w:
                act.wait_ge(o_turn, w + 1)
                act.activation(att_t[:].rearrange("p a b -> p (a b)"), ps_1[:, 0, :], ACT.Copy).then_inc(o_attt, 1)
                act.wait_ge(o_stat, w * 2 + 1)
                act.activation(dev[:, 0:1], mv[:, 0, 1:2], ACT.Sqrt, bias=eps[:]).then_inc(o_dev, 1)
                act.wait_ge(o_turn2, w + 1)
                for k in range(2):
                    ins = act.activation(xn_t[:, k, :], ps_2[:, k * P:(k + 1) * P], ACT.Identity,
                                         bias=shift[:, k:k + 1], scale=gain[:, k:k + 1])
                ins.then_inc(o_xnt, 1)
                act.wait_ge(o_ff, w + 1)
                for f in range(FT):
                    ins = act.activation(gel[:, f, :], ps_f[:, f, :], ACT.Gelu, bias=b_1[:, f:f + 1])
                ins.then_inc(o_gel, 1)
                act.wait_ge(o_stat, w * 2 + 2)
                act.activation(dev[:, 1:2], mv[:, 1, 1:2], ACT.Sqrt, bias=eps[:]).then_inc(o_dev, 1)

        @block.tensor
        def _(pe):
            pe.wait_ge(o_w, 16 * 10)
            with pe.Fori(0, WINDOWS) as w:
                pe.wait_ge(o_att, w + 1)
                for k in range(2):
                    mm = pe.transpose(ps_1[:, 0, k * P:(k + 1) * P], att[:, k * P:(k + 1) * P], g.ident[:])
                mm.then_inc(o_turn, 1)
                pe.wait_ge(o_attt, w + 1)
                for k in range(2):
                    mm = pe.matmul(ps_1[:, 1, :], att_t[:, k, :], w_o[:, k, :], start=(k == 0), stop=(k == 1),
                                   skip_group_check=True)
                mm.then_inc(o_o, 1)
                pe.wait_ge(o_xn, w + 1)
                for k in range(2):
                    mm = pe.transpose(ps_2[:, k * P:(k + 1) * P], xn[:, k * P:(k + 1) * P], g.ident[:])
                mm.then_inc(o_turn2, 1)
                pe.wait_ge(o_xnt, w + 1)
                for f in range(FT):
                    for k in range(2):
                        mm = pe.matmul(ps_f[:, f, :], w_1[:, k, f * P:(f + 1) * P], xn_t[:, k, :], start=(k == 0),
                                       stop=(k == 1))
                mm.then_inc(o_ff, 1)
                pe.wait_ge(o_gel, w + 1)
                for f in range(FT):
                    mm = pe.matmul(ps_y[:], gel[:, f, :], w_2[:, f, :], start=(f == 0), stop=(f == FT - 1))
                mm.then_inc(o_y, 1)

        @block.vector
        def _(dve):
            dve.sem_inc(o_free, 2)
            dve.memset(eps[:], EPS).then_inc(o_eps, 1)
            dve.wait_ge(o_w, 16 * 10)
            with dve.Fori(0, WINDOWS // 2) as t:
                for u in range(2):
                    w = t * 2 + u
                    chain = [w * 15]

                    def then(ins):
                        chain[0] = chain[0] + 1
                        ins.then_inc(o_chain, 1)
                        dve.wait_ge(o_chain, chain[0])

                    now = g.acc[:, bass.ds(w, 1), :].rearrange("p a d -> p (a d)")
                    x1 = g.x1[:, bass.ds(w, 1), :].rearrange("p a d -> p (a d)")
                    then(dve.tensor_scalar(den[:], now[:, D:], TINY, None, ALU.max))
                    then(dve.reciprocal(den[:], den[:]))
                    dve.tensor_tensor(att[:].rearrange("p (h d) -> p h d", h=HEADS),
                                      now[:, 0:D].rearrange("p (h d) -> p h d", h=HEADS),
                                      den[:].rearrange("p (h d) -> p h d", d=1).broadcast_to([P, HEADS, DH]),
                                      ALU.mult).then_inc(o_att, 1)
                    dve.wait_ge(o_o, w + 1)
                    then(dve.tensor_tensor(t_o[:], ps_1[:, 1, :], b_o[:], ALU.add))
                    then(dve.scalar_tensor_tensor(x2[:], t_o[:], alpha[:], x1, ALU.mult, ALU.add))
                    then(dve.bn_stats(stats[:, 0, :], x2[:]))
                    dve.memset(spare[:], 0.0)
                    dve.bn_aggr(mv[:, 0, :], stats[:, 0, :]).then_inc(o_stat, 1)
                    dve.wait_ge(o_dev, w * 2 + 1)
                    then(dve.reciprocal(rstd[:, 0:1], dev[:, 0:1]))
                    dve.tensor_scalar(xn[:], x2[:], mv[:, 0, 0:1], rstd[:, 0:1], ALU.subtract,
                                      ALU.mult).then_inc(o_xn, 1)
                    then(dve.tensor_tensor(x2[:], x2[:], x1, ALU.add))
                    dve.wait_ge(o_y, w + 1)
                    then(dve.tensor_tensor(y[:], ps_y[:], b_2[:], ALU.add))
                    then(dve.scalar_tensor_tensor(y[:], y[:], beta[:], x2[:], ALU.mult, ALU.add))
                    then(dve.bn_stats(stats[:, 1, :], y[:]))
                    dve.memset(spare[:], 0.0)
                    dve.bn_aggr(mv[:, 1, :], stats[:, 1, :]).then_inc(o_stat, 1)
                    dve.wait_ge(o_dev, w * 2 + 2)
                    then(dve.reciprocal(rstd[:, 1:2], dev[:, 1:2]))
                    dve.wait_ge(o_free, w + 1)
                    dve.tensor_scalar(res[:, u, :], y[:], mv[:, 1, 0:1], rstd[:, 1:2], ALU.subtract,
                                      ALU.mult).then_inc(o_res, 1)
                    dve.wait_ge(o_res, w + 1)
                    for _ in range(4):
                        dve.sem_inc(o_chain, 1)


def build(nc, g):
    g.k_rows = nc.dram_tensor("k_rows", (NODES_PAD, D), F32).ap()
    g.v_rows = nc.dram_tensor("v_rows", (NODES_PAD, D), F32).ap()
    with ExitStack() as ctx:
        def sb(name, shape, dt=F32, within=ctx):
            return within.enter_context(nc.sbuf_tensor(name, shape, dt))

        g.ident = sb("ident", [P, P])
        g.ones = sb("ones", [P, P])
        g.iota_node = sb("iota_node", [P, (WINDOWS + 1) * P])
        codes = sb("codes", [1, TABLE + 1], I32)
        g.code, g.code_before = codes[:, 1:TABLE + 1], codes[:, 0:TABLE]
        g.pairs = sb("pairs", [1, 1], I32)
        g.src_i = sb("src_i", [P, COLS], I32)
        g.ew = sb("ew", [P, COLS])
        g.rec = sb("rec", [P, COLS, 4])
        g.acc = sb("acc", [P, WINDOWS + 1, D + HEADS])
        g.w1 = sb("w1", [NB, NH])
        g.w2 = sb("w2", [NH, NPATH * MUL])
        g.lin = sb("lin", [P, 2, P])
        stage_tables(nc, g)
        stage_messages(nc, g)
        g.x1 = sb("x1", [P, WINDOWS, D])
        g.score = sb("score", [P, COLS, HEADS])
        with ExitStack() as queries:
            g.q3 = sb("q3", [P, WINDOWS + 1, 3, D], BF16, within=queries)
            stage_project(nc, g)
            stage_scores(nc, g)
        stage_softmax(nc, g)
        stage_values(nc, g)
        stage_output(nc, g)


def by_edge(a, fill):
    a = np.asarray(a)
    full = np.full((EDGES_PAD,) + a.shape[1:], fill, a.dtype)
    full[:EDGES] = a
    return np.ascontiguousarray(np.moveaxis(full.reshape((COLS, P) + a.shape[1:]), 0, 1))


def by_feature(a):
    a = np.asarray(a)
    full = np.zeros((a.shape[1], EDGES_PAD), a.dtype)
    full[:, :EDGES] = a.T
    return full


def kernel(**inputs):
    import concourse.bacc as bacc
    from concourse.bass_utils import run_bass_kernel_spmd

    order = np.concatenate([np.arange(MUL)] + [MUL + 3 * np.arange(MUL) + j for j in range(3)])
    a = {n: np.asarray(v) for n, v in inputs.items()}
    x = np.zeros((NODES_PAD + 2 * P, D), a["x"].dtype)
    x[:NODES] = a["x"][:, order]
    dst_row = np.full((EDGES_PAD + 2,), -1, a["dst"].dtype)
    dst_row[1:EDGES + 1] = a["dst"]
    l1 = {n[len("L1_gnn_"):]: v for n, v in a.items() if n.startswith("L1_gnn_")}
    columns = lambda v: np.ascontiguousarray(v.reshape(-1, P).T)
    laid = {
        "src_t": by_edge(a["src"], 0), "dst_t": by_edge(a["dst"], -1), "dst_row": dst_row,
        "vec_t": by_edge(a["edge_attr_3"], 0), "ew_t": by_edge(a["edge_weight"], 0),
        "emb_t": by_feature(a["edge_attr_8"]), "ef_t": by_feature(a["edge_attr_64"]),
        "x_rows": x,
        "fc_w1": a["L0_gnn_fc_w1"], "fc_w2": a["L0_gnn_fc_w2"],
        "lin_w0": a["L0_gnn_lin_w0"], "lin_w1": a["L0_gnn_lin_w1"],
        "Wq": l1["Wq"][order], "Wk": l1["Wk"][order], "Wv": l1["Wv"][order],
        "bq": l1["bq"], "bk": l1["bk"], "bv": l1["bv"], "We": l1["We"], "be": l1["be"],
        "Wo": l1["Wo"][:, order], "bo": l1["bo"][order],
        "ln1_g": columns(l1["ln1_g"][order]), "ln1_b": columns(l1["ln1_b"][order]),
        "ln2_g": columns(l1["ln2_g"][order]), "ln2_b": columns(l1["ln2_b"][order]),
        "W1": l1["W1"][order], "b1": columns(l1["b1"]), "W2": l1["W2"][:, order], "b2": l1["b2"][order],
        "alpha": l1["alpha"], "beta": l1["beta"],
    }
    nc = bacc.Bacc("TRN2", target_bir_lowering=False, num_devices=1)
    dram = {name: nc.dram_tensor("in_" + name, v.shape, mybir.dt.from_np(v.dtype), kind="ExternalInput").ap()
            for name, v in laid.items()}
    g = Held()
    g.src_t = dram["src_t"]
    g.dst_t = dram["dst_t"]
    g.dst_row = dram["dst_row"]
    g.vec_t = dram["vec_t"]
    g.ew_t = dram["ew_t"]
    g.emb_t = dram["emb_t"]
    g.ef_t = dram["ef_t"]
    g.x_rows = dram["x_rows"]
    g.fc_w1 = dram["fc_w1"]
    g.fc_w2 = dram["fc_w2"]
    g.lin_w0 = dram["lin_w0"]
    g.lin_w1 = dram["lin_w1"]
    g.Wq = dram["Wq"]
    g.Wk = dram["Wk"]
    g.Wv = dram["Wv"]
    g.bq = dram["bq"]
    g.bk = dram["bk"]
    g.bv = dram["bv"]
    g.We = dram["We"]
    g.be = dram["be"]
    g.Wo = dram["Wo"]
    g.bo = dram["bo"]
    g.ln1_g = dram["ln1_g"]
    g.ln1_b = dram["ln1_b"]
    g.ln2_g = dram["ln2_g"]
    g.ln2_b = dram["ln2_b"]
    g.W1 = dram["W1"]
    g.b1 = dram["b1"]
    g.W2 = dram["W2"]
    g.b2 = dram["b2"]
    g.alpha = dram["alpha"]
    g.beta = dram["beta"]
    arrays = {"in_" + name: np.ascontiguousarray(v) for name, v in laid.items()}
    g.w_qkv, g.b_qkv = (g.Wq, g.Wk, g.Wv), (g.bq, g.bk, g.bv)
    g.out = nc.dram_tensor("out", (NODES_PAD, D), F32, kind="ExternalOutput").ap()
    build(nc, g)
    r = run_bass_kernel_spmd(nc, [arrays], core_ids=[0])
    got = r.results[0]["out"][:NODES]
    back = np.empty_like(got)
    back[:, order] = got
    return back
```

```python
from contextlib import ExitStack

import numpy as np

import concourse.bass as bass
from concourse import mybir

F32 = mybir.dt.float32
BF16 = mybir.dt.bfloat16
I32 = mybir.dt.int32
ALU = mybir.AluOpType
ACT = mybir.ActivationFunctionType
AX = mybir.AxisListType

P = 128
NODES = 2500
EDGES = 82500
MUL = 64
D = 4 * MUL
HEADS = 8
DH = D // HEADS
ED = 64
NB = 8
NH = 64
NPATH = 5
FF = 4 * D
EPS = 1e-5
AVG_NEIGH = 16.0

WINDOWS = -(-NODES // P)
CHUNKS = 4
SUPER = CHUNKS * P
BLOCKS = P // HEADS
COLS = -(-(-(-EDGES // P)) // BLOCKS) * BLOCKS
GROUPS = COLS // BLOCKS
BLOCK_EDGES = GROUPS * P
SUPERS = COLS // CHUNKS
EDGES_PAD = COLS * P
NODES_PAD = WINDOWS * P
SPAN = 32
IDLE = WINDOWS
TURN = 4
TABLE = -(-(SUPERS * WINDOWS + 2 * TURN) // 512) * 512
MAX_TURNS = TABLE // TURN - 2
FAR = 4096.0
NEG = -1.0e30
TINY = 1.0e-30


class Held:
    pass


def step_of(nc, eng, code_row, i):
    code = eng.value_load(code_row[0:1, bass.ds(i, 1)], min_val=0, max_val=(SUPERS - 1) * SPAN + IDLE)
    sc = nc.s_assert_within(eng.snap(code // SPAN), 0, SUPERS - 1,
                            skip_runtime_bounds_check_because="a step's code holds a super-chunk's number")
    w = nc.s_assert_within(eng.snap(code % SPAN), 0, IDLE,
                           skip_runtime_bounds_check_because="a step's code holds a window's number")
    return sc, w


def stage_tables(nc, g):
    with ExitStack() as ctx:
        def sb(name, shape, dt=F32):
            return ctx.enter_context(nc.sbuf_tensor(name, shape, dt))

        dst_i = sb("dst_i", [P, COLS], I32)
        win_i = sb("win_i", [P, COLS], I32)
        win_f = sb("win_f", [P, COLS])
        pad_far = sb("pad_far", [P, COLS])
        vec = sb("vec", [P, COLS, 3])
        vec2 = sb("vec2", [P, COLS, 3])
        length = sb("length", [P, COLS])
        inv_len = sb("inv_len", [P, COLS])
        win_hi = sb("win_hi", [P, SUPERS])
        win_lo = sb("win_lo", [P, SUPERS])
        hi = sb("hi", [P, 2])
        lo = sb("lo", [P, 2])
        count = sb("count", [P, 2])
        count0 = sb("count0", [P, 2])
        has = sb("has", [P, 2])
        first = sb("first", [P, 2])
        after = sb("after", [P, 2])
        code_of = sb("code_of", [P, 2])
        upper = sb("upper", [P, P])
        iota_step = sb("iota_step", [P, TABLE])
        from_first = sb("from_first", [P, 2, 512])
        member = sb("member", [P, 2, 512])
        code_t = sb("code_t", [1, 512])
        total = sb("total", [1, 2])
        total1 = sb("total1", [1, 1])
        total_i = sb("total_i", [1, 1], I32)
        ps_t = ctx.enter_context(nc.psum_tensor("ps_t", [P, 2, 512], F32))
        ps_n = ctx.enter_context(nc.psum_tensor("ps_n", [P, 512], F32))
        ps_c = ctx.enter_context(nc.psum_tensor("ps_c", [1, 2, 2, 512], F32))
        t_dst = ctx.enter_context(nc.semaphore("t_dst"))
        t_vec = ctx.enter_context(nc.semaphore("t_vec"))
        t_ew = ctx.enter_context(nc.semaphore("t_ew"))
        t_x = ctx.enter_context(nc.semaphore("t_x"))
        t_wz = ctx.enter_context(nc.semaphore("t_wz"))
        t_w = ctx.enter_context(nc.semaphore("t_w"))
        t_const = ctx.enter_context(nc.semaphore("t_const"))
        t_turn = ctx.enter_context(nc.semaphore("t_turn"))
        t_dve = ctx.enter_context(nc.semaphore("t_dve"))
        t_len = ctx.enter_context(nc.semaphore("t_len"))
        t_act = ctx.enter_context(nc.semaphore("t_act"))
        t_pe = ctx.enter_context(nc.semaphore("t_pe"))
        t_mem = ctx.enter_context(nc.semaphore("t_mem"))
        t_code = ctx.enter_context(nc.semaphore("t_code"))
        t_lin = ctx.enter_context(nc.semaphore("t_lin"))
        block = ctx.enter_context(nc.Block())

        @block.sync
        def _(sp):
            sp.dma_start(dst_i[:], g.dst_t).then_inc(t_dst, 16)
            sp.dma_start(vec[:], g.vec_t).then_inc(t_vec, 16)
            sp.dma_start(g.src_i[:], g.src_t).then_inc(t_x, 16)
            sp.dma_start(g.ew[:], g.ew_t).then_inc(t_ew, 16)
            sp.wait_ge(t_wz, 2)
            for half in range(2):
                sp.dma_start(g.w1[half * NB:(half + 1) * NB, half * NH:(half + 1) * NH], g.fc_w1).then_inc(t_w, 16)
                for path, place in enumerate((0, 4, 2, 1, 3)):
                    sp.dma_start(g.w2[half * NH:(half + 1) * NH, half, place * MUL:(place + 1) * MUL],
                                 g.fc_w2[:, path * MUL:(path + 1) * MUL]).then_inc(t_w, 16)
            sp.wait_ge(t_x, 16)
            sp.wait_ge(t_ew, 16)

        @block.gpsimd
        def _(pool):
            pool.memset(g.w1[:], 0.0).then_inc(t_wz, 1)
            pool.memset(g.w2[:], 0.0).then_inc(t_wz, 1)
            pool.iota(iota_step[:], [[1, TABLE]], base=0, channel_multiplier=0,
                      allow_small_or_imprecise_dtypes=True).then_inc(t_const, 1)
            pool.iota(g.iota_node[:], [[1, (WINDOWS + 1) * P]], base=0, channel_multiplier=0,
                      allow_small_or_imprecise_dtypes=True).then_inc(t_const, 1)
            pool.iota(first[:], [[P, 2]], base=0, channel_multiplier=1,
                      allow_small_or_imprecise_dtypes=True).then_inc(t_const, 1)
            pool.memset(g.ident[:], 0.0).then_inc(t_const, 1)
            pool.memset(upper[:], 1.0).then_inc(t_const, 1)
            pool.memset(g.ones[:], 1.0).then_inc(t_const, 1)
            pool.memset(g.acc[:], 0.0).then_inc(t_const, 1)
            pool.memset(g.lin[:], 0.0).then_inc(t_const, 1)
            pool.wait_ge(t_const, 8)
            pool.affine_select(out=g.ident[:], in_=g.ident[:], compare_op=ALU.not_equal, fill=1.0, base=0,
                               pattern=[[-1, P]], channel_multiplier=1).then_inc(t_const, 1)
            pool.affine_select(out=upper[:], in_=upper[:], compare_op=ALU.is_ge, fill=0.0, base=0,
                               pattern=[[1, P]], channel_multiplier=-1).then_inc(t_const, 1)
            pool.dma_start(g.lin[0:64, 0, 0:64], g.lin_w0).then_inc(t_lin, 16)
            pool.dma_start(g.lin[64:128, 0, 64:128], g.lin_w1).then_inc(t_lin, 16)
            pool.dma_start(g.lin[0:64, 1, 0:64], g.lin_w1).then_inc(t_lin, 16)
            pool.dma_start(g.lin[64:128, 1, 64:128], g.lin_w1).then_inc(t_lin, 16)
            pool.wait_ge(t_lin, 64)

        @block.scalar
        def _(act):
            act.wait_ge(t_len, 1)
            act.activation(length[:], length[:], ACT.Sqrt).then_inc(t_act, 1)

        @block.tensor
        def _(pe):
            pe.wait_ge(t_const, 10)
            pe.wait_ge(t_turn, 2)
            pe.transpose(ps_t[:, 0, 0:128], win_hi[:, 0:128], g.ident[:])
            pe.transpose(ps_t[0:SUPERS - 128, 0, 128:256], win_hi[:, 128:SUPERS], g.ident[:])
            pe.transpose(ps_t[:, 1, 0:128], win_lo[:, 0:128], g.ident[:])
            pe.transpose(ps_t[0:SUPERS - 128, 1, 128:256], win_lo[:, 128:SUPERS], g.ident[:]).then_inc(t_pe, 1)
            pe.wait_ge(t_turn, 3)
            pe.matmul(ps_n[:, 0:2], upper[:], count[:], start=True, stop=False)
            pe.matmul(ps_n[:, 0:2], g.ones[:], count0[:], start=False, stop=True)
            pe.matmul(ps_n[0:1, 4:6], g.ones[:, 0:1], count[:], start=True, stop=True,
                      skip_group_check=True).then_inc(t_pe, 1)
            for b in range(TABLE // 512):
                pe.wait_ge(t_mem, b + 1)
                if b >= 2:
                    pe.wait_ge(t_code, b - 1)
                for row, lhs in ((0, code_of), (1, g.ones)):
                    for c in range(2):
                        mm = pe.matmul(ps_c[:, b % 2, row, :], lhs[:, c:c + 1], member[:, c, :],
                                       start=(c == 0), stop=(c == 1))
                mm.then_inc(t_pe, 1)

        @block.vector
        def _(dve):
            done = [0]

            def then(ins):
                done[0] += 1
                ins.then_inc(t_dve, 1)
                dve.wait_ge(t_dve, done[0])

            dve.wait_ge(t_dst, 16)
            then(dve.tensor_scalar(win_i[:], dst_i[:], 7, None, ALU.arith_shift_right))
            then(dve.tensor_copy(win_f[:], win_i[:]))
            then(dve.tensor_scalar(pad_far[:], win_f[:], 0.0, -FAR, ALU.is_lt, ALU.mult))
            then(dve.scalar_tensor_tensor(pad_far[:], win_f[:], -1.0, pad_far[:], ALU.mult, ALU.add))
            dve.tensor_reduce(win_hi[:], win_f[:].rearrange("p (s c) -> p s c", c=CHUNKS), AX.X,
                              ALU.max).then_inc(t_turn, 1)
            dve.tensor_reduce(win_lo[:], pad_far[:].rearrange("p (s c) -> p s c", c=CHUNKS), AX.X,
                              ALU.max).then_inc(t_turn, 1)
            dve.tensor_copy(g.rec[:, :, 0], dst_i[:])
            dve.wait_ge(t_vec, 16)
            then(dve.tensor_tensor(vec2[:], vec[:], vec[:], ALU.mult))
            dve.tensor_reduce(length[:], vec2[:], AX.X, ALU.add).then_inc(t_len, 1)
            dve.memset(g.code_before[:, 0:1], IDLE)
            dve.memset(hi[:], -1.0)
            dve.memset(count0[:], 0.0)
            then(dve.memset(lo[:], -FAR))
            dve.wait_ge(t_pe, 1)
            rest = SUPERS - 128
            dve.tensor_reduce(hi[:, 0:1], ps_t[:, 0, 0:128], AX.X, ALU.max)
            dve.tensor_reduce(hi[0:rest, 1:2], ps_t[0:rest, 0, 128:256], AX.X, ALU.max)
            dve.tensor_reduce(lo[:, 0:1], ps_t[:, 1, 0:128], AX.X, ALU.max)
            then(dve.tensor_reduce(lo[0:rest, 1:2], ps_t[0:rest, 1, 128:256], AX.X, ALU.max))
            then(dve.tensor_tensor(count[:], hi[:], lo[:], ALU.add))
            then(dve.tensor_scalar(count[:], count[:], 1.0, 0.0, ALU.add, ALU.max))
            then(dve.tensor_scalar(has[:], count[:], 0.0, None, ALU.is_gt))
            dve.tensor_copy(count0[:, 1:2], count[:, 0:1]).then_inc(t_turn, 1)
            then(dve.tensor_tensor(lo[:], lo[:], has[:], ALU.mult))
            dve.wait_ge(t_const, 10)
            then(dve.tensor_scalar(code_of[:], first[:], float(SPAN), -float(IDLE), ALU.mult, ALU.add))
            then(dve.tensor_tensor(code_of[:], code_of[:], lo[:], ALU.subtract))
            dve.wait_ge(t_pe, 2)
            then(dve.tensor_copy(after[:], ps_n[:, 0:2]))
            then(dve.tensor_tensor(first[:], after[:], count[:], ALU.subtract))
            then(dve.tensor_tensor(code_of[:], code_of[:], first[:], ALU.subtract))
            then(dve.tensor_copy(total[:], ps_n[0:1, 4:6]))
            then(dve.tensor_tensor(total1[:], total[:, 0:1], total[:, 1:2], ALU.add))
            then(dve.tensor_scalar(total1[:], total1[:], float(TURN - 1), None, ALU.add))
            then(dve.tensor_copy(total_i[:], total1[:]))
            then(dve.tensor_scalar(g.turns[:], total_i[:], TURN.bit_length() - 1, None, ALU.arith_shift_right))
            for b in range(TABLE // 512):
                cut = slice(b * 512, (b + 1) * 512)
                if b >= 1:
                    dve.wait_ge(t_pe, 2 + b)
                for c in range(2):
                    then(dve.tensor_scalar(from_first[:, c, :], iota_step[:, cut], first[:, c:c + 1], None,
                                           ALU.is_ge))
                    ins = dve.scalar_tensor_tensor(member[:, c, :], iota_step[:, cut], after[:, c:c + 1],
                                                   from_first[:, c, :], ALU.is_lt, ALU.mult)
                    if c == 1:
                        ins.then_inc(t_mem, 1)
                dve.wait_ge(t_pe, 3 + b)
                then(dve.tensor_tensor(code_t[:], ps_c[:, b % 2, 1, :], iota_step[0:1, cut], ALU.mult))
                done[0] += 1
                dve.scalar_tensor_tensor(code_t[:], ps_c[:, b % 2, 0, :], float(IDLE), code_t[:],
                                         ALU.add, ALU.add).then_inc(t_dve, 1)
                dve.wait_ge(t_dve, done[0])
                dve.tensor_copy(g.code[:, cut], code_t[:]).then_inc(t_code, 1)
                dve.wait_ge(t_code, b + 1)
            dve.wait_ge(t_act, 1)
            then(dve.tensor_scalar(length[:], length[:], 1e-9, None, ALU.add))
            then(dve.reciprocal(inv_len[:], length[:]))
            for j in range(3):
                dve.scalar_tensor_tensor(g.rec[:, :, 1 + j], vec[:, :, j], float(np.sqrt(3.0)), inv_len[:],
                                         ALU.mult, ALU.mult)
            dve.wait_ge(t_w, 16 * 2 * (1 + NPATH))
            dve.tensor_scalar(g.w1[:], g.w1[:], 1.0 / float(np.sqrt(NB)), None, ALU.mult)
            out = 1.0 / (np.sqrt(NH) * AVG_NEIGH * np.sqrt(MUL))
            r2, r3 = 1.0 / np.sqrt(2.0), 1.0 / np.sqrt(3.0)
            for path, scale in enumerate((r2, r3 * r2, r3, r3 * r2, r3)):
                cols = g.w2[:, :, path * MUL:(path + 1) * MUL]
                dve.tensor_scalar(cols, cols, float(out * scale), None, ALU.mult)


def stage_messages(nc, g):
    with ExitStack() as ctx:
        def sb(name, shape, dt=F32):
            return ctx.enter_context(nc.sbuf_tensor(name, shape, dt))

        emb = sb("emb", [P, 2, SUPER // 2])
        hid = sb("hid", [2 * NH, 2, SUPER // 2])
        idx = sb("idx", [P, TURN, CHUNKS], I32)
        feat = sb("feat", [P, TURN, CHUNKS, 4, MUL])
        rec_a = sb("rec_a", [P, 2, CHUNKS, 4])
        rec_v = sb("rec_v", [P, 2, CHUNKS, 4])
        iota_w = sb("iota_w", [P, 2, P])
        vsh = sb("vsh", [P, 2, CHUNKS, 3, 4, MUL])
        dots = sb("dots", [P, 2, CHUNKS, 4, MUL])
        hot = sb("hot", [P, CHUNKS, P])
        msg = sb("msg", [P, CHUNKS, 3, 4, MUL])
        ps_h = ctx.enter_context(nc.psum_tensor("ps_h", [2 * NH, 2, 512], F32))
        ps_w = ctx.enter_context(nc.psum_tensor("ps_w", [P, CHUNKS, 512], F32))
        ps_a = ctx.enter_context(nc.psum_tensor("ps_a", [P, 2, 512], F32))
        m_zero = ctx.enter_context(nc.semaphore("m_zero"))
        m_emb = [ctx.enter_context(nc.semaphore(f"m_emb{u}")) for u in range(2)]
        m_snd = [ctx.enter_context(nc.semaphore(f"m_snd{u}")) for u in range(TURN)]
        m_emb_used = ctx.enter_context(nc.semaphore("m_emb_used"))
        m_hps = ctx.enter_context(nc.semaphore("m_hps"))
        m_hid = ctx.enter_context(nc.semaphore("m_hid"))
        m_w = ctx.enter_context(nc.semaphore("m_w"))
        m_idx = ctx.enter_context(nc.semaphore("m_idx"))
        m_ask = ctx.enter_context(nc.semaphore("m_ask"))
        m_snd_used = ctx.enter_context(nc.semaphore("m_snd_used"))
        m_reca = ctx.enter_context(nc.semaphore("m_reca"))
        m_rec = ctx.enter_context(nc.semaphore("m_rec"))
        m_vsh = ctx.enter_context(nc.semaphore("m_vsh"))
        m_vsh_used = ctx.enter_context(nc.semaphore("m_vsh_used"))
        m_cross = ctx.enter_context(nc.semaphore("m_cross"))
        m_dot = ctx.enter_context(nc.semaphore("m_dot"))
        m_prod = ctx.enter_context(nc.semaphore("m_prod"))
        m_msg = ctx.enter_context(nc.semaphore("m_msg"))
        m_used = ctx.enter_context(nc.semaphore("m_used"))
        m_clear = ctx.enter_context(nc.semaphore("m_clear"))
        m_acc = ctx.enter_context(nc.semaphore("m_acc"))
        block = ctx.enter_context(nc.Block())

        @block.sync
        def _(sp):
            sp.sem_inc(m_emb_used, 2)
            turns = sp.value_load(g.turns[0:1, 0:1], min_val=0, max_val=MAX_TURNS)
            sp.wait_ge(m_zero, 1)

            def load(i, u):
                sc, _w = step_of(nc, sp, g.code, i)
                sp.wait_ge(m_emb_used, i + 1)
                sp.dma_start(emb[0:2 * NB, u % 2, :],
                             g.emb_t[:, bass.ds(sc * (SUPER // 2), SUPER // 2)]).then_inc(m_emb[u % 2], 16)

            load(0, 0)
            load(1, 1)
            with sp.Fori(0, turns) as t:
                for u in range(TURN):
                    load(t * TURN + u + 2, u + 2)

        @block.gpsimd
        def _(pool):
            pool.sem_inc(m_snd_used, TURN)
            turns = pool.value_load(g.turns[0:1, 0:1], min_val=0, max_val=MAX_TURNS)

            def gather(i, u):
                sc, _w = step_of(nc, pool, g.code, i)
                pool.wait_ge(m_snd_used, i + 1)
                pool.tensor_copy(idx[:, u, :], g.src_i[:, bass.ds(sc * CHUNKS, CHUNKS)]).then_inc(m_idx, 1)
                pool.wait_ge(m_idx, i + 1)
                pool.sem_inc(m_ask, 1)
                for c in range(CHUNKS):
                    pool.indirect_dma_start(
                        out=feat[:, u, c, :, :].rearrange("p a b -> p (a b)"), out_offset=None, in_=g.x_rows,
                        in_offset=bass.IndirectOffsetOnAxis(ap=idx[:, u, c:c + 1], axis=0),
                    ).then_inc(m_snd[u], 16)

            def cross(i, u):
                pool.wait_ge(m_vsh, i + 1)
                pool.sem_inc(m_ask, 1)
                v = vsh[:, u % 2]
                for k in range(3):
                    a, b = (k + 1) % 3, (k + 2) % 3
                    ins = pool.tensor_tensor(dots[:, u % 2, :, 1 + k, :], v[:, :, b, 1 + a, :], v[:, :, a, 1 + b, :],
                                             ALU.subtract)
                ins.then_inc(m_cross, 1)

            for u in range(TURN - 1):
                gather(u, u)
            cross(0, 0)
            with pool.Fori(0, turns) as t:
                for u in range(TURN):
                    gather(t * TURN + u + TURN - 1, (u + TURN - 1) % TURN)
                    cross(t * TURN + u + 1, u + 1)

        @block.scalar
        def _(act):
            act.sem_inc(m_vsh_used, 2)
            turns = act.value_load(g.turns[0:1, 0:1], min_val=0, max_val=MAX_TURNS)

            def prepare(i, u, landed):
                sc, _w = step_of(nc, act, g.code, i)
                act.activation(rec_a[:, u % 2, :, :], g.rec[:, bass.ds(sc * CHUNKS, CHUNKS), :],
                               ACT.Copy).then_inc(m_reca, 1)
                act.wait_ge(m_hps, i + 1)
                act.activation(hid[:, u % 2, :], ps_h[:, u % 2, 0:SUPER // 2], ACT.Silu).then_inc(m_hid, 1)
                act.wait_ge(m_reca, i + 1)
                act.wait_ge(m_snd[u % TURN], landed)
                act.wait_ge(m_vsh_used, i + 1)
                for c in range(CHUNKS):
                    for j in range(3):
                        ins = act.activation(vsh[:, u % 2, c, j, :, :], feat[:, u % TURN, c, :, :], ACT.Copy,
                                             scale=rec_a[:, u % 2, c, 1 + j:2 + j])
                ins.then_inc(m_vsh, 1)

            prepare(0, 0, 16 * CHUNKS)
            with act.Fori(0, turns) as t:
                for u in range(1, TURN + 1):
                    prepare(t * TURN + u, u, (t + 1 + u // TURN) * (16 * CHUNKS))

        @block.tensor
        def _(pe):
            turns = pe.value_load(g.turns[0:1, 0:1], min_val=0, max_val=MAX_TURNS)

            def hidden(i, u, landed):
                pe.wait_ge(m_emb[u % 2], landed)
                pe.matmul(ps_h[:, u % 2, 0:SUPER // 2], g.w1[:], emb[:, u % 2, :], start=True, stop=True,
                          skip_group_check=True).then_inc(m_hps, 1)
                pe.wait_ge(m_hps, i + 1)
                pe.sem_inc(m_emb_used, 1)

            def weights(i, u, c):
                half, at = c // 2, (c % 2) * P
                pe.matmul(ps_w[:, c, 0:NPATH * MUL], hid[:, u % 2, at:at + P], g.w2[:, half, :], start=True,
                          stop=True).then_inc(m_w, 1)

            hidden(0, 0, 16)
            hidden(1, 1, 16)
            pe.wait_ge(m_hid, 1)
            for c in range(CHUNKS):
                weights(0, 0, c)
            pe.wait_ge(m_clear, 1)
            with pe.Fori(0, turns) as t:
                for u in range(TURN):
                    i = t * TURN + u
                    pe.wait_ge(m_acc, i + 1)
                    for c in range(CHUNKS):
                        pe.wait_ge(m_msg, i * CHUNKS + c + 1)
                        out = ps_a[:, u % 2, :]
                        rows = msg[:, c].rearrange("p a b c -> p a (b c)")
                        pe.matmul(out[:, 0:D], hot[:, c, :], rows[:, 0, :], start=(c == 0), stop=False,
                                  skip_group_check=True)
                        pe.matmul(out[:, MUL:D], hot[:, c, :], rows[:, 2, MUL:D], start=False,
                                  stop=(c == CHUNKS - 1), skip_group_check=True).then_inc(m_used, 1)
                        if c == 0:
                            pe.wait_ge(m_hid, i + 2)
                        weights(i + 1, u + 1, c)
                        if c == 1:
                            hidden(i + 2, u, t * (16 * TURN // 2) + 16 * (u // 2 + 2))

        @block.vector
        def _(dve):
            dve.sem_inc(m_used, CHUNKS)
            dve.sem_inc(m_acc, 1)
            dve.memset(emb[:], 0.0).then_inc(m_zero, 1)
            dve.memset(ps_a[:], 0.0).then_inc(m_clear, 1)
            dve.wait_ge(m_clear, 1)
            turns = dve.value_load(g.turns[0:1, 0:1], min_val=0, max_val=MAX_TURNS)

            def add_sums(i, u):
                _sc, w = step_of(nc, dve, g.code_before, i)
                dve.wait_ge(m_used, i * CHUNKS + CHUNKS)
                dve.wait_ge(m_acc, i + 1)
                dve.tensor_tensor(g.acc[:, bass.ds(w, 1), 0:D], g.acc[:, bass.ds(w, 1), 0:D],
                                  ps_a[:, (u + 1) % 2:(u + 1) % 2 + 1, 0:D], ALU.add).then_inc(m_acc, 1)

            with dve.Fori(0, turns) as t:
                for u in range(TURN):
                    i = t * TURN + u
                    sc, w = step_of(nc, dve, g.code, i)
                    r = rec_v[:, u % 2]
                    dve.tensor_copy(r, g.rec[:, bass.ds(sc * CHUNKS, CHUNKS), :])
                    dve.tensor_copy(iota_w[:, u % 2], g.iota_node[:, bass.ds(w * P, P)]).then_inc(m_rec, 1)
                    dve.wait_ge(m_vsh, i + 1)
                    v, f, x = vsh[:, u % 2], feat[:, u], dots[:, u % 2]
                    dve.tensor_tensor(x[:, :, 0, :], v[:, :, 0, 1, :], v[:, :, 1, 2, :], ALU.add).then_inc(m_dot, 1)
                    dve.wait_ge(m_dot, i * 2 + 1)
                    dve.tensor_tensor(x[:, :, 0, :], x[:, :, 0, :], v[:, :, 2, 3, :], ALU.add).then_inc(m_dot, 1)
                    dve.wait_ge(m_rec, i + 1)

                    def sum_paths(c):
                        dve.wait_ge(m_prod, i * CHUNKS + c + 1)
                        dve.tensor_tensor(msg[:, c, 0], msg[:, c, 0], msg[:, c, 1], ALU.add).then_inc(m_msg, 1)

                    for c in range(CHUNKS):
                        dve.wait_ge(m_used, i * CHUNKS + c + 1)
                        dve.tensor_scalar(hot[:, c, :], iota_w[:, u % 2], r[:, c, 0:1], None, ALU.is_equal)
                        dve.wait_ge(m_w, i * CHUNKS + c + 1)
                        wt = ps_w[:, c, 0:NPATH * MUL].rearrange("p (a b) -> p a b", a=NPATH)
                        dve.tensor_tensor(msg[:, c, 2, 1:4, :], wt[:, 4:5, :].broadcast_to([P, 3, MUL]),
                                          v[:, c, :, 0, :], ALU.mult)
                        dve.tensor_tensor(msg[:, c, 0, 1:4, :], wt[:, 2:3, :].broadcast_to([P, 3, MUL]),
                                          f[:, c, 1:4, :], ALU.mult)
                        dve.tensor_tensor(msg[:, c, 0, 0, :], wt[:, 0, :], f[:, c, 0, :], ALU.mult)
                        if c == 0:
                            dve.wait_ge(m_dot, i * 2 + 2)
                            dve.wait_ge(m_cross, i + 1)
                        dve.tensor_tensor(msg[:, c, 1, 1:4, :], wt[:, 3:4, :].broadcast_to([P, 3, MUL]),
                                          x[:, c, 1:4, :], ALU.mult)
                        dve.tensor_tensor(msg[:, c, 1, 0, :], wt[:, 1, :], x[:, c, 0, :],
                                          ALU.mult).then_inc(m_prod, 1)
                        if c >= 1:
                            sum_paths(c - 1)
                        if c == 1:
                            add_sums(i, u)
                    sum_paths(CHUNKS - 1)
                    dve.sem_inc(m_snd_used, 1)
                    dve.sem_inc(m_vsh_used, 1)
            add_sums(turns * TURN, TURN)


def stage_project(nc, g):
    with ExitStack() as ctx:
        def sb(name, shape, dt=F32):
            return ctx.enter_context(nc.sbuf_tensor(name, shape, dt))

        w_qkv = sb("w_qkv", [P, 2, 3 * D])
        b_qkv = sb("b_qkv", [P, 3 * D])
        gain = sb("gain", [P, 2])
        shift = sb("shift", [P, 2])
        xw = sb("xw", [P, 2, D])
        agg = sb("agg", [P, D])
        agg_t = sb("agg_t", [P, 2, P])
        y = sb("y", [P, D])
        stats = sb("stats", [P, 2, 6])
        mv = sb("mv", [P, 2, 2])
        dev = sb("dev", [P, 2])
        rstd = sb("rstd", [P, 2])
        xn = sb("xn", [P, D])
        xn_t = sb("xn_t", [P, 2, P])
        qkv = sb("qkv", [P, 2, 3 * D])
        left = sb("left", [P, D])
        eps = sb("eps", [P, 1])
        x1 = sb("x1_w", [P, D])
        spare = sb("spare", [P, 1])
        ps_1 = ctx.enter_context(nc.psum_tensor("ps_1", [P, 2, 2 * P], F32))
        ps_2 = ctx.enter_context(nc.psum_tensor("ps_2", [P, 2, 2 * P], F32))
        ps_q = ctx.enter_context(nc.psum_tensor("ps_q", [P, 2, 512], F32))
        p_w = ctx.enter_context(nc.semaphore("p_w"))
        p_x0 = ctx.enter_context(nc.semaphore("p_x0"))
        p_x1 = ctx.enter_context(nc.semaphore("p_x1"))
        p_agg = ctx.enter_context(nc.semaphore("p_agg"))
        p_turn = ctx.enter_context(nc.semaphore("p_turn"))
        p_aggt = ctx.enter_context(nc.semaphore("p_aggt"))
        p_upd = ctx.enter_context(nc.semaphore("p_upd"))
        p_y = ctx.enter_context(nc.semaphore("p_y"))
        p_stat = ctx.enter_context(nc.semaphore("p_stat"))
        p_dev = ctx.enter_context(nc.semaphore("p_dev"))
        p_x1done = ctx.enter_context(nc.semaphore("p_x1done"))
        p_xn = ctx.enter_context(nc.semaphore("p_xn"))
        p_turn2 = ctx.enter_context(nc.semaphore("p_turn2"))
        p_xnt = ctx.enter_context(nc.semaphore("p_xnt"))
        p_qkv = ctx.enter_context(nc.semaphore("p_qkv"))
        p_bias = ctx.enter_context(nc.semaphore("p_bias"))
        p_split = ctx.enter_context(nc.semaphore("p_split"))
        p_kv0 = ctx.enter_context(nc.semaphore("p_kv0"))
        p_kv1 = ctx.enter_context(nc.semaphore("p_kv1"))
        p_eps = ctx.enter_context(nc.semaphore("p_eps"))
        p_clear = ctx.enter_context(nc.semaphore("p_clear"))
        p_chain = ctx.enter_context(nc.semaphore("p_chain"))
        p_free = ctx.enter_context(nc.semaphore("p_free"))
        x_landed = (p_x0, p_x1)
        kv_stored = (p_kv0, p_kv1)
        block = ctx.enter_context(nc.Block())

        @block.sync
        def _(sp):
            for n, w in enumerate(g.w_qkv):
                sp.dma_start(w_qkv[:, :, n * D:(n + 1) * D], w.rearrange("(k p) n -> p k n", p=P)).then_inc(p_w, 16)
            for n, b in enumerate(g.b_qkv):
                sp.dma_start(b_qkv[:, n * D:(n + 1) * D],
                             b.rearrange("(a d) -> a d", a=1).broadcast_to([P, D])).then_inc(p_w, 16)
            sp.dma_start(gain[:], g.ln1_g).then_inc(p_w, 16)
            sp.dma_start(shift[:], g.ln1_b).then_inc(p_w, 16)
            for u in range(2):
                sp.dma_start(xw[:, u, :], g.x_rows[u * P:(u + 1) * P, :]).then_inc(x_landed[u], 16)
            with sp.Fori(0, WINDOWS // 2) as t:
                for u in range(2):
                    w = t * 2 + u
                    sp.wait_ge(p_bias, w + 2)
                    rows = bass.ds(w * P, P)
                    sp.dma_start(g.k_rows[rows, :], qkv[:, u, D:2 * D]).then_inc(kv_stored[u], 16)
                    sp.dma_start(g.v_rows[rows, :], qkv[:, u, 2 * D:3 * D]).then_inc(kv_stored[u], 16)
                    sp.wait_ge(kv_stored[u], t * 32 + 32)
                    sp.sem_inc(p_free, 1)
                    sp.dma_start(xw[:, u, :], g.x_rows[bass.ds(w * P + 2 * P, P), :]).then_inc(x_landed[u], 16)
            for u in range(2):
                sp.wait_ge(x_landed[u], 16 * (WINDOWS // 2 + 1))

        @block.scalar
        def _(act):
            act.wait_ge(p_eps, 1)
            act.sem_inc(p_turn, 1)
            with act.Fori(0, WINDOWS) as w:
                act.wait_ge(p_turn, w + 1)
                act.activation(agg[:], g.acc[:, bass.ds(w, 1), 0:D].rearrange("p a d -> p (a d)"),
                               ACT.Copy).then_inc(p_agg, 1)
                act.wait_ge(p_turn, w + 2)
                act.activation(agg_t[:].rearrange("p a b -> p (a b)"), ps_1[:, 0, :], ACT.Copy).then_inc(p_aggt, 1)
                for n in range(2):
                    act.wait_ge(p_stat, w * 2 + n + 1)
                    act.activation(dev[:, n:n + 1], mv[:, n, 1:2], ACT.Sqrt, bias=eps[:]).then_inc(p_dev, 1)
                act.wait_ge(p_turn2, w + 1)
                for k in range(2):
                    ins = act.activation(xn_t[:, k, :], ps_2[:, 0, k * P:(k + 1) * P], ACT.Identity,
                                         bias=shift[:, k:k + 1], scale=gain[:, k:k + 1])
                ins.then_inc(p_xnt, 1)

        @block.tensor
        def _(pe):
            pe.wait_ge(p_w, 16 * 8)
            with pe.Fori(0, WINDOWS) as w:
                pe.wait_ge(p_agg, w + 1)
                for k in range(2):
                    mm = pe.transpose(ps_1[:, 0, k * P:(k + 1) * P], agg[:, k * P:(k + 1) * P], g.ident[:])
                mm.then_inc(p_turn, 1)
                pe.wait_ge(p_aggt, w + 1)
                for k in range(2):
                    mm = pe.matmul(ps_1[:, 1, k * P:(k + 1) * P], agg_t[:, k, :], g.lin[:, k, :], start=True,
                                   stop=True, skip_group_check=True)
                mm.then_inc(p_upd, 1)
                pe.wait_ge(p_xn, w + 1)
                for k in range(2):
                    mm = pe.transpose(ps_2[:, 0, k * P:(k + 1) * P], xn[:, k * P:(k + 1) * P], g.ident[:])
                mm.then_inc(p_turn2, 1)
                pe.wait_ge(p_xnt, w + 1)
                pe.wait_ge(p_bias, w + 1)
                for k in range(2):
                    pe.matmul(ps_q[:, 0, :], xn_t[:, k, :], w_qkv[:, k, 0:512], start=(k == 0), stop=(k == 1))
                for k in range(2):
                    mm = pe.matmul(ps_q[:, 1, 0:256], xn_t[:, k, :], w_qkv[:, k, 512:768], start=(k == 0),
                                   stop=(k == 1))
                mm.then_inc(p_qkv, 1)

        @block.vector
        def _(dve):
            dve.sem_inc(p_bias, 1)
            dve.sem_inc(p_free, 2)
            dve.memset(eps[:], EPS).then_inc(p_eps, 1)
            dve.memset(g.q3[:, IDLE, :, :], 0.0)
            dve.wait_ge(p_w, 16 * 8)
            with dve.Fori(0, WINDOWS // 2) as t:
                for u in range(2):
                    w = t * 2 + u
                    chain = [w * 9]

                    def then(ins):
                        chain[0] = chain[0] + 1
                        ins.then_inc(p_chain, 1)
                        dve.wait_ge(p_chain, chain[0])

                    dve.wait_ge(p_upd, w + 1)
                    dve.wait_ge(x_landed[u], t * 16 + 16)
                    then(dve.scalar_tensor_tensor(y[:], xw[:, u, :], 2.0, ps_1[:, 1, :], ALU.mult, ALU.add))
                    then(dve.bn_stats(stats[:, 0, :], y[:]))
                    dve.memset(spare[:], 0.0)
                    dve.bn_aggr(mv[:, 0, :], stats[:, 0, :]).then_inc(p_stat, 1)
                    dve.wait_ge(p_dev, w * 2 + 1)
                    then(dve.reciprocal(rstd[:, 0:1], dev[:, 0:1]))
                    then(dve.tensor_scalar(x1[:], y[:], mv[:, 0, 0:1], rstd[:, 0:1], ALU.subtract, ALU.mult))
                    then(dve.bn_stats(stats[:, 1, :], x1[:]))
                    dve.memset(spare[:], 0.0)
                    dve.bn_aggr(mv[:, 1, :], stats[:, 1, :]).then_inc(p_stat, 1)
                    dve.wait_ge(p_dev, w * 2 + 2)
                    then(dve.reciprocal(rstd[:, 1:2], dev[:, 1:2]))
                    dve.tensor_scalar(xn[:], x1[:], mv[:, 1, 0:1], rstd[:, 1:2], ALU.subtract,
                                      ALU.mult).then_inc(p_xn, 1)
                    dve.tensor_copy(g.x1[:, bass.ds(w, 1), :].rearrange("p a d -> p (a d)"), x1[:])
                    dve.wait_ge(p_qkv, w + 1)
                    dve.wait_ge(p_free, w + 1)
                    dve.tensor_tensor(qkv[:, u, 0:512], ps_q[:, 0, :], b_qkv[:, 0:512], ALU.add)
                    dve.tensor_tensor(qkv[:, u, 512:768], ps_q[:, 1, 0:256], b_qkv[:, 512:768],
                                      ALU.add).then_inc(p_bias, 1)
                    dve.wait_ge(p_bias, w + 2)
                    q = qkv[:, u, 0:D]
                    q3 = [g.q3[:, bass.ds(w, 1), n, :].rearrange("p a d -> p (a d)") for n in range(3)]
                    then(dve.tensor_scalar(q, q, float(DH) ** -0.5, None, ALU.mult))
                    dve.tensor_copy(q3[0], q).then_inc(p_split, 1)
                    dve.wait_ge(p_split, w * 3 + 1)
                    then(dve.tensor_tensor(left[:], q, q3[0], ALU.subtract))
                    dve.tensor_copy(q3[1], left[:]).then_inc(p_split, 1)
                    dve.wait_ge(p_split, w * 3 + 2)
                    dve.tensor_tensor(q3[2], left[:], q3[1], ALU.subtract).then_inc(p_split, 1)
                    dve.wait_ge(p_split, w * 3 + 3)
                    then(dve.memset(y[:, 0:1], 0.0))

        @block.gpsimd
        def _(pool):
            pool.wait_ge(p_turn, WINDOWS + 1)
            pool.memset(g.acc[:], 0.0).then_inc(p_clear, 1)


def stage_scores(nc, g):
    with ExitStack() as ctx:
        def sb(name, shape, dt=F32):
            return ctx.enter_context(nc.sbuf_tensor(name, shape, dt))

        ef = sb("ef", [ED, 2, SUPER])
        w_e = sb("w_e", [ED, DH])
        b_e = sb("b_e", [P, DH])
        idx = sb("idx3", [P, TURN, CHUNKS], I32)
        key = sb("key", [P, TURN, CHUNKS, HEADS, DH])
        rec_v = sb("rec_v3", [P, 2, CHUNKS, 4])
        iota_w = sb("iota_w3", [P, 2, P])
        hot = sb("hot3", [P, 2, CHUNKS, P], BF16)
        hot_t = sb("hot_t", [P, 2, SUPER], BF16)
        ident_b = sb("ident_b", [P, P], BF16)
        ep = sb("ep", [P, 2, CHUNKS, DH])
        part = sb("part", [P, CHUNKS, HEADS])
        ps_t = ctx.enter_context(nc.psum_tensor("ps_t3", [P, 2, 2, SUPER], BF16))
        ps_e = ctx.enter_context(nc.psum_tensor("ps_e", [P, 2, 512], F32))
        ps_x = ctx.enter_context(nc.psum_tensor("ps_x", [P, 2, CHUNKS, D], F32))
        c_w = ctx.enter_context(nc.semaphore("c_w"))
        c_ef0 = ctx.enter_context(nc.semaphore("c_ef0"))
        c_ef1 = ctx.enter_context(nc.semaphore("c_ef1"))
        c_ef_used = ctx.enter_context(nc.semaphore("c_ef_used"))
        c_idx = ctx.enter_context(nc.semaphore("c_idx"))
        c_ask = ctx.enter_context(nc.semaphore("c_ask"))
        key_landed = [ctx.enter_context(nc.semaphore(f"c_key{u}")) for u in range(TURN)]
        c_key_used = ctx.enter_context(nc.semaphore("c_key_used"))
        c_rec = ctx.enter_context(nc.semaphore("c_rec"))
        c_hot = ctx.enter_context(nc.semaphore("c_hot"))
        c_turn = ctx.enter_context(nc.semaphore("c_turn"))
        c_hott = ctx.enter_context(nc.semaphore("c_hott"))
        c_eps = ctx.enter_context(nc.semaphore("c_eps"))
        c_ep = ctx.enter_context(nc.semaphore("c_ep"))
        c_qx = ctx.enter_context(nc.semaphore("c_qx"))
        c_sum = ctx.enter_context(nc.semaphore("c_sum"))
        c_mul = ctx.enter_context(nc.semaphore("c_mul"))
        c_red = ctx.enter_context(nc.semaphore("c_red"))
        c_add = ctx.enter_context(nc.semaphore("c_add"))
        c_id = ctx.enter_context(nc.semaphore("c_id"))
        c_zero = ctx.enter_context(nc.semaphore("c_zero"))
        ef_landed = (c_ef0, c_ef1)
        block = ctx.enter_context(nc.Block())

        @block.sync
        def _(sp):
            sp.dma_start(w_e[:], g.We).then_inc(c_w, 16)
            sp.dma_start(b_e[:], g.be.rearrange("(a d) -> a d", a=1).broadcast_to([P, DH])).then_inc(c_w, 16)
            sp.sem_inc(c_ef_used, 2)
            turns = sp.value_load(g.turns[0:1, 0:1], min_val=0, max_val=MAX_TURNS)
            with sp.Fori(0, turns) as t:
                for u in range(TURN):
                    i = t * TURN + u
                    sc, _w = step_of(nc, sp, g.code, i)
                    sp.wait_ge(c_ef_used, i + 1)
                    sp.dma_start(ef[:, u % 2, :], g.ef_t[:, bass.ds(sc * SUPER, SUPER)]).then_inc(ef_landed[u % 2], 16)

        @block.gpsimd
        def _(pool):
            pool.memset(g.score[:], 0.0).then_inc(c_zero, 1)
            pool.sem_inc(c_key_used, TURN)
            turns = pool.value_load(g.turns[0:1, 0:1], min_val=0, max_val=MAX_TURNS)
            with pool.Fori(0, turns) as t:
                for u in range(TURN):
                    i = t * TURN + u
                    sc, _w = step_of(nc, pool, g.code, i)
                    pool.wait_ge(c_key_used, i + 1)
                    pool.tensor_copy(idx[:, u, :], g.src_i[:, bass.ds(sc * CHUNKS, CHUNKS)]).then_inc(c_idx, 1)
                    pool.wait_ge(c_idx, i + 1)
                    pool.sem_inc(c_ask, 1)
                    for c in range(CHUNKS):
                            pool.indirect_dma_start(
                            out=key[:, u, c, :, :].rearrange("p a b -> p (a b)"), out_offset=None, in_=g.k_rows,
                            in_offset=bass.IndirectOffsetOnAxis(ap=idx[:, u, c:c + 1], axis=0),
                        ).then_inc(key_landed[u], 16)

        @block.scalar
        def _(act):
            turns = act.value_load(g.turns[0:1, 0:1], min_val=0, max_val=MAX_TURNS)
            act.sem_inc(c_mul, 2)
            with act.Fori(0, turns) as t:
                for u in range(TURN):
                    i = t * TURN + u
                    act.wait_ge(c_turn, i + 1)
                    act.wait_ge(c_mul, i + 1)
                    act.activation(hot_t[:, u % 2, :], ps_t[:, u % 2, 0, :], ACT.Copy).then_inc(c_hott, 1)

        @block.tensor
        def _(pe):
            pe.wait_ge(c_w, 32)
            pe.wait_ge(c_id, 1)
            turns = pe.value_load(g.turns[0:1, 0:1], min_val=0, max_val=MAX_TURNS)
            with pe.Fori(0, turns) as t:
                for u in range(TURN):
                    i = t * TURN + u
                    _sc, w = step_of(nc, pe, g.code, i)
                    pe.wait_ge(c_hot, i + 1)
                    for c in range(CHUNKS):
                        mm = pe.transpose(ps_t[:, u % 2, 0, c * P:(c + 1) * P], hot[:, u % 2, c, :], ident_b[:])
                    mm.then_inc(c_turn, 1)
                    pe.wait_ge(ef_landed[u % 2], t * (16 * TURN // 2) + 16 * (u // 2 + 1))
                    pe.wait_ge(c_mul, i + 1)
                    for c in range(CHUNKS):
                        mm = pe.matmul(ps_e[:, u % 2, c * DH:(c + 1) * DH], ef[:, u % 2, c * P:(c + 1) * P], w_e[:],
                                       start=True, stop=True, skip_group_check=True)
                    mm.then_inc(c_eps, 1)
                    pe.wait_ge(c_hott, i + 1)
                    for c in range(CHUNKS):
                        for n in range(3):
                            mm = pe.matmul(ps_x[:, u % 2, c, :], hot_t[:, u % 2, c * P:(c + 1) * P],
                                           g.q3[:, bass.ds(w, 1), n, :].rearrange("p a d -> p (a d)"),
                                           start=(n == 0), stop=(n == 2), skip_group_check=True)
                    mm.then_inc(c_qx, 1)

        @block.vector
        def _(dve):
            dve.sem_inc(c_add, 1)
            dve.tensor_copy(ident_b[:], g.ident[:]).then_inc(c_id, 1)
            dve.wait_ge(c_w, 32)
            dve.wait_ge(c_zero, 1)
            turns = dve.value_load(g.turns[0:1, 0:1], min_val=0, max_val=MAX_TURNS)

            def one_hots(i, u):
                sc, w = step_of(nc, dve, g.code, i)
                dve.tensor_copy(rec_v[:, u % 2], g.rec[:, bass.ds(sc * CHUNKS, CHUNKS), :])
                dve.tensor_copy(iota_w[:, u % 2], g.iota_node[:, bass.ds(w * P, P)]).then_inc(c_rec, 1)
                dve.wait_ge(c_rec, i + 1)
                for c in range(CHUNKS):
                    ins = dve.tensor_scalar(hot[:, u % 2, c, :], iota_w[:, u % 2], rec_v[:, u % 2, c, 0:1], None, ALU.is_equal)
                ins.then_inc(c_hot, 1)

            one_hots(0, 0)
            with dve.Fori(0, turns) as t:
                for u in range(TURN):
                    i = t * TURN + u
                    sc, _w = step_of(nc, dve, g.code, i)
                    one_hots(i + 1, u + 1)
                    dve.wait_ge(key_landed[u], (t + 1) * (16 * CHUNKS))
                    dve.wait_ge(c_eps, i + 1)
                    dve.tensor_tensor(ep[:, u % 2], ps_e[:, u % 2, 0:CHUNKS * DH].rearrange("p (c d) -> p c d", c=CHUNKS),
                                      b_e[:].rearrange("p (a d) -> p a d", a=1).broadcast_to([P, CHUNKS, DH]),
                                      ALU.add).then_inc(c_ep, 1)
                    dve.wait_ge(c_ep, i + 1)
                    k = key[:, u]
                    dve.tensor_tensor(k, k, ep[:, u % 2].rearrange("p c (h d) -> p c h d", h=1)
                                      .broadcast_to([P, CHUNKS, HEADS, DH]), ALU.add).then_inc(c_sum, 1)
                    dve.wait_ge(c_sum, i + 1)
                    dve.wait_ge(c_qx, i + 1)
                    flat = k.rearrange("p c h d -> p (c h d)")
                    dve.tensor_tensor(flat, flat, ps_x[:, u % 2].rearrange("p c d -> p (c d)"),
                                      ALU.mult).then_inc(c_mul, 1)
                    dve.wait_ge(c_mul, i + 3)
                    dve.tensor_reduce(part[:], k, AX.X, ALU.add).then_inc(c_red, 1)
                    dve.wait_ge(c_red, i + 1)
                    dve.sem_inc(c_key_used, 1)
                    dve.sem_inc(c_ef_used, 1)
                    mine = g.score[:, bass.ds(sc * CHUNKS, CHUNKS), :]
                    dve.wait_ge(c_add, i + 1)
                    dve.tensor_tensor(mine, mine, part[:], ALU.add).then_inc(c_add, 1)


def stage_softmax(nc, g):
    with ExitStack() as ctx:
        def sb(name, shape, dt=F32):
            return ctx.enter_context(nc.sbuf_tensor(name, shape, dt))

        row = sb("row", [P, BLOCK_EDGES])
        top = sb("top", [P, BLOCK_EDGES])
        dst_r = sb("dst_r", [P, BLOCK_EDGES + 2], I32)
        new = sb("new", [P, BLOCK_EDGES + 1])
        ends = sb("ends", [P, 2])
        ends_r = sb("ends_r", [1, 2, P])
        carry_r = sb("carry_r", [1, P])
        carry_c = sb("carry_c", [P, 1])
        edge_t = sb("edge_t", [P, COLS])
        one = sb("one", [1, 1])
        ps_r = ctx.enter_context(nc.psum_tensor("ps_r", [P, 4, 512], F32))
        ps_e = ctx.enter_context(nc.psum_tensor("ps_e4", [P, 512], F32))
        x_dst = ctx.enter_context(nc.semaphore("x_dst"))
        x_ew = ctx.enter_context(nc.semaphore("x_ew"))
        x_turn = ctx.enter_context(nc.semaphore("x_turn"))
        x_row = ctx.enter_context(nc.semaphore("x_row"))
        x_dve = ctx.enter_context(nc.semaphore("x_dve"))
        x_pe = ctx.enter_context(nc.semaphore("x_pe"))
        x_exp = ctx.enter_context(nc.semaphore("x_exp"))
        x_back = ctx.enter_context(nc.semaphore("x_back"))
        x_out = ctx.enter_context(nc.semaphore("x_out"))
        block = ctx.enter_context(nc.Block())
        GB = 4
        NG = -(-GROUPS // GB)

        def blocks(c):
            return top[:, c * P:(c + 1) * P]

        @block.sync
        def _(sp):
            sp.dma_start(dst_r[:], bass.AP(g.dst_row.tensor, 0, [[BLOCK_EDGES, BLOCKS], [0, HEADS],
                                                                  [1, BLOCK_EDGES + 2]])).then_inc(x_dst, 16)

        @block.tensor
        def _(pe):
            pe.wait_ge(x_ew, 1)
            for n in range(NG):
                if n >= 4:
                    pe.wait_ge(x_row, n - 3)
                for m in range(min(GB, GROUPS - n * GB)):
                    mm = pe.transpose(ps_r[:, n % 4, m * P:(m + 1) * P], blocks(n * GB + m), g.ident[:])
                mm.then_inc(x_turn, 1)
            for k in range(2):
                pe.wait_ge(x_pe, 2 * k + 1)
                pe.transpose(ps_e[0:1, 0:P], ends[:, 0:1], g.ident[:])
                pe.transpose(ps_e[0:1, P:2 * P], ends[:, 1:2], g.ident[:]).then_inc(x_turn, 1)
                pe.wait_ge(x_pe, 2 * k + 2)
                pe.matmul(ps_e[:, 256 + k:257 + k], carry_r[:], one[:], start=True, stop=True,
                          skip_group_check=True).then_inc(x_turn, 1)
            for n in range(NG):
                pe.wait_ge(x_exp, n + 1)
                if n >= 4:
                    pe.wait_ge(x_out, n - 3)
                for m in range(min(GB, GROUPS - n * GB)):
                    c = n * GB + m
                    mm = pe.transpose(ps_r[:, n % 4, m * P:(m + 1) * P], row[:, c * P:(c + 1) * P], g.ident[:])
                mm.then_inc(x_back, 1)

        @block.scalar
        def _(act):
            for n in range(NG):
                w = min(GB, GROUPS - n * GB) * P
                act.wait_ge(x_turn, n + 1)
                act.activation(row[:, n * GB * P:n * GB * P + w], ps_r[:, n % 4, 0:w],
                               ACT.Copy).then_inc(x_row, 1)
            act.wait_ge(x_dve, 1)
            for n in range(NG):
                w = min(GB, GROUPS - n * GB) * P
                cut = row[:, n * GB * P:n * GB * P + w]
                act.activation(cut, cut, ACT.Exp).then_inc(x_exp, 1)

        @block.vector
        def _(dve):
            chain = [0]
            link = ctx.enter_context(nc.semaphore("x_link"))

            def then(ins):
                chain[0] += 1
                ins.then_inc(link, 1)
                dve.wait_ge(link, chain[0])

            dve.memset(one[:], 1.0)
            dve.tensor_tensor(top[:].rearrange("p (c b h) -> p b c h", b=BLOCKS, h=HEADS),
                              g.score[:].rearrange("p (b c) h -> p b c h", b=BLOCKS),
                              g.ew[:].rearrange("p (b c h) -> p b c h", b=BLOCKS, h=1)
                              .broadcast_to([P, BLOCKS, GROUPS, HEADS]), ALU.mult).then_inc(x_ew, 1)
            dve.wait_ge(x_dst, 16)
            then(dve.tensor_tensor(new[:], dst_r[:, 1:], dst_r[:, :-1], ALU.not_equal))
            then(dve.tensor_scalar(new[:], new[:], NEG, None, ALU.mult))
            dve.wait_ge(x_row, NG)
            start, nxt = new[:, 0:BLOCK_EDGES], new[:, 1:BLOCK_EDGES + 1]

            def sweep(k, data, pen, initial, out):
                then(dve.tensor_tensor_scan(out, pen, data, initial, ALU.add, ALU.max))

            for k, (data, pen, out) in enumerate(((row[:], start, top[:]),
                                                  (top[:][:, ::-1], nxt[:, ::-1], top[:][:, ::-1]))):
                if k == 0:
                    sweep(k, data, pen, NEG, out)
                else:
                    sweep(k, data, pen, NEG, out)
                at = BLOCK_EDGES - 1 if k == 0 else 0
                then(dve.tensor_copy(ends[:, 0:1], top[:, at:at + 1]))
                dve.tensor_reduce(ends[:, 1:2], pen if k == 0 else nxt, AX.X, ALU.min).then_inc(x_pe, 1)
                dve.wait_ge(x_turn, NG + 2 * k + 1)
                then(dve.tensor_copy(ends_r[:], ps_e[0:1, 0:2 * P].rearrange("p (a b) -> p a b", a=2)))
                then(dve.memset(carry_r[:], NEG))
                for h in range(HEADS):
                    last = ends_r[:, 0, h::HEADS]
                    keep = ends_r[:, 1, h::HEADS]
                    take = carry_r[:, h::HEADS]
                    n = BLOCKS - 1
                    if k == 0:
                        last, keep, take = last[:, 0:n], keep[:, 0:n], take[:, 1:]
                    else:
                        last, keep, take = last[:, 1:][:, ::-1], keep[:, 1:][:, ::-1], take[:, 0:n][:, ::-1]
                    ins = dve.tensor_tensor_scan(take, keep, last, NEG, ALU.add, ALU.max)
                ins.then_inc(x_pe, 1)
                dve.wait_ge(x_turn, NG + 2 * k + 2)
                then(dve.tensor_copy(carry_c[:], ps_e[:, 256 + k:257 + k]))
                sweep(k, data, pen, carry_c[:], out)
            dve.tensor_tensor(row[:], row[:], top[:], ALU.subtract).then_inc(x_dve, 1)
            for n in range(NG):
                m = min(GB, GROUPS - n * GB)
                dve.wait_ge(x_back, n + 1)
                where = g.score[:].rearrange("p (b c) h -> p c b h", b=BLOCKS)[:, n * GB:n * GB + m]
                dve.tensor_copy(where, ps_r[:, n % 4, 0:m * P].rearrange("p (c b h) -> p c b h", c=m, b=BLOCKS)
                                ).then_inc(x_out, 1)


def stage_values(nc, g):
    with ExitStack() as ctx:
        def sb(name, shape, dt=F32):
            return ctx.enter_context(nc.sbuf_tensor(name, shape, dt))

        idx = sb("idx5", [P, TURN, CHUNKS], I32)
        val = sb("val", [P, TURN, CHUNKS, HEADS, DH])
        rec_v = sb("rec_v5", [P, 2, CHUNKS, 4])
        iota_w = sb("iota_w5", [P, 2, P])
        hot = sb("hot5", [P, 2, CHUNKS, P])
        msg = sb("msg5", [P, 2, CHUNKS, D + HEADS])
        ps_a = ctx.enter_context(nc.psum_tensor("ps_a5", [P, 2, 512], F32))
        v_idx = ctx.enter_context(nc.semaphore("v_idx"))
        v_ask = ctx.enter_context(nc.semaphore("v_ask"))
        val_landed = [ctx.enter_context(nc.semaphore(f"v_val{u}")) for u in range(TURN)]
        v_used = ctx.enter_context(nc.semaphore("v_used"))
        v_rec = ctx.enter_context(nc.semaphore("v_rec"))
        v_p = ctx.enter_context(nc.semaphore("v_p"))
        v_msg = ctx.enter_context(nc.semaphore("v_msg"))
        v_sum = ctx.enter_context(nc.semaphore("v_sum"))
        v_acc = ctx.enter_context(nc.semaphore("v_acc"))
        v_clear = ctx.enter_context(nc.semaphore("v_clear"))
        block = ctx.enter_context(nc.Block())

        @block.gpsimd
        def _(pool):
            pool.sem_inc(v_used, TURN)
            turns = pool.value_load(g.turns[0:1, 0:1], min_val=0, max_val=MAX_TURNS)
            with pool.Fori(0, turns) as t:
                for u in range(TURN):
                    i = t * TURN + u
                    sc, _w = step_of(nc, pool, g.code, i)
                    pool.wait_ge(v_used, i + 1)
                    pool.tensor_copy(idx[:, u, :], g.src_i[:, bass.ds(sc * CHUNKS, CHUNKS)]).then_inc(v_idx, 1)
                    pool.wait_ge(v_idx, i + 1)
                    pool.sem_inc(v_ask, 1)
                    for c in range(CHUNKS):
                            pool.indirect_dma_start(
                            out=val[:, u, c, :, :].rearrange("p a b -> p (a b)"), out_offset=None, in_=g.v_rows,
                            in_offset=bass.IndirectOffsetOnAxis(ap=idx[:, u, c:c + 1], axis=0),
                        ).then_inc(val_landed[u], 16)

        @block.tensor
        def _(pe):
            turns = pe.value_load(g.turns[0:1, 0:1], min_val=0, max_val=MAX_TURNS)
            pe.wait_ge(v_clear, 1)
            with pe.Fori(0, turns) as t:
                for u in range(TURN):
                    i = t * TURN + u
                    pe.wait_ge(v_msg, i + 1)
                    pe.wait_ge(v_acc, i + 1)
                    for c in range(CHUNKS):
                        mm = pe.matmul(ps_a[:, u % 2, 0:D + HEADS], hot[:, u % 2, c, :], msg[:, u % 2, c, :],
                                       start=(c == 0), stop=(c == CHUNKS - 1))
                    mm.then_inc(v_sum, 1)

        @block.vector
        def _(dve):
            dve.sem_inc(v_sum, 2)
            dve.sem_inc(v_acc, 1)
            dve.memset(ps_a[:], 0.0).then_inc(v_clear, 1)
            dve.wait_ge(v_clear, 1)
            turns = dve.value_load(g.turns[0:1, 0:1], min_val=0, max_val=MAX_TURNS)

            def add_sums(i, u):
                _sc, w = step_of(nc, dve, g.code_before, i)
                dve.wait_ge(v_sum, i + 2)
                dve.wait_ge(v_acc, i + 1)
                dve.tensor_tensor(g.acc[:, bass.ds(w, 1), :], g.acc[:, bass.ds(w, 1), :],
                                  ps_a[:, (u + 1) % 2:(u + 1) % 2 + 1, 0:D + HEADS], ALU.add).then_inc(v_acc, 1)

            with dve.Fori(0, turns) as t:
                for u in range(TURN):
                    i = t * TURN + u
                    sc, w = step_of(nc, dve, g.code, i)
                    r, m = rec_v[:, u % 2], msg[:, u % 2]
                    dve.wait_ge(v_sum, i + 1)
                    dve.tensor_copy(r, g.rec[:, bass.ds(sc * CHUNKS, CHUNKS), :])
                    dve.tensor_copy(m[:, :, D:], g.score[:, bass.ds(sc * CHUNKS, CHUNKS), :])
                    dve.tensor_copy(iota_w[:, u % 2], g.iota_node[:, bass.ds(w * P, P)]).then_inc(v_rec, 1)
                    dve.wait_ge(v_rec, i + 1)
                    for c in range(CHUNKS):
                        dve.tensor_scalar(hot[:, u % 2, c, :], iota_w[:, u % 2], r[:, c, 0:1], None, ALU.is_equal)
                    dve.wait_ge(val_landed[u], (t + 1) * (16 * CHUNKS))
                    p = m[:, :, D:].rearrange("p c (h d) -> p c h d", d=1).broadcast_to([P, CHUNKS, HEADS, DH])
                    dve.tensor_tensor(m[:, :, 0:D].rearrange("p c (h d) -> p c h d", h=HEADS), val[:, u], p,
                                      ALU.mult).then_inc(v_msg, 1)
                    add_sums(i, u)
                    dve.wait_ge(v_msg, i + 1)
                    dve.sem_inc(v_used, 1)
            add_sums(turns * TURN, TURN)


def stage_output(nc, g):
    FT = FF // P
    with ExitStack() as ctx:
        def sb(name, shape, dt=F32):
            return ctx.enter_context(nc.sbuf_tensor(name, shape, dt))

        w_o = sb("w_o", [P, 2, D])
        w_1 = sb("w_1", [P, 2, FF])
        w_2 = sb("w_2", [P, FT, D])
        b_o = sb("b_o", [P, D])
        b_2 = sb("b_2", [P, D])
        b_1 = sb("b_1", [P, FT])
        gain = sb("gain6", [P, 2])
        shift = sb("shift6", [P, 2])
        alpha = sb("alpha", [P, 1])
        beta = sb("beta", [P, 1])
        eps = sb("eps6", [P, 1])
        den = sb("den", [P, HEADS])
        att = sb("att", [P, D])
        att_t = sb("att_t", [P, 2, P])
        t_o = sb("t_o", [P, D])
        x2 = sb("x2", [P, D])
        stats = sb("stats6", [P, 2, 6])
        mv = sb("mv6", [P, 2, 2])
        dev = sb("dev6", [P, 2])
        rstd = sb("rstd6", [P, 2])
        xn = sb("xn6", [P, D])
        xn_t = sb("xn_t6", [P, 2, P])
        gel = sb("gel", [P, FT, P])
        y = sb("y6", [P, D])
        res = sb("res", [P, 2, D])
        spare = sb("spare6", [P, 1])
        ps_1 = ctx.enter_context(nc.psum_tensor("ps_16", [P, 2, 2 * P], F32))
        ps_2 = ctx.enter_context(nc.psum_tensor("ps_26", [P, 2 * P], F32))
        ps_f = ctx.enter_context(nc.psum_tensor("ps_f", [P, FT, P], F32))
        ps_y = ctx.enter_context(nc.psum_tensor("ps_y", [P, D], F32))
        o_w = ctx.enter_context(nc.semaphore("o_w"))
        o_eps = ctx.enter_context(nc.semaphore("o_eps"))
        o_att = ctx.enter_context(nc.semaphore("o_att"))
        o_turn = ctx.enter_context(nc.semaphore("o_turn"))
        o_attt = ctx.enter_context(nc.semaphore("o_attt"))
        o_o = ctx.enter_context(nc.semaphore("o_o"))
        o_stat = ctx.enter_context(nc.semaphore("o_stat"))
        o_dev = ctx.enter_context(nc.semaphore("o_dev"))
        o_xn = ctx.enter_context(nc.semaphore("o_xn"))
        o_turn2 = ctx.enter_context(nc.semaphore("o_turn2"))
        o_xnt = ctx.enter_context(nc.semaphore("o_xnt"))
        o_ff = ctx.enter_context(nc.semaphore("o_ff"))
        o_gel = ctx.enter_context(nc.semaphore("o_gel"))
        o_y = ctx.enter_context(nc.semaphore("o_y"))
        o_res = ctx.enter_context(nc.semaphore("o_res"))
        o_st0 = ctx.enter_context(nc.semaphore("o_st0"))
        o_st1 = ctx.enter_context(nc.semaphore("o_st1"))
        o_chain = ctx.enter_context(nc.semaphore("o_chain"))
        o_free = ctx.enter_context(nc.semaphore("o_free"))
        stored = (o_st0, o_st1)
        block = ctx.enter_context(nc.Block())

        @block.sync
        def _(sp):
            sp.dma_start(w_o[:], g.Wo.rearrange("(k p) n -> p k n", p=P)).then_inc(o_w, 16)
            sp.dma_start(w_1[:], g.W1.rearrange("(k p) n -> p k n", p=P)).then_inc(o_w, 16)
            sp.dma_start(w_2[:], g.W2.rearrange("(k p) n -> p k n", p=P)).then_inc(o_w, 16)
            for tile, b in ((b_o, g.bo), (b_2, g.b2)):
                sp.dma_start(tile[:], b.rearrange("(a d) -> a d", a=1).broadcast_to([P, D])).then_inc(o_w, 16)
            for tile, b in ((alpha, g.alpha), (beta, g.beta)):
                sp.dma_start(tile[:], b.rearrange("(a d) -> a d", a=1).broadcast_to([P, 1])).then_inc(o_w, 16)
            sp.dma_start(gain[:], g.ln2_g).then_inc(o_w, 16)
            sp.dma_start(shift[:], g.ln2_b).then_inc(o_w, 16)
            sp.dma_start(b_1[:], g.b1).then_inc(o_w, 16)
            with sp.Fori(0, WINDOWS // 2) as t:
                for u in range(2):
                    w = t * 2 + u
                    sp.wait_ge(o_res, w + 1)
                    sp.dma_start(g.out[bass.ds(w * P, P), :], res[:, u, :]).then_inc(stored[u], 16)
                    sp.wait_ge(stored[u], t * 16 + 16)
                    sp.sem_inc(o_free, 1)

        @block.scalar
        def _(act):
            act.wait_ge(o_eps, 1)
            act.wait_ge(o_w, 16 * 10)
            with act.Fori(0, WINDOWS) as w:
                act.wait_ge(o_turn, w + 1)
                act.activation(att_t[:].rearrange("p a b -> p (a b)"), ps_1[:, 0, :], ACT.Copy).then_inc(o_attt, 1)
                act.wait_ge(o_stat, w * 2 + 1)
                act.activation(dev[:, 0:1], mv[:, 0, 1:2], ACT.Sqrt, bias=eps[:]).then_inc(o_dev, 1)
                act.wait_ge(o_turn2, w + 1)
                for k in range(2):
                    ins = act.activation(xn_t[:, k, :], ps_2[:, k * P:(k + 1) * P], ACT.Identity,
                                         bias=shift[:, k:k + 1], scale=gain[:, k:k + 1])
                ins.then_inc(o_xnt, 1)
                act.wait_ge(o_ff, w + 1)
                for f in range(FT):
                    ins = act.activation(gel[:, f, :], ps_f[:, f, :], ACT.Gelu, bias=b_1[:, f:f + 1])
                ins.then_inc(o_gel, 1)
                act.wait_ge(o_stat, w * 2 + 2)
                act.activation(dev[:, 1:2], mv[:, 1, 1:2], ACT.Sqrt, bias=eps[:]).then_inc(o_dev, 1)

        @block.tensor
        def _(pe):
            pe.wait_ge(o_w, 16 * 10)
            with pe.Fori(0, WINDOWS) as w:
                pe.wait_ge(o_att, w + 1)
                for k in range(2):
                    mm = pe.transpose(ps_1[:, 0, k * P:(k + 1) * P], att[:, k * P:(k + 1) * P], g.ident[:])
                mm.then_inc(o_turn, 1)
                pe.wait_ge(o_attt, w + 1)
                for k in range(2):
                    mm = pe.matmul(ps_1[:, 1, :], att_t[:, k, :], w_o[:, k, :], start=(k == 0), stop=(k == 1),
                                   skip_group_check=True)
                mm.then_inc(o_o, 1)
                pe.wait_ge(o_xn, w + 1)
                for k in range(2):
                    mm = pe.transpose(ps_2[:, k * P:(k + 1) * P], xn[:, k * P:(k + 1) * P], g.ident[:])
                mm.then_inc(o_turn2, 1)
                pe.wait_ge(o_xnt, w + 1)
                for f in range(FT):
                    for k in range(2):
                        mm = pe.matmul(ps_f[:, f, :], w_1[:, k, f * P:(f + 1) * P], xn_t[:, k, :], start=(k == 0),
                                       stop=(k == 1))
                mm.then_inc(o_ff, 1)
                pe.wait_ge(o_gel, w + 1)
                for f in range(FT):
                    mm = pe.matmul(ps_y[:], gel[:, f, :], w_2[:, f, :], start=(f == 0), stop=(f == FT - 1))
                mm.then_inc(o_y, 1)

        @block.vector
        def _(dve):
            dve.sem_inc(o_free, 2)
            dve.memset(eps[:], EPS).then_inc(o_eps, 1)
            dve.wait_ge(o_w, 16 * 10)
            with dve.Fori(0, WINDOWS // 2) as t:
                for u in range(2):
                    w = t * 2 + u
                    chain = [w * 15]

                    def then(ins):
                        chain[0] = chain[0] + 1
                        ins.then_inc(o_chain, 1)
                        dve.wait_ge(o_chain, chain[0])

                    now = g.acc[:, bass.ds(w, 1), :].rearrange("p a d -> p (a d)")
                    x1 = g.x1[:, bass.ds(w, 1), :].rearrange("p a d -> p (a d)")
                    then(dve.tensor_scalar(den[:], now[:, D:], TINY, None, ALU.max))
                    then(dve.reciprocal(den[:], den[:]))
                    dve.tensor_tensor(att[:].rearrange("p (h d) -> p h d", h=HEADS),
                                      now[:, 0:D].rearrange("p (h d) -> p h d", h=HEADS),
                                      den[:].rearrange("p (h d) -> p h d", d=1).broadcast_to([P, HEADS, DH]),
                                      ALU.mult).then_inc(o_att, 1)
                    dve.wait_ge(o_o, w + 1)
                    then(dve.tensor_tensor(t_o[:], ps_1[:, 1, :], b_o[:], ALU.add))
                    then(dve.scalar_tensor_tensor(x2[:], t_o[:], alpha[:], x1, ALU.mult, ALU.add))
                    then(dve.bn_stats(stats[:, 0, :], x2[:]))
                    dve.memset(spare[:], 0.0)
                    dve.bn_aggr(mv[:, 0, :], stats[:, 0, :]).then_inc(o_stat, 1)
                    dve.wait_ge(o_dev, w * 2 + 1)
                    then(dve.reciprocal(rstd[:, 0:1], dev[:, 0:1]))
                    dve.tensor_scalar(xn[:], x2[:], mv[:, 0, 0:1], rstd[:, 0:1], ALU.subtract,
                                      ALU.mult).then_inc(o_xn, 1)
                    then(dve.tensor_tensor(x2[:], x2[:], x1, ALU.add))
                    dve.wait_ge(o_y, w + 1)
                    then(dve.tensor_tensor(y[:], ps_y[:], b_2[:], ALU.add))
                    then(dve.scalar_tensor_tensor(y[:], y[:], beta[:], x2[:], ALU.mult, ALU.add))
                    then(dve.bn_stats(stats[:, 1, :], y[:]))
                    dve.memset(spare[:], 0.0)
                    dve.bn_aggr(mv[:, 1, :], stats[:, 1, :]).then_inc(o_stat, 1)
                    dve.wait_ge(o_dev, w * 2 + 2)
                    then(dve.reciprocal(rstd[:, 1:2], dev[:, 1:2]))
                    dve.wait_ge(o_free, w + 1)
                    dve.tensor_scalar(res[:, u, :], y[:], mv[:, 1, 0:1], rstd[:, 1:2], ALU.subtract,
                                      ALU.mult).then_inc(o_res, 1)
                    dve.wait_ge(o_res, w + 1)
                    for _ in range(4):
                        dve.sem_inc(o_chain, 1)


def build(nc, g):
    g.k_rows = nc.dram_tensor("k_rows", (NODES_PAD, D), F32).ap()
    g.v_rows = nc.dram_tensor("v_rows", (NODES_PAD, D), F32).ap()
    with ExitStack() as ctx:
        def sb(name, shape, dt=F32, within=ctx):
            return within.enter_context(nc.sbuf_tensor(name, shape, dt))

        g.ident = sb("ident", [P, P])
        g.ones = sb("ones", [P, P])
        g.iota_node = sb("iota_node", [P, (WINDOWS + 1) * P])
        codes = sb("codes", [1, TABLE + 1], I32)
        g.code, g.code_before = codes[:, 1:TABLE + 1], codes[:, 0:TABLE]
        g.turns = sb("turns", [1, 1], I32)
        g.src_i = sb("src_i", [P, COLS], I32)
        g.ew = sb("ew", [P, COLS])
        g.rec = sb("rec", [P, COLS, 4])
        g.acc = sb("acc", [P, WINDOWS + 1, D + HEADS])
        g.w1 = sb("w1", [P, 2 * NH])
        g.w2 = sb("w2", [2 * NH, 2, NPATH * MUL])
        g.lin = sb("lin", [P, 2, P])
        stage_tables(nc, g)
        stage_messages(nc, g)
        g.x1 = sb("x1", [P, WINDOWS, D])
        g.score = sb("score", [P, COLS, HEADS])
        with ExitStack() as queries:
            g.q3 = sb("q3", [P, WINDOWS + 1, 3, D], BF16, within=queries)
            stage_project(nc, g)
            stage_scores(nc, g)
        stage_softmax(nc, g)
        stage_values(nc, g)
        stage_output(nc, g)


def by_edge(a, fill):
    a = np.asarray(a)
    full = np.full((EDGES_PAD,) + a.shape[1:], fill, a.dtype)
    full[:EDGES] = a
    return np.ascontiguousarray(np.moveaxis(full.reshape((COLS, P) + a.shape[1:]), 0, 1))


def by_feature(a):
    a = np.asarray(a)
    full = np.zeros((a.shape[1], EDGES_PAD), a.dtype)
    full[:, :EDGES] = a.T
    return full


def by_half(a):
    rows = by_feature(a)
    return np.ascontiguousarray(rows.reshape(len(rows), SUPERS, 2, SUPER // 2).transpose(2, 0, 1, 3)
                                .reshape(2 * len(rows), EDGES_PAD // 2))


def kernel(**inputs):
    import concourse.bacc as bacc
    from concourse.bass_utils import run_bass_kernel_spmd

    order = np.concatenate([np.arange(MUL)] + [MUL + 3 * np.arange(MUL) + j for j in range(3)])
    a = {n: np.asarray(v) for n, v in inputs.items()}
    x = np.zeros((NODES_PAD + 2 * P, D), a["x"].dtype)
    x[:NODES] = a["x"][:, order]
    dst_row = np.full((EDGES_PAD + 2,), -1, a["dst"].dtype)
    dst_row[1:EDGES + 1] = a["dst"]
    l1 = {n[len("L1_gnn_"):]: v for n, v in a.items() if n.startswith("L1_gnn_")}
    columns = lambda v: np.ascontiguousarray(v.reshape(-1, P).T)
    laid = {
        "src_t": by_edge(a["src"], 0), "dst_t": by_edge(a["dst"], -1), "dst_row": dst_row,
        "vec_t": by_edge(a["edge_attr_3"], 0), "ew_t": by_edge(a["edge_weight"], 0),
        "emb_t": by_half(a["edge_attr_8"]), "ef_t": by_feature(a["edge_attr_64"]),
        "x_rows": x,
        "fc_w1": a["L0_gnn_fc_w1"], "fc_w2": a["L0_gnn_fc_w2"],
        "lin_w0": a["L0_gnn_lin_w0"], "lin_w1": a["L0_gnn_lin_w1"],
        "Wq": l1["Wq"][order], "Wk": l1["Wk"][order], "Wv": l1["Wv"][order],
        "bq": l1["bq"], "bk": l1["bk"], "bv": l1["bv"], "We": l1["We"], "be": l1["be"],
        "Wo": l1["Wo"][:, order], "bo": l1["bo"][order],
        "ln1_g": columns(l1["ln1_g"][order]), "ln1_b": columns(l1["ln1_b"][order]),
        "ln2_g": columns(l1["ln2_g"][order]), "ln2_b": columns(l1["ln2_b"][order]),
        "W1": l1["W1"][order], "b1": columns(l1["b1"]), "W2": l1["W2"][:, order], "b2": l1["b2"][order],
        "alpha": l1["alpha"], "beta": l1["beta"],
    }
    nc = bacc.Bacc("TRN2", target_bir_lowering=False, num_devices=1)
    dram = {name: nc.dram_tensor("in_" + name, v.shape, mybir.dt.from_np(v.dtype), kind="ExternalInput").ap()
            for name, v in laid.items()}
    g = Held()
    g.src_t = dram["src_t"]
    g.dst_t = dram["dst_t"]
    g.dst_row = dram["dst_row"]
    g.vec_t = dram["vec_t"]
    g.ew_t = dram["ew_t"]
    g.emb_t = dram["emb_t"]
    g.ef_t = dram["ef_t"]
    g.x_rows = dram["x_rows"]
    g.fc_w1 = dram["fc_w1"]
    g.fc_w2 = dram["fc_w2"]
    g.lin_w0 = dram["lin_w0"]
    g.lin_w1 = dram["lin_w1"]
    g.Wq = dram["Wq"]
    g.Wk = dram["Wk"]
    g.Wv = dram["Wv"]
    g.bq = dram["bq"]
    g.bk = dram["bk"]
    g.bv = dram["bv"]
    g.We = dram["We"]
    g.be = dram["be"]
    g.Wo = dram["Wo"]
    g.bo = dram["bo"]
    g.ln1_g = dram["ln1_g"]
    g.ln1_b = dram["ln1_b"]
    g.ln2_g = dram["ln2_g"]
    g.ln2_b = dram["ln2_b"]
    g.W1 = dram["W1"]
    g.b1 = dram["b1"]
    g.W2 = dram["W2"]
    g.b2 = dram["b2"]
    g.alpha = dram["alpha"]
    g.beta = dram["beta"]
    arrays = {"in_" + name: np.ascontiguousarray(v) for name, v in laid.items()}
    g.w_qkv, g.b_qkv = (g.Wq, g.Wk, g.Wv), (g.bq, g.bk, g.bv)
    g.out = nc.dram_tensor("out", (NODES_PAD, D), F32, kind="ExternalOutput").ap()
    build(nc, g)
    r = run_bass_kernel_spmd(nc, [arrays], core_ids=[0])
    got = r.results[0]["out"][:NODES]
    back = np.empty_like(got)
    back[:, order] = got
    return back
```

```python
from contextlib import ExitStack

import numpy as np

import concourse.bass as bass
from concourse import mybir

F32 = mybir.dt.float32
BF16 = mybir.dt.bfloat16
I32 = mybir.dt.int32
ALU = mybir.AluOpType
ACT = mybir.ActivationFunctionType
AX = mybir.AxisListType

P = 128
NODES = 2500
EDGES = 82500
MUL = 64
D = 4 * MUL
HEADS = 8
DH = D // HEADS
ED = 64
NB = 8
NH = 64
NPATH = 5
FF = 4 * D
EPS = 1e-5
AVG_NEIGH = 16.0

WINDOWS = -(-NODES // P)
CHUNKS = 4
SUPER = CHUNKS * P
BLOCKS = P // HEADS
COLS = -(-(-(-EDGES // P)) // BLOCKS) * BLOCKS
GROUPS = COLS // BLOCKS
BLOCK_EDGES = GROUPS * P
SUPERS = COLS // CHUNKS
EDGES_PAD = COLS * P
NODES_PAD = WINDOWS * P
SPAN = 32
IDLE = WINDOWS
TURN = 4
TABLE = -(-(SUPERS * WINDOWS + 2 * TURN) // 512) * 512
MAX_TURNS = TABLE // TURN - 2
FAR = 4096.0
NEG = -1.0e30
TINY = 1.0e-30


class Held:
    pass


def step_of(nc, eng, code_row, i):
    code = eng.value_load(code_row[0:1, bass.ds(i, 1)], min_val=0, max_val=(SUPERS - 1) * SPAN + IDLE)
    sc = nc.s_assert_within(eng.snap(code // SPAN), 0, SUPERS - 1,
                            skip_runtime_bounds_check_because="a step's code holds a super-chunk's number")
    w = nc.s_assert_within(eng.snap(code % SPAN), 0, IDLE,
                           skip_runtime_bounds_check_because="a step's code holds a window's number")
    return sc, w


def one_hots(dve, g, out, sc, w):
    nodes = g.iota_node[:, bass.ds(w * P, P)].rearrange("p (a n) -> p a n", a=1).broadcast_to([P, CHUNKS, P])
    receivers = g.rec[:, bass.ds(sc * CHUNKS, CHUNKS), 0:1].broadcast_to([P, CHUNKS, P])
    return dve.tensor_tensor(out, nodes, receivers, ALU.is_equal)


def stage_tables(nc, g):
    with ExitStack() as ctx:
        def sb(name, shape, dt=F32):
            return ctx.enter_context(nc.sbuf_tensor(name, shape, dt))

        dst_i = sb("dst_i", [P, COLS], I32)
        win_i = sb("win_i", [P, COLS], I32)
        win_f = sb("win_f", [P, COLS])
        pad_far = sb("pad_far", [P, COLS])
        vec = sb("vec", [P, COLS, 3])
        vec2 = sb("vec2", [P, COLS, 3])
        length = sb("length", [P, COLS])
        inv_len = sb("inv_len", [P, COLS])
        win_hi = sb("win_hi", [P, SUPERS])
        win_lo = sb("win_lo", [P, SUPERS])
        hi = sb("hi", [P, 2])
        lo = sb("lo", [P, 2])
        count = sb("count", [P, 2])
        count0 = sb("count0", [P, 2])
        has = sb("has", [P, 2])
        first = sb("first", [P, 2])
        after = sb("after", [P, 2])
        code_of = sb("code_of", [P, 2])
        upper = sb("upper", [P, P])
        iota_step = sb("iota_step", [P, TABLE])
        from_first = sb("from_first", [P, 2, 512])
        member = sb("member", [P, 2, 512])
        code_t = sb("code_t", [1, 512])
        total = sb("total", [1, 2])
        total1 = sb("total1", [1, 1])
        total_i = sb("total_i", [1, 1], I32)
        along = sb("along", [P, COLS + 1], I32)
        falls = sb("falls", [P, COLS])
        fall = sb("fall", [P, 1])
        apart = sb("apart", [1, 1])
        step_blocks = sb("step_blocks", [1, 1], I32)
        blocks_f = sb("blocks_f", [1, 1])
        ps_t = ctx.enter_context(nc.psum_tensor("ps_t", [P, 2, 512], F32))
        ps_n = ctx.enter_context(nc.psum_tensor("ps_n", [P, 512], F32))
        ps_c = ctx.enter_context(nc.psum_tensor("ps_c", [1, 2, 512], F32))
        t_dst = ctx.enter_context(nc.semaphore("t_dst"))
        t_vec = ctx.enter_context(nc.semaphore("t_vec"))
        t_along = ctx.enter_context(nc.semaphore("t_along"))
        t_ew = ctx.enter_context(nc.semaphore("t_ew"))
        t_x = ctx.enter_context(nc.semaphore("t_x"))
        t_wz = ctx.enter_context(nc.semaphore("t_wz"))
        t_w = ctx.enter_context(nc.semaphore("t_w"))
        t_const = ctx.enter_context(nc.semaphore("t_const"))
        t_turn = ctx.enter_context(nc.semaphore("t_turn"))
        t_dve = ctx.enter_context(nc.semaphore("t_dve"))
        t_len = ctx.enter_context(nc.semaphore("t_len"))
        t_act = ctx.enter_context(nc.semaphore("t_act"))
        t_pe = ctx.enter_context(nc.semaphore("t_pe"))
        t_first = ctx.enter_context(nc.semaphore("t_first"))
        t_mem = ctx.enter_context(nc.semaphore("t_mem"))
        t_blocks = ctx.enter_context(nc.semaphore("t_blocks"))
        t_from = ctx.enter_context(nc.semaphore("t_from"))
        t_made = ctx.enter_context(nc.semaphore("t_made"))
        t_code = ctx.enter_context(nc.semaphore("t_code"))
        t_lin = ctx.enter_context(nc.semaphore("t_lin"))
        block = ctx.enter_context(nc.Block())

        @block.sync
        def _(sp):
            sp.dma_start(dst_i[:], g.dst_t).then_inc(t_dst, 16)
            sp.dma_start(vec[:], g.vec_t).then_inc(t_vec, 16)
            sp.dma_start(along[:], bass.AP(g.dst_row.tensor, 1, [[COLS, P], [1, COLS + 1]])).then_inc(t_along, 16)
            sp.dma_start(g.src_i[:], g.src_t).then_inc(t_x, 16)
            sp.dma_start(g.ew[:], g.ew_t).then_inc(t_ew, 16)
            sp.wait_ge(t_wz, 2)
            for half in range(2):
                sp.dma_start(g.w1[half * NB:(half + 1) * NB, half * NH:(half + 1) * NH], g.fc_w1).then_inc(t_w, 16)
                for path, place in enumerate((0, 4, 2, 1, 3)):
                    sp.dma_start(g.w2[half * NH:(half + 1) * NH, half, place * MUL:(place + 1) * MUL],
                                 g.fc_w2[:, path * MUL:(path + 1) * MUL]).then_inc(t_w, 16)
            sp.wait_ge(t_x, 16)
            sp.wait_ge(t_ew, 16)

        @block.gpsimd
        def _(pool):
            pool.memset(g.w1[:], 0.0).then_inc(t_wz, 1)
            pool.memset(g.w2[:], 0.0).then_inc(t_wz, 1)
            pool.iota(iota_step[:], [[1, TABLE]], base=0, channel_multiplier=0,
                      allow_small_or_imprecise_dtypes=True).then_inc(t_const, 1)
            pool.iota(g.iota_node[:], [[1, (WINDOWS + 1) * P]], base=0, channel_multiplier=0,
                      allow_small_or_imprecise_dtypes=True).then_inc(t_const, 1)
            pool.iota(first[:], [[P, 2]], base=0, channel_multiplier=1,
                      allow_small_or_imprecise_dtypes=True).then_inc(t_const, 1)
            pool.memset(g.ident[:], 0.0).then_inc(t_const, 1)
            pool.memset(upper[:], 1.0).then_inc(t_const, 1)
            pool.memset(g.ones[:], 1.0).then_inc(t_const, 1)
            pool.memset(g.acc[:], 0.0).then_inc(t_const, 1)
            pool.memset(g.lin[:], 0.0).then_inc(t_const, 1)
            pool.wait_ge(t_const, 8)
            pool.affine_select(out=g.ident[:], in_=g.ident[:], compare_op=ALU.not_equal, fill=1.0, base=0,
                               pattern=[[-1, P]], channel_multiplier=1).then_inc(t_const, 1)
            pool.affine_select(out=upper[:], in_=upper[:], compare_op=ALU.is_ge, fill=0.0, base=0,
                               pattern=[[1, P]], channel_multiplier=-1).then_inc(t_const, 1)
            pool.dma_start(g.lin[0:64, 0, 0:64], g.lin_w0).then_inc(t_lin, 16)
            pool.dma_start(g.lin[64:128, 0, 64:128], g.lin_w1).then_inc(t_lin, 16)
            pool.dma_start(g.lin[0:64, 1, 0:64], g.lin_w1).then_inc(t_lin, 16)
            pool.dma_start(g.lin[64:128, 1, 64:128], g.lin_w1).then_inc(t_lin, 16)
            pool.wait_ge(t_lin, 64)

        @block.scalar
        def _(act):
            act.wait_ge(t_len, 1)
            act.activation(length[:], length[:], ACT.Sqrt).then_inc(t_act, 1)

        @block.tensor
        def _(pe):
            pe.wait_ge(t_const, 10)
            pe.wait_ge(t_turn, 2)
            pe.transpose(ps_t[:, 0, 0:128], win_hi[:, 0:128], g.ident[:])
            pe.transpose(ps_t[0:SUPERS - 128, 0, 128:256], win_hi[:, 128:SUPERS], g.ident[:])
            pe.transpose(ps_t[:, 1, 0:128], win_lo[:, 0:128], g.ident[:])
            pe.transpose(ps_t[0:SUPERS - 128, 1, 128:256], win_lo[:, 128:SUPERS], g.ident[:]).then_inc(t_pe, 1)
            pe.wait_ge(t_turn, 3)
            pe.matmul(ps_n[:, 0:2], upper[:], count[:], start=True, stop=False)
            pe.matmul(ps_n[:, 0:2], g.ones[:], count0[:], start=False, stop=True)
            pe.matmul(ps_n[:, 8:9], g.ones[:], fall[:], start=True, stop=True, skip_group_check=True)
            pe.matmul(ps_n[0:1, 4:6], g.ones[:, 0:1], count[:], start=True, stop=True,
                      skip_group_check=True).then_inc(t_pe, 1)
            pe.wait_ge(t_blocks, 1)
            for c in range(2):
                mm = pe.transpose(ps_n[0:1, (c + 1) * P:(c + 2) * P], first[:, c:c + 1], g.ident[:])
            mm.then_inc(t_first, 1)
            blocks = pe.value_load(step_blocks[0:1, 0:1], min_val=1, max_val=TABLE // 512)
            with pe.Fori(0, blocks) as b:
                pe.wait_ge(t_mem, b + 1)
                for row, lhs in ((0, code_of), (1, g.ones)):
                    for c in range(2):
                        mm = pe.matmul(ps_c[:, row, :], lhs[:, c:c + 1], member[:, c, :],
                                       start=(c == 0), stop=(c == 1))
                mm.then_inc(t_made, 1)

        @block.vector
        def _(dve):
            done = [0]

            def then(ins):
                done[0] += 1
                ins.then_inc(t_dve, 1)
                dve.wait_ge(t_dve, done[0])

            dve.wait_ge(t_dst, 16)
            then(dve.tensor_scalar(win_i[:], dst_i[:], 7, None, ALU.arith_shift_right))
            then(dve.tensor_copy(win_f[:], win_i[:]))
            then(dve.tensor_scalar(pad_far[:], win_f[:], 0.0, -FAR, ALU.is_lt, ALU.mult))
            then(dve.scalar_tensor_tensor(pad_far[:], win_f[:], -1.0, pad_far[:], ALU.mult, ALU.add))
            dve.tensor_reduce(win_hi[:], win_f[:].rearrange("p (s c) -> p s c", c=CHUNKS), AX.X,
                              ALU.max).then_inc(t_turn, 1)
            dve.tensor_reduce(win_lo[:], pad_far[:].rearrange("p (s c) -> p s c", c=CHUNKS), AX.X,
                              ALU.max).then_inc(t_turn, 1)
            dve.wait_ge(t_along, 16)
            then(dve.tensor_tensor(falls[:], along[:, 0:COLS], along[:, 1:], ALU.is_gt))
            then(dve.tensor_reduce(fall[:], falls[:], AX.X, ALU.add))
            dve.tensor_copy(g.rec[:, :, 0], dst_i[:])
            dve.wait_ge(t_vec, 16)
            then(dve.tensor_tensor(vec2[:], vec[:], vec[:], ALU.mult))
            dve.tensor_reduce(length[:], vec2[:], AX.X, ALU.add).then_inc(t_len, 1)
            dve.memset(g.codes[:], IDLE)
            dve.memset(hi[:], -1.0)
            dve.memset(count0[:], 0.0)
            then(dve.memset(lo[:], -FAR))
            dve.wait_ge(t_pe, 1)
            rest = SUPERS - 128
            dve.tensor_reduce(hi[:, 0:1], ps_t[:, 0, 0:128], AX.X, ALU.max)
            dve.tensor_reduce(hi[0:rest, 1:2], ps_t[0:rest, 0, 128:256], AX.X, ALU.max)
            dve.tensor_reduce(lo[:, 0:1], ps_t[:, 1, 0:128], AX.X, ALU.max)
            then(dve.tensor_reduce(lo[0:rest, 1:2], ps_t[0:rest, 1, 128:256], AX.X, ALU.max))
            then(dve.tensor_tensor(count[:], hi[:], lo[:], ALU.add))
            then(dve.tensor_scalar(count[:], count[:], 1.0, 0.0, ALU.add, ALU.max))
            then(dve.tensor_scalar(has[:], count[:], 0.0, None, ALU.is_gt))
            dve.tensor_copy(count0[:, 1:2], count[:, 0:1]).then_inc(t_turn, 1)
            then(dve.tensor_tensor(lo[:], lo[:], has[:], ALU.mult))
            dve.wait_ge(t_const, 10)
            then(dve.tensor_scalar(code_of[:], first[:], float(SPAN), -float(IDLE), ALU.mult, ALU.add))
            then(dve.tensor_tensor(code_of[:], code_of[:], lo[:], ALU.subtract))
            dve.wait_ge(t_pe, 2)
            then(dve.tensor_copy(after[:], ps_n[:, 0:2]))
            then(dve.tensor_tensor(first[:], after[:], count[:], ALU.subtract))
            then(dve.tensor_tensor(code_of[:], code_of[:], first[:], ALU.subtract))
            then(dve.tensor_copy(total[:], ps_n[0:1, 4:6]))
            then(dve.tensor_tensor(total1[:], total[:, 0:1], total[:, 1:2], ALU.add))
            dve.tensor_scalar(g.sorted[:], ps_n[:, 8:9], 1.5, -1.0, ALU.is_lt, ALU.mult)
            then(dve.tensor_scalar(g.unsorted[:], ps_n[:, 8:9], 1.5, -1.0, ALU.is_gt, ALU.mult))
            then(dve.tensor_tensor(apart[:], total1[:], g.unsorted[0:1, :], ALU.mult))
            then(dve.tensor_scalar(apart[:], apart[:], -1.0, 1.0, ALU.mult, ALU.max))
            then(dve.tensor_copy(g.apart_steps[:], apart[:]))
            then(dve.tensor_scalar(total1[:], total1[:], float(TURN - 1), None, ALU.add))
            then(dve.tensor_copy(total_i[:], total1[:]))
            then(dve.tensor_scalar(g.turns[:], total_i[:], TURN.bit_length() - 1, None, ALU.arith_shift_right))
            then(dve.tensor_scalar(step_blocks[:], total_i[:], 9, None, ALU.arith_shift_right))
            then(dve.tensor_copy(blocks_f[:], step_blocks[:]))
            then(dve.tensor_scalar(blocks_f[:], blocks_f[:], 1.0, float(TABLE // 512), ALU.add, ALU.min))
            dve.tensor_copy(step_blocks[:], blocks_f[:]).then_inc(t_blocks, 1)
            dve.wait_ge(t_blocks, 1)
            dve.memset(g.starts[:, 0:3], TURN)
            dve.wait_ge(t_first, 1)
            dve.tensor_scalar(g.starts[:, 3:], ps_n[0:1, P:P + SUPERS - 3], float(TURN), None, ALU.add)
            blocks = dve.value_load(step_blocks[0:1, 0:1], min_val=1, max_val=TABLE // 512)
            with dve.Fori(0, blocks) as b:
                steps = iota_step[:, bass.ds(b * 512, 512)]
                for c in range(2):
                    dve.tensor_scalar(from_first[:, c, :], steps, first[:, c:c + 1], None, ALU.is_ge).then_inc(t_from, 1)
                    dve.wait_ge(t_from, b * 2 + c + 1)
                    ins = dve.scalar_tensor_tensor(member[:, c, :], steps, after[:, c:c + 1], from_first[:, c, :],
                                                   ALU.is_lt, ALU.mult)
                ins.then_inc(t_mem, 1)
                dve.wait_ge(t_made, b + 1)
                dve.tensor_tensor(code_t[:], ps_c[:, 1, :], iota_step[0:1, bass.ds(b * 512, 512)],
                                  ALU.mult).then_inc(t_code, 1)
                dve.wait_ge(t_code, b * 3 + 1)
                dve.scalar_tensor_tensor(code_t[:], ps_c[:, 0, :], float(IDLE), code_t[:], ALU.add,
                                         ALU.add).then_inc(t_code, 1)
                dve.wait_ge(t_code, b * 3 + 2)
                dve.tensor_copy(g.code[:, bass.ds(b * 512, 512)], code_t[:]).then_inc(t_code, 1)
                dve.wait_ge(t_code, b * 3 + 3)
            dve.wait_ge(t_act, 1)
            then(dve.tensor_scalar(length[:], length[:], 1e-9, None, ALU.add))
            then(dve.reciprocal(inv_len[:], length[:]))
            for j in range(3):
                dve.scalar_tensor_tensor(g.rec[:, :, 1 + j], vec[:, :, j], float(np.sqrt(3.0)), inv_len[:],
                                         ALU.mult, ALU.mult)
            dve.wait_ge(t_w, 16 * 2 * (1 + NPATH))
            dve.tensor_scalar(g.w1[:], g.w1[:], 1.0 / float(np.sqrt(NB)), None, ALU.mult)
            out = 1.0 / (np.sqrt(NH) * AVG_NEIGH * np.sqrt(MUL))
            r2, r3 = 1.0 / np.sqrt(2.0), 1.0 / np.sqrt(3.0)
            for path, scale in enumerate((r2, r3 * r2, r3, r3 * r2, r3)):
                cols = g.w2[:, :, path * MUL:(path + 1) * MUL]
                dve.tensor_scalar(cols, cols, float(out * scale), None, ALU.mult)


def stage_messages(nc, g):
    with ExitStack() as ctx:
        def sb(name, shape, dt=F32):
            return ctx.enter_context(nc.sbuf_tensor(name, shape, dt))

        emb = sb("emb", [P, 2, SUPER // 2])
        hid = sb("hid", [2 * NH, 2, SUPER // 2])
        idx = sb("idx", [P, TURN, CHUNKS], I32)
        feat = sb("feat", [P, TURN, CHUNKS, 2, 4, MUL])
        rec_a = sb("rec_a", [P, 2, CHUNKS, 4])
        vsh = sb("vsh", [P, TURN, CHUNKS, 3, 4, MUL])
        hot = sb("hot", [P, 2, CHUNKS, P])
        msg = sb("msg", [P, CHUNKS, 3, 4, MUL])
        ps_h = ctx.enter_context(nc.psum_tensor("ps_h", [2 * NH, 2, 512], F32))
        ps_w = ctx.enter_context(nc.psum_tensor("ps_w", [P, CHUNKS, 512], F32))
        ps_a = ctx.enter_context(nc.psum_tensor("ps_a", [P, 2, 512], F32))
        m_zero = ctx.enter_context(nc.semaphore("m_zero"))
        m_emb = [ctx.enter_context(nc.semaphore(f"m_emb{u}")) for u in range(2)]
        m_snd = [ctx.enter_context(nc.semaphore(f"m_snd{u}")) for u in range(TURN)]
        m_emb_used = ctx.enter_context(nc.semaphore("m_emb_used"))
        m_hps = ctx.enter_context(nc.semaphore("m_hps"))
        m_hid = ctx.enter_context(nc.semaphore("m_hid"))
        m_w = ctx.enter_context(nc.semaphore("m_w"))
        m_idx = ctx.enter_context(nc.semaphore("m_idx"))
        m_ask = ctx.enter_context(nc.semaphore("m_ask"))
        m_reca = ctx.enter_context(nc.semaphore("m_reca"))
        m_vsh = ctx.enter_context(nc.semaphore("m_vsh"))
        m_cross = ctx.enter_context(nc.semaphore("m_cross"))
        m_dot = ctx.enter_context(nc.semaphore("m_dot"))
        m_prod = ctx.enter_context(nc.semaphore("m_prod"))
        m_msg = ctx.enter_context(nc.semaphore("m_msg"))
        m_used = ctx.enter_context(nc.semaphore("m_used"))
        m_clear = ctx.enter_context(nc.semaphore("m_clear"))
        m_acc = ctx.enter_context(nc.semaphore("m_acc"))
        block = ctx.enter_context(nc.Block())

        @block.sync
        def _(sp):
            sp.sem_inc(m_emb_used, 2)
            turns = sp.value_load(g.turns[0:1, 0:1], min_val=0, max_val=MAX_TURNS)
            sp.wait_ge(m_zero, 1)

            def load(i, u):
                sc, _w = step_of(nc, sp, g.code, i)
                sp.wait_ge(m_emb_used, i + 1)
                sp.dma_start(emb[0:2 * NB, u % 2, :],
                             g.emb_t[:, bass.ds(sc * (SUPER // 2), SUPER // 2)]).then_inc(m_emb[u % 2], 16)

            load(0, 0)
            load(1, 1)
            with sp.Fori(0, turns) as t:
                for u in range(TURN):
                    load(t * TURN + u + 2, u + 2)

        @block.gpsimd
        def _(pool):
            turns = pool.value_load(g.turns[0:1, 0:1], min_val=0, max_val=MAX_TURNS)

            def gather(i, u):
                sc, _w = step_of(nc, pool, g.code, i)
                pool.wait_ge(m_prod, i * 2 + 2)
                pool.tensor_copy(idx[:, u, :], g.src_i[:, bass.ds(sc * CHUNKS, CHUNKS)]).then_inc(m_idx, 1)
                pool.wait_ge(m_idx, i + 1)
                pool.sem_inc(m_ask, 1)
                for c in range(CHUNKS):
                    pool.indirect_dma_start(
                        out=feat[:, u, c, 0, :, :].rearrange("p a b -> p (a b)"), out_offset=None, in_=g.x_rows,
                        in_offset=bass.IndirectOffsetOnAxis(ap=idx[:, u, c:c + 1], axis=0),
                    ).then_inc(m_snd[u], 16)

            def cross(i, u):
                pool.wait_ge(m_vsh, i + 1)
                pool.sem_inc(m_ask, 1)
                v = vsh[:, u % TURN]
                for k in range(3):
                    a, b = (k + 1) % 3, (k + 2) % 3
                    ins = pool.tensor_tensor(feat[:, u % TURN, :, 1, 1 + k, :], v[:, :, b, 1 + a, :], v[:, :, a, 1 + b, :],
                                             ALU.subtract)
                ins.then_inc(m_cross, 1)

            for u in range(TURN - 1):
                gather(u, u)
            cross(0, 0)
            with pool.Fori(0, turns) as t:
                for u in range(TURN):
                    gather(t * TURN + u + TURN - 1, (u + TURN - 1) % TURN)
                    cross(t * TURN + u + 1, u + 1)

        @block.scalar
        def _(act):
            turns = act.value_load(g.turns[0:1, 0:1], min_val=0, max_val=MAX_TURNS)

            def prepare(i, u, landed):
                sc, _w = step_of(nc, act, g.code, i)
                act.activation(rec_a[:, u % 2, :, :], g.rec[:, bass.ds(sc * CHUNKS, CHUNKS), :],
                               ACT.Copy).then_inc(m_reca, 1)
                act.wait_ge(m_hps, i + 1)
                act.activation(hid[:, u % 2, :], ps_h[:, u % 2, 0:SUPER // 2], ACT.Silu).then_inc(m_hid, 1)
                act.wait_ge(m_reca, i + 1)
                act.wait_ge(m_snd[u % TURN], landed)
                act.wait_ge(m_prod, i * 2 + 2)
                for c in range(CHUNKS):
                    for j in range(3):
                        ins = act.activation(vsh[:, u % TURN, c, j, :, :], feat[:, u % TURN, c, 0, :, :], ACT.Copy,
                                             scale=rec_a[:, u % 2, c, 1 + j:2 + j])
                ins.then_inc(m_vsh, 1)

            prepare(0, 0, 16 * CHUNKS)
            with act.Fori(0, turns) as t:
                for u in range(1, TURN + 1):
                    prepare(t * TURN + u, u, (t + 1 + u // TURN) * (16 * CHUNKS))

        @block.tensor
        def _(pe):
            turns = pe.value_load(g.turns[0:1, 0:1], min_val=0, max_val=MAX_TURNS)

            def hidden(i, u, landed):
                pe.wait_ge(m_emb[u % 2], landed)
                pe.matmul(ps_h[:, u % 2, 0:SUPER // 2], g.w1[:], emb[:, u % 2, :], start=True, stop=True,
                          skip_group_check=True).then_inc(m_hps, 1)
                pe.wait_ge(m_hps, i + 1)
                pe.sem_inc(m_emb_used, 1)

            def weights(i, u, c):
                half, at = c // 2, (c % 2) * P
                pe.matmul(ps_w[:, c, 0:NPATH * MUL], hid[:, u % 2, at:at + P], g.w2[:, half, :], start=True,
                          stop=True).then_inc(m_w, 1)

            hidden(0, 0, 16)
            hidden(1, 1, 16)
            pe.wait_ge(m_hid, 1)
            for c in range(CHUNKS):
                weights(0, 0, c)
            pe.wait_ge(m_clear, 1)
            with pe.Fori(0, turns) as t:
                for u in range(TURN):
                    i = t * TURN + u
                    hidden(i + 2, u, t * (16 * TURN // 2) + 16 * (u // 2 + 2))
                    pe.wait_ge(m_acc, i + 1)
                    for c in range(CHUNKS):
                        if c % 2 == 0:
                            pe.wait_ge(m_msg, i * 2 + c // 2 + 1)
                        out = ps_a[:, u % 2, :]
                        rows = msg[:, c].rearrange("p a b c -> p a (b c)")
                        pe.matmul(out[:, 0:D], hot[:, u % 2, c, :], rows[:, 0, :], start=(c == 0), stop=False,
                                  skip_group_check=True)
                        pe.matmul(out[:, MUL:D], hot[:, u % 2, c, :], rows[:, 2, MUL:D], start=False,
                                  stop=(c == CHUNKS - 1), skip_group_check=True).then_inc(m_used, 1)
                        if c == 0:
                            pe.wait_ge(m_hid, i + 2)
                        weights(i + 1, u + 1, c)

        @block.vector
        def _(dve):
            dve.sem_inc(m_prod, 2 * TURN)
            dve.sem_inc(m_used, CHUNKS)
            dve.sem_inc(m_acc, 1)
            dve.memset(emb[:], 0.0).then_inc(m_zero, 1)
            dve.memset(ps_a[:], 0.0).then_inc(m_clear, 1)
            dve.wait_ge(m_clear, 1)
            turns = dve.value_load(g.turns[0:1, 0:1], min_val=0, max_val=MAX_TURNS)

            def add_sums(i, u, w):
                dve.wait_ge(m_used, i * CHUNKS + CHUNKS)
                dve.wait_ge(m_acc, i + 1)
                dve.tensor_tensor(g.acc[:, bass.ds(w, 1), 0:D], g.acc[:, bass.ds(w, 1), 0:D],
                                  ps_a[:, (u + 1) % 2:(u + 1) % 2 + 1, 0:D], ALU.add).then_inc(m_acc, 1)

            def sum_paths(i, pair):
                m = msg[:, pair * 2:pair * 2 + 2]
                dve.wait_ge(m_prod, i * 2 + pair + 1 + 2 * TURN)
                dve.tensor_tensor(m[:, :, 0], m[:, :, 0], m[:, :, 1], ALU.add).then_inc(m_msg, 1)

            sc, w = step_of(nc, dve, g.code, 0)
            one_hots(dve, g, hot[:, 0], sc, w)
            with dve.Fori(0, turns) as t:
                for u in range(TURN):
                    i = t * TURN + u
                    dve.wait_ge(m_vsh, i + 1)
                    v, f = vsh[:, u], feat[:, u]
                    dot = f[:, :, 1, 0, :]
                    dve.tensor_tensor(dot, v[:, :, 0, 1, :], v[:, :, 1, 2, :], ALU.add).then_inc(m_dot, 1)
                    if u == 0:
                        _sc, w_before = step_of(nc, dve, g.code_before, i)
                    else:
                        w_before = w_now
                    dve.wait_ge(m_dot, i * 2 + 1)
                    dve.tensor_tensor(dot, dot, v[:, :, 2, 3, :], ALU.add).then_inc(m_dot, 1)
                    for pair in range(2):
                        two = slice(pair * 2, pair * 2 + 2)
                        dve.wait_ge(m_used, i * CHUNKS + pair * 2 + 2)
                        dve.wait_ge(m_w, i * CHUNKS + pair * 2 + 2)
                        wt = ps_w[:, two, 0:NPATH * MUL].rearrange("p c (a b) -> p c a b", a=NPATH)
                        dve.tensor_tensor(msg[:, two, 2, 1:4, :], wt[:, :, 4:5, :].broadcast_to([P, 2, 3, MUL]),
                                          v[:, two, :, 0, :], ALU.mult)
                        if pair == 0:
                            dve.wait_ge(m_dot, i * 2 + 2)
                        dve.tensor_tensor(msg[:, two, 0:2, 0, :], wt[:, :, 0:2, :], f[:, two, :, 0, :], ALU.mult)
                        if pair == 0:
                            dve.wait_ge(m_cross, i + 1)
                        for c in range(2):
                            by = wt[:, c, 2:4, :].rearrange("p (a o) b -> p a o b", o=1)
                            ins = dve.tensor_tensor(msg[:, pair * 2 + c, 0:2, 1:4, :],
                                                    by.broadcast_to([P, 2, 3, MUL]), f[:, pair * 2 + c, :, 1:4, :],
                                                    ALU.mult)
                        ins.then_inc(m_prod, 1)
                        if pair == 0:
                            add_sums(i, u, w_before)
                            if u == 0:
                                _sc, w_now = step_of(nc, dve, g.code, i)
                            else:
                                w_now = w
                        else:
                            sc, w = step_of(nc, dve, g.code, i + 1)
                        sum_paths(i, pair)
                    one_hots(dve, g, hot[:, (u + 1) % 2], sc, w)
            _sc, w_before = step_of(nc, dve, g.code_before, turns * TURN)
            add_sums(turns * TURN, TURN, w_before)


def stage_project(nc, g):
    with ExitStack() as ctx:
        def sb(name, shape, dt=F32):
            return ctx.enter_context(nc.sbuf_tensor(name, shape, dt))

        w_qkv = sb("w_qkv", [P, 2, 3 * D])
        b_row = sb("b_row", [P, 3 * D])
        gain = sb("gain", [P, 2])
        shift = sb("shift", [P, 2])
        xw = sb("xw", [P, 2, D])
        agg = sb("agg", [P, D])
        agg_t = sb("agg_t", [P, 2, P])
        y = sb("y", [P, D])
        stats = sb("stats", [P, 2, 6])
        mv = sb("mv", [P, 2, 2])
        dev = sb("dev", [P, 2])
        rstd = sb("rstd", [P, 2])
        eps = sb("eps", [P, 1])
        x1 = sb("x1_w", [P, D])
        xn = sb("xn", [P, D])
        xn_t = sb("xn_t", [P, 2, P])
        q = sb("q", [P, D])
        left = sb("left", [P, D])
        kv = sb("kv", [P, 2, 2 * D])
        spare = sb("spare", [P, 1])
        ps_a = ctx.enter_context(nc.psum_tensor("ps_a2", [P, 512], F32))
        ps_u = ctx.enter_context(nc.psum_tensor("ps_u", [P, 512], F32))
        ps_n = ctx.enter_context(nc.psum_tensor("ps_n2", [P, 512], F32))
        ps_q = ctx.enter_context(nc.psum_tensor("ps_q", [P, 512], F32))
        ps_kv = ctx.enter_context(nc.psum_tensor("ps_kv", [P, 512], F32))
        p_x = [ctx.enter_context(nc.semaphore(f"p_x{u}")) for u in range(2)]
        p_st = [ctx.enter_context(nc.semaphore(f"p_st{u}")) for u in range(2)]
        p_w = ctx.enter_context(nc.semaphore("p_w"))
        p_zero = ctx.enter_context(nc.semaphore("p_zero"))
        p_agg = ctx.enter_context(nc.semaphore("p_agg"))
        p_turn = ctx.enter_context(nc.semaphore("p_turn"))
        p_aggt = ctx.enter_context(nc.semaphore("p_aggt"))
        p_upd = ctx.enter_context(nc.semaphore("p_upd"))
        p_xn = ctx.enter_context(nc.semaphore("p_xn"))
        p_turn2 = ctx.enter_context(nc.semaphore("p_turn2"))
        p_xnt = ctx.enter_context(nc.semaphore("p_xnt"))
        p_qkv = ctx.enter_context(nc.semaphore("p_qkv"))
        p_q = ctx.enter_context(nc.semaphore("p_q"))
        p_kv = ctx.enter_context(nc.semaphore("p_kv"))
        p_stat = ctx.enter_context(nc.semaphore("p_stat"))
        p_dev = ctx.enter_context(nc.semaphore("p_dev"))
        p_eps = ctx.enter_context(nc.semaphore("p_eps"))
        p_clear = ctx.enter_context(nc.semaphore("p_clear"))
        p_norm = ctx.enter_context(nc.semaphore("p_norm"))
        p_split = ctx.enter_context(nc.semaphore("p_split"))
        block = ctx.enter_context(nc.Block())

        @block.sync
        def _(sp):
            for u in range(2):
                sp.dma_start(xw[:, u, :], g.x_rows[u * P:(u + 1) * P, :]).then_inc(p_x[u], 16)
            sp.dma_start(gain[:], g.ln1_g).then_inc(p_w, 16)
            sp.dma_start(shift[:], g.ln1_b).then_inc(p_w, 16)
            for n, w in enumerate(g.w_qkv):
                sp.dma_start(w_qkv[:, :, n * D:(n + 1) * D], w.rearrange("(k p) n -> p k n", p=P)).then_inc(p_w, 16)
            sp.wait_ge(p_zero, 1)
            for n, b in enumerate(g.b_qkv):
                sp.dma_start(b_row[0:1, n * D:(n + 1) * D], b.rearrange("(a d) -> a d", a=1)).then_inc(p_w, 16)
            with sp.Fori(0, WINDOWS // 2) as t:
                for u in range(2):
                    w = t * 2 + u
                    sp.wait_ge(p_xn, w + 1)
                    sp.dma_start(xw[:, u, :], g.x_rows[bass.ds(w * P + 2 * P, P), :]).then_inc(p_x[u], 16)
                    sp.wait_ge(p_kv, w + 2)
                    rows = bass.ds(w * P, P)
                    sp.dma_start(g.k_rows[rows, :], kv[:, u, 0:D]).then_inc(p_st[u], 16)
                    sp.dma_start(g.v_rows[rows, :], kv[:, u, D:2 * D]).then_inc(p_st[u], 16)
            for u in range(2):
                sp.wait_ge(p_x[u], 16 * (WINDOWS // 2 + 1))
                sp.wait_ge(p_st[u], 32 * (WINDOWS // 2 + 1))

        @block.scalar
        def _(act):
            act.sem_inc(p_kv, 1)
            act.sem_inc(p_turn, 1)
            for u in range(2):
                act.sem_inc(p_st[u], 32)

            def set_out(w):
                act.wait_ge(p_turn, w + 1)
                act.activation(agg[:], g.acc[:, bass.ds(w, 1), 0:D].rearrange("p a d -> p (a d)"),
                               ACT.Copy).then_inc(p_agg, 1)

            def sums_out(w):
                act.wait_ge(p_turn, w + 2)
                act.activation(agg_t[:].rearrange("p a b -> p (a b)"), ps_a[:, 0:D], ACT.Copy).then_inc(p_aggt, 1)

            def deviations(w):
                for n in range(2):
                    act.wait_ge(p_stat, w * 2 + n + 1)
                    act.activation(dev[:, n:n + 1], mv[:, n, 1:2], ACT.Sqrt, bias=eps[:]).then_inc(p_dev, 1)

            act.wait_ge(p_eps, 1)
            set_out(0)
            sums_out(0)
            deviations(0)
            act.wait_ge(p_w, 16 * 8)
            with act.Fori(0, WINDOWS // 2) as t:
                for u in range(2):
                    w = t * 2 + u
                    set_out(w + 1)
                    act.wait_ge(p_turn2, w + 1)
                    for k in range(2):
                        ins = act.activation(xn_t[:, k, :], ps_n[:, k * P:(k + 1) * P], ACT.Identity,
                                             bias=shift[:, k:k + 1], scale=gain[:, k:k + 1])
                    ins.then_inc(p_xnt, 1)
                    sums_out(w + 1)
                    deviations(w + 1)
                    act.wait_ge(p_qkv, w + 1)
                    act.wait_ge(p_st[u], t * 32 + 32)
                    act.activation(kv[:, u, :], ps_kv[:], ACT.Copy).then_inc(p_kv, 1)

        @block.tensor
        def _(pe):
            def turn_sums(w):
                pe.wait_ge(p_agg, w + 1)
                for k in range(2):
                    mm = pe.transpose(ps_a[:, k * P:(k + 1) * P], agg[:, k * P:(k + 1) * P], g.ident[:])
                mm.then_inc(p_turn, 1)

            def update(w):
                pe.wait_ge(p_aggt, w + 1)
                for k in range(2):
                    mm = pe.matmul(ps_u[:, k * P:(k + 1) * P], agg_t[:, k, :], g.lin[:, k, :], start=True,
                                   stop=True, skip_group_check=True)
                mm.then_inc(p_upd, 1)

            turn_sums(0)
            update(0)
            pe.wait_ge(p_w, 16 * 8)
            with pe.Fori(0, WINDOWS) as w:
                pe.wait_ge(p_xn, w + 1)
                for k in range(2):
                    mm = pe.transpose(ps_n[:, k * P:(k + 1) * P], xn[:, k * P:(k + 1) * P], g.ident[:])
                mm.then_inc(p_turn2, 1)
                turn_sums(w + 1)
                update(w + 1)
                pe.wait_ge(p_q, w + 1)
                pe.matmul(ps_q[:, 0:D], g.ones[:], b_row[:, 0:D], start=True, stop=False)
                pe.wait_ge(p_kv, w + 1)
                pe.matmul(ps_kv[:], g.ones[:], b_row[:, D:3 * D], start=True, stop=False)
                pe.wait_ge(p_xnt, w + 1)
                for k in range(2):
                    pe.matmul(ps_q[:, 0:D], xn_t[:, k, :], w_qkv[:, k, 0:D], start=False, stop=(k == 1))
                for k in range(2):
                    mm = pe.matmul(ps_kv[:], xn_t[:, k, :], w_qkv[:, k, D:3 * D], start=False, stop=(k == 1))
                mm.then_inc(p_qkv, 1)

        @block.vector
        def _(dve):
            dve.sem_inc(p_q, 1)
            dve.memset(eps[:], EPS).then_inc(p_eps, 1)
            dve.memset(b_row[:], 0.0).then_inc(p_zero, 1)
            dve.memset(g.q3[:, IDLE, :, :], 0.0)
            NORMS, PARTS = 6, 3

            def norms(w, u, landed):
                link = [w * NORMS]

                def then(ins):
                    link[0] = link[0] + 1
                    ins.then_inc(p_norm, 1)
                    dve.wait_ge(p_norm, link[0])

                dve.wait_ge(p_upd, w + 1)
                dve.wait_ge(p_x[u], landed)
                then(dve.scalar_tensor_tensor(y[:], xw[:, u, :], 2.0, ps_u[:, 0:D], ALU.mult, ALU.add))
                for n, (of, to) in enumerate(((y, x1), (x1, xn))):
                    then(dve.bn_stats(stats[:, n, :], of[:]))
                    dve.memset(spare[:], 0.0)
                    dve.bn_aggr(mv[:, n, :], stats[:, n, :]).then_inc(p_stat, 1)
                    dve.wait_ge(p_dev, w * 2 + n + 1)
                    then(dve.reciprocal(rstd[:, n:n + 1], dev[:, n:n + 1]))
                    ins = dve.tensor_scalar(to[:], of[:], mv[:, n, 0:1], rstd[:, n:n + 1], ALU.subtract, ALU.mult)
                    if n == 0:
                        then(ins)
                ins.then_inc(p_xn, 1)
                dve.tensor_copy(g.x1[:, bass.ds(w, 1), :].rearrange("p a d -> p (a d)"), x1[:])

            def parts(w):
                q3 = [g.q3[:, bass.ds(w, 1), n, :].rearrange("p a d -> p (a d)") for n in range(3)]
                dve.wait_ge(p_qkv, w + 1)
                dve.tensor_scalar(q[:], ps_q[:, 0:D], float(DH) ** -0.5, None, ALU.mult).then_inc(p_q, 1)
                dve.wait_ge(p_q, w + 2)
                dve.tensor_copy(q3[0], q[:]).then_inc(p_split, 1)
                dve.wait_ge(p_split, w * PARTS + 1)
                dve.tensor_tensor(left[:], q[:], q3[0], ALU.subtract).then_inc(p_split, 1)
                dve.wait_ge(p_split, w * PARTS + 2)
                dve.tensor_copy(q3[1], left[:]).then_inc(p_split, 1)
                dve.wait_ge(p_split, w * PARTS + 3)
                dve.tensor_tensor(q3[2], left[:], q3[1], ALU.subtract)

            norms(0, 0, 16)
            with dve.Fori(0, WINDOWS // 2) as t:
                for u in range(2):
                    w = t * 2 + u
                    norms(w + 1, (u + 1) % 2, (t + u) * 16 + 16)
                    parts(w)

        @block.gpsimd
        def _(pool):
            pool.wait_ge(p_agg, WINDOWS + 1)
            pool.memset(g.acc[:], 0.0).then_inc(p_clear, 1)


def stage_scores(nc, g):
    with ExitStack() as ctx:
        def sb(name, shape, dt=F32):
            return ctx.enter_context(nc.sbuf_tensor(name, shape, dt))

        ef = sb("ef", [ED + 1, 2, SUPER])
        w_e = sb("w_e", [ED + 1, DH])
        idx = sb("idx3", [P, TURN, CHUNKS], I32)
        key = sb("key", [P, TURN, CHUNKS, HEADS, DH])
        hot = sb("hot3", [P, 2, CHUNKS, P], BF16)
        hot_t = sb("hot_t", [P, 2, SUPER], BF16)
        away = sb("away", [P, CHUNKS, P])
        rec_a = sb("rec_a3", [P, 2, CHUNKS])
        k_edge = sb("k_edge", [P, 2, CHUNKS, HEADS, DH])
        ident_b = sb("ident_b", [P, P], BF16)
        part = sb("part", [P, 2, CHUNKS, HEADS])
        ps_t = ctx.enter_context(nc.psum_tensor("ps_t3", [P, 2, 2, SUPER], BF16))
        ps_e = ctx.enter_context(nc.psum_tensor("ps_e", [P, 2, 512], F32))
        ps_x = ctx.enter_context(nc.psum_tensor("ps_x", [P, 2, CHUNKS, D], F32))
        c_w = ctx.enter_context(nc.semaphore("c_w"))
        c_ef0 = ctx.enter_context(nc.semaphore("c_ef0"))
        c_ef1 = ctx.enter_context(nc.semaphore("c_ef1"))
        c_land = ctx.enter_context(nc.semaphore("c_land"))
        c_rec = ctx.enter_context(nc.semaphore("c_rec"))
        c_away = ctx.enter_context(nc.semaphore("c_away"))
        c_idx = ctx.enter_context(nc.semaphore("c_idx"))
        c_ask = ctx.enter_context(nc.semaphore("c_ask"))
        key_landed = [ctx.enter_context(nc.semaphore(f"c_key{u}")) for u in range(TURN)]
        c_hot = ctx.enter_context(nc.semaphore("c_hot"))
        c_turn = ctx.enter_context(nc.semaphore("c_turn"))
        c_hott = ctx.enter_context(nc.semaphore("c_hott"))
        c_eps = ctx.enter_context(nc.semaphore("c_eps"))
        c_qx = ctx.enter_context(nc.semaphore("c_qx"))
        c_sum = ctx.enter_context(nc.semaphore("c_sum"))
        c_mul = ctx.enter_context(nc.semaphore("c_mul"))
        c_red = ctx.enter_context(nc.semaphore("c_red"))
        c_add = ctx.enter_context(nc.semaphore("c_add"))
        c_id = ctx.enter_context(nc.semaphore("c_id"))
        c_zero = ctx.enter_context(nc.semaphore("c_zero"))
        ef_landed = (c_ef0, c_ef1)
        block = ctx.enter_context(nc.Block())

        @block.sync
        def _(sp):
            sp.dma_start(w_e[0:ED, :], g.We).then_inc(c_w, 16)
            sp.dma_start(w_e[ED:ED + 1, :], g.be.rearrange("(a d) -> a d", a=1)).then_inc(c_w, 16)
            sp.sem_inc(c_eps, 2)
            turns = sp.value_load(g.turns[0:1, 0:1], min_val=0, max_val=MAX_TURNS)
            with sp.Fori(0, turns) as t:
                for u in range(TURN):
                    i = t * TURN + u
                    sc, _w = step_of(nc, sp, g.code, i)
                    sp.wait_ge(c_eps, i + 1)
                    sp.dma_start(ef[0:ED, u % 2, :], g.ef_t[:, bass.ds(sc * SUPER, SUPER)]).then_inc(ef_landed[u % 2], 16)

        @block.gpsimd
        def _(pool):
            pool.memset(g.score[:], 0.0).then_inc(c_zero, 1)
            pool.sem_inc(c_sum, TURN)

            def gather(s, u):
                pool.tensor_copy(idx[:, u, :], g.src_i[:, bass.ds(s * CHUNKS, CHUNKS)]).then_inc(c_idx, 1)
                pool.wait_ge(c_idx, s + 1)
                pool.sem_inc(c_ask, 1)
                for c in range(CHUNKS):
                    pool.indirect_dma_start(
                        out=key[:, u, c, :, :].rearrange("p a b -> p (a b)"), out_offset=None, in_=g.k_rows,
                        in_offset=bass.IndirectOffsetOnAxis(ap=idx[:, u, c:c + 1], axis=0),
                    ).then_inc(key_landed[u], 16)

            def landed(u, count):
                pool.wait_ge(key_landed[u], count)
                pool.sem_inc(c_land, 1)

            for u in range(TURN):
                gather(u, u)
                if u > 0:
                    landed(u - 1, 16 * CHUNKS)
            with pool.Fori(1, SUPERS // TURN) as t:
                for u in range(TURN):
                    steps = pool.value_load(g.starts[0:1, bass.ds(t * TURN + u, 1)], min_val=TURN,
                                            max_val=TABLE + TURN)
                    pool.wait_ge(c_sum, steps)
                    pool.sem_inc(c_ask, 1)
                    gather(t * TURN + u, u)
                    landed((u - 1) % TURN, t * (16 * CHUNKS) if u == 0 else (t + 1) * (16 * CHUNKS))
            landed(TURN - 1, 16 * CHUNKS * (SUPERS // TURN))

        @block.scalar
        def _(act):
            turns = act.value_load(g.turns[0:1, 0:1], min_val=0, max_val=MAX_TURNS)
            act.sem_inc(c_mul, 2)

            def make_hots(i, u):
                sc, w = step_of(nc, act, g.code, i)
                act.activation(rec_a[:, u % 2, :], g.rec[:, bass.ds(sc * CHUNKS, CHUNKS), 0],
                               ACT.Copy).then_inc(c_rec, 1)
                act.wait_ge(c_rec, i + 1)
                for c in range(CHUNKS):
                    ins = act.activation(away[:, c, :], g.iota_node[:, bass.ds(w * P, P)], ACT.Abs,
                                         bias=rec_a[:, u % 2, c:c + 1], scale=-1.0)
                ins.then_inc(c_away, 1)
                act.wait_ge(c_away, i + 1)
                act.activation(hot[:, u % 2], away[:], ACT.Relu, bias=g.ones[:, 0:1], scale=-1.0).then_inc(c_hot, 1)

            make_hots(0, 0)
            with act.Fori(0, turns) as t:
                for u in range(TURN):
                    i = t * TURN + u
                    make_hots(i + 1, u + 1)
                    act.wait_ge(c_turn, i + 1)
                    act.wait_ge(c_mul, i + 1)
                    act.activation(hot_t[:, u % 2, :], ps_t[:, u % 2, 0, :], ACT.Copy).then_inc(c_hott, 1)

        @block.tensor
        def _(pe):
            pe.wait_ge(c_w, 32)
            pe.wait_ge(c_id, 2)
            turns = pe.value_load(g.turns[0:1, 0:1], min_val=0, max_val=MAX_TURNS)
            with pe.Fori(0, turns) as t:
                for u in range(TURN):
                    i = t * TURN + u
                    _sc, w = step_of(nc, pe, g.code, i)
                    pe.wait_ge(c_hot, i + 1)
                    for c in range(CHUNKS):
                        mm = pe.transpose(ps_t[:, u % 2, 0, c * P:(c + 1) * P], hot[:, u % 2, c, :], ident_b[:])
                    mm.then_inc(c_turn, 1)
                    pe.wait_ge(ef_landed[u % 2], t * (16 * TURN // 2) + 16 * (u // 2 + 1))
                    pe.wait_ge(c_mul, i + 1)
                    for c in range(CHUNKS):
                        mm = pe.matmul(ps_e[:, u % 2, c * DH:(c + 1) * DH], ef[:, u % 2, c * P:(c + 1) * P], w_e[:],
                                       start=True, stop=True, skip_group_check=True)
                    mm.then_inc(c_eps, 1)
                    pe.wait_ge(c_hott, i + 1)
                    for c in range(CHUNKS):
                        for n in range(3):
                            mm = pe.matmul(ps_x[:, u % 2, c, :], hot_t[:, u % 2, c * P:(c + 1) * P],
                                           g.q3[:, bass.ds(w, 1), n, :].rearrange("p a d -> p (a d)"),
                                           start=(n == 0), stop=(n == 2), skip_group_check=True)
                    mm.then_inc(c_qx, 1)

        @block.vector
        def _(dve):
            dve.sem_inc(c_add, 1)
            dve.sem_inc(c_red, 1)
            dve.memset(ef[ED:ED + 1], 1.0).then_inc(c_id, 1)
            dve.tensor_copy(ident_b[:], g.ident[:]).then_inc(c_id, 1)
            dve.memset(part[:], 0.0).then_inc(c_add, 1)
            dve.wait_ge(c_zero, 1)
            turns = dve.value_load(g.turns[0:1, 0:1], min_val=0, max_val=MAX_TURNS)

            def add_part(i, u, sc):
                mine = g.score[:, bass.ds(sc * CHUNKS, CHUNKS), :]
                dve.wait_ge(c_add, i + 2)
                dve.wait_ge(c_red, i + 1)
                dve.tensor_tensor(mine, mine, part[:, (u + 1) % 2], ALU.add).then_inc(c_add, 1)

            with dve.Fori(0, turns) as t:
                for u in range(TURN):
                    i = t * TURN + u
                    if u == 0:
                        sc, _w = step_of(nc, dve, g.code, i)
                    dve.wait_ge(c_land, sc + 1)
                    dve.wait_ge(c_eps, i + 3)
                    slot = nc.s_assert_within(dve.snap(sc % TURN), 0, TURN - 1,
                                              skip_runtime_bounds_check_because="a remainder of TURN")
                    rows = key[:, bass.ds(slot, 1)].rearrange("p a c h d -> p (a c) h d")
                    k = k_edge[:, u % 2]
                    edge_part = ps_e[:, u % 2, 0:CHUNKS * DH].rearrange("p (c h d) -> p c h d", c=CHUNKS, h=1)
                    dve.tensor_tensor(k, rows, edge_part.broadcast_to([P, CHUNKS, HEADS, DH]),
                                      ALU.add).then_inc(c_sum, 1)
                    if u == 0:
                        sc_before, _w = step_of(nc, dve, g.code_before, i)
                    next_sc, _w = step_of(nc, dve, g.code, i + 1)
                    add_part(i, u, sc_before)
                    sc_before, sc = sc, next_sc
                    dve.wait_ge(c_sum, i + 1 + TURN)
                    dve.wait_ge(c_qx, i + 1)
                    flat = k.rearrange("p c h d -> p (c h d)")
                    dve.tensor_tensor(flat, flat, ps_x[:, u % 2].rearrange("p c d -> p (c d)"),
                                      ALU.mult).then_inc(c_mul, 1)
                    dve.wait_ge(c_mul, i + 3)
                    dve.tensor_reduce(part[:, u % 2], k, AX.X, ALU.add).then_inc(c_red, 1)
            sc_before, _w = step_of(nc, dve, g.code_before, turns * TURN)
            add_part(turns * TURN, TURN, sc_before)


def stage_apart(nc, g):
    with ExitStack() as ctx:
        def sb(name, shape, dt=F32):
            return ctx.enter_context(nc.sbuf_tensor(name, shape, dt))

        best = sb("best", [P, WINDOWS + 1, HEADS])
        hot = sb("hot4", [P, CHUNKS, P])
        hot_t = sb("hot_t4", [P, CHUNKS, P])
        outside = sb("outside", [P, CHUNKS, P])
        s = sb("s4", [P, CHUNKS, HEADS])
        mine = sb("mine", [P, HEADS, P])
        most = sb("most", [P, HEADS, P])
        step_best = sb("step_best", [P, HEADS])
        ps_m = ctx.enter_context(nc.psum_tensor("ps_m", [P, HEADS, P], F32))
        ps_h = ctx.enter_context(nc.psum_tensor("ps_h4", [P, CHUNKS, P], F32))
        ps_b = ctx.enter_context(nc.psum_tensor("ps_b", [P, CHUNKS, HEADS], F32))
        a_link = ctx.enter_context(nc.semaphore("a_link"))
        a_link2 = ctx.enter_context(nc.semaphore("a_link2"))
        a_dst = ctx.enter_context(nc.semaphore("a_dst"))
        a_start = ctx.enter_context(nc.semaphore("a_start"))
        a_most = ctx.enter_context(nc.semaphore("a_most"))
        a_turn = ctx.enter_context(nc.semaphore("a_turn"))
        a_hot = ctx.enter_context(nc.semaphore("a_hot"))
        a_hott = ctx.enter_context(nc.semaphore("a_hott"))
        a_out = ctx.enter_context(nc.semaphore("a_out"))
        a_max = ctx.enter_context(nc.semaphore("a_max"))
        block = ctx.enter_context(nc.Block())

        @block.sync
        def _(sp):
            sp.dma_start(g.dst_r[:], bass.AP(g.dst_row.tensor, 0, [[BLOCK_EDGES, BLOCKS], [0, HEADS],
                                                                    [1, BLOCK_EDGES + 2]])).then_inc(a_dst, 16)
            sp.wait_ge(a_dst, 16)

        @block.tensor
        def _(pe):
            steps = pe.value_load(g.apart_steps[0:1, 0:1], min_val=1, max_val=TABLE)
            with pe.Fori(0, steps) as i:
                pe.wait_ge(a_most, i + 1)
                for h in range(HEADS):
                    mm = pe.transpose(ps_m[:, h, :], most[:, h, :], g.ident[:])
                mm.then_inc(a_turn, 1)
            with pe.Fori(0, steps) as i:
                _sc, w = step_of(nc, pe, g.code, i)
                pe.wait_ge(a_hot, i + 1)
                for c in range(CHUNKS):
                    mm = pe.transpose(ps_h[:, c, :], hot[:, c, :], g.ident[:])
                mm.then_inc(a_hott, 1)
                pe.wait_ge(a_out, i + 1)
                for c in range(CHUNKS):
                    mm = pe.matmul(ps_b[:, c, :], hot_t[:, c, :],
                                   best[:, bass.ds(w, 1), :].rearrange("p a h -> p (a h)"), start=True, stop=True,
                                   skip_group_check=True)
                mm.then_inc(a_max, 1)

        @block.vector
        def _(dve):
            LINKS = 5 + 3 * CHUNKS - 2
            dve.memset(best[:], NEG)
            dve.tensor_tensor(g.score[:], g.score[:],
                              g.ew[:].rearrange("p (c h) -> p c h", h=1).broadcast_to([P, COLS, HEADS]),
                              ALU.mult).then_inc(a_start, 1)
            dve.wait_ge(a_start, 1)
            steps = dve.value_load(g.apart_steps[0:1, 0:1], min_val=1, max_val=TABLE)
            with dve.Fori(0, steps) as i:
                link = [i * LINKS]

                def then(ins):
                    link[0] = link[0] + 1
                    ins.then_inc(a_link, 1)
                    dve.wait_ge(a_link, link[0])

                sc, w = step_of(nc, dve, g.code, i)
                then(one_hots(dve, g, hot[:], sc, w))
                then(dve.tensor_copy(s[:], g.score[:, bass.ds(sc * CHUNKS, CHUNKS), :]))
                then(dve.tensor_scalar(outside[:], hot[:], -NEG, NEG, ALU.mult, ALU.add))
                for c in range(CHUNKS):
                    out = most if c == 0 else mine
                    at = hot[:, c:c + 1, :].broadcast_to([P, HEADS, P])
                    score = s[:, c, :].rearrange("p (h a) -> p h a", a=1).broadcast_to([P, HEADS, P])
                    then(dve.tensor_tensor(out[:], at, score, ALU.mult))
                    ins = dve.tensor_tensor(out[:], out[:], outside[:, c:c + 1, :].broadcast_to([P, HEADS, P]),
                                            ALU.add)
                    then(ins)
                    if c > 0 and c < CHUNKS - 1:
                        then(dve.tensor_tensor(most[:], most[:], mine[:], ALU.max))
                dve.tensor_tensor(most[:], most[:], mine[:], ALU.max).then_inc(a_most, 1)
                dve.wait_ge(a_turn, i + 1)
                then(dve.tensor_reduce(step_best[:], ps_m[:], AX.X, ALU.max))
                rows = best[:, bass.ds(w, 1), :].rearrange("p a h -> p (a h)")
                then(dve.tensor_tensor(rows, rows, step_best[:], ALU.max))
            with dve.Fori(0, steps) as i:
                sc, w = step_of(nc, dve, g.code, i)
                one_hots(dve, g, hot[:], sc, w).then_inc(a_hot, 1)
                dve.wait_ge(a_hott, i + 1)
                dve.tensor_copy(hot_t[:], ps_h[:]).then_inc(a_out, 1)
                dve.wait_ge(a_max, i + 1)
                there = g.score[:, bass.ds(sc * CHUNKS, CHUNKS), :]
                dve.scalar_tensor_tensor(there, ps_b[:], g.unsorted[:], there, ALU.mult, ALU.add).then_inc(a_link2, 1)
                dve.wait_ge(a_link2, i + 1)


def stage_softmax(nc, g):
    with ExitStack() as ctx:
        def sb(name, shape, dt=F32):
            return ctx.enter_context(nc.sbuf_tensor(name, shape, dt))

        row = sb("row", [P, BLOCK_EDGES])
        top = sb("top", [P, BLOCK_EDGES])
        new = sb("new", [P, BLOCK_EDGES + 1])
        inner = sb("inner", [P, 1])
        has_start = sb("has_start", [P, 2])
        ends = sb("ends", [P, 2])
        ends_r = sb("ends_r", [1, 2, P])
        carry_r = sb("carry_r", [1, P])
        carry_c = sb("carry_c", [P, 1])
        one = sb("one", [1, 1])
        ps_r = ctx.enter_context(nc.psum_tensor("ps_r", [P, 4, 512], F32))
        ps_e = ctx.enter_context(nc.psum_tensor("ps_e4", [P, 512], F32))
        x_ew = ctx.enter_context(nc.semaphore("x_ew"))
        x_turn = ctx.enter_context(nc.semaphore("x_turn"))
        x_row = ctx.enter_context(nc.semaphore("x_row"))
        x_dve = ctx.enter_context(nc.semaphore("x_dve"))
        x_pe = ctx.enter_context(nc.semaphore("x_pe"))
        x_exp = ctx.enter_context(nc.semaphore("x_exp"))
        x_back = ctx.enter_context(nc.semaphore("x_back"))
        x_out = ctx.enter_context(nc.semaphore("x_out"))
        block = ctx.enter_context(nc.Block())
        GB = 4
        NG = -(-GROUPS // GB)

        def blocks(c):
            return top[:, c * P:(c + 1) * P]

        @block.tensor
        def _(pe):
            pe.wait_ge(x_ew, 1)
            for n in range(NG):
                if n >= 4:
                    pe.wait_ge(x_row, n - 3)
                for m in range(min(GB, GROUPS - n * GB)):
                    mm = pe.transpose(ps_r[:, n % 4, m * P:(m + 1) * P], blocks(n * GB + m), g.ident[:])
                mm.then_inc(x_turn, 1)
            for k in range(2):
                pe.wait_ge(x_pe, 2 * k + 1)
                pe.transpose(ps_e[0:1, 0:P], ends[:, 0:1], g.ident[:])
                pe.transpose(ps_e[0:1, P:2 * P], ends[:, 1:2], g.ident[:]).then_inc(x_turn, 1)
                pe.wait_ge(x_pe, 2 * k + 2)
                pe.matmul(ps_e[:, 256 + k:257 + k], carry_r[:], one[:], start=True, stop=True,
                          skip_group_check=True).then_inc(x_turn, 1)
            for n in range(NG):
                pe.wait_ge(x_exp, n + 1)
                if n >= 4:
                    pe.wait_ge(x_out, n - 3)
                for m in range(min(GB, GROUPS - n * GB)):
                    c = n * GB + m
                    mm = pe.transpose(ps_r[:, n % 4, m * P:(m + 1) * P], row[:, c * P:(c + 1) * P], g.ident[:])
                mm.then_inc(x_back, 1)

        @block.scalar
        def _(act):
            for n in range(NG):
                w = min(GB, GROUPS - n * GB) * P
                act.wait_ge(x_turn, n + 1)
                act.activation(row[:, n * GB * P:n * GB * P + w], ps_r[:, n % 4, 0:w],
                               ACT.Copy).then_inc(x_row, 1)
            for n in range(NG):
                act.wait_ge(x_dve, n + 1)
                w = min(GB, GROUPS - n * GB) * P
                cut = row[:, n * GB * P:n * GB * P + w]
                act.activation(cut, cut, ACT.Exp).then_inc(x_exp, 1)

        @block.vector
        def _(dve):
            chain = [0]
            link = ctx.enter_context(nc.semaphore("x_link"))

            def then(ins):
                chain[0] += 1
                ins.then_inc(link, 1)
                dve.wait_ge(link, chain[0])

            dve.memset(one[:], 1.0)
            dve.tensor_copy(top[:].rearrange("p (c b h) -> p b c h", b=BLOCKS, h=HEADS),
                            g.score[:].rearrange("p (b c) h -> p b c h", b=BLOCKS)).then_inc(x_ew, 1)
            then(dve.tensor_tensor(new[:], g.dst_r[:, 1:], g.dst_r[:, :-1], ALU.not_equal))
            then(dve.tensor_scalar(new[:], new[:], NEG, None, ALU.mult))
            then(dve.tensor_reduce(inner[:], new[:, 1:BLOCK_EDGES], AX.X, ALU.min))
            dve.tensor_tensor(has_start[:, 0:1], inner[:], new[:, 0:1], ALU.min)
            then(dve.tensor_tensor(has_start[:, 1:2], inner[:], new[:, BLOCK_EDGES:], ALU.min))
            dve.wait_ge(x_row, NG)
            start, nxt = new[:, 0:BLOCK_EDGES], new[:, 1:BLOCK_EDGES + 1]

            def sweep(data, pen, initial, out):
                then(dve.tensor_tensor_scan(out, pen, data, initial, ALU.add, ALU.max))

            for k, (data, pen, out) in enumerate(((row[:], start, top[:]),
                                                  (top[:][:, ::-1], nxt[:, ::-1], top[:][:, ::-1]))):
                sweep(data, pen, NEG, out)
                at = BLOCK_EDGES - 1 if k == 0 else 0
                dve.tensor_copy(ends[:, 1:2], has_start[:, k:k + 1])
                dve.tensor_copy(ends[:, 0:1], top[:, at:at + 1]).then_inc(x_pe, 1)
                dve.wait_ge(x_turn, NG + 2 * k + 1)
                then(dve.tensor_copy(ends_r[:], ps_e[0:1, 0:2 * P].rearrange("p (a b) -> p a b", a=2)))
                then(dve.memset(carry_r[:], NEG))
                for h in range(HEADS):
                    last = ends_r[:, 0, h::HEADS]
                    keep = ends_r[:, 1, h::HEADS]
                    take = carry_r[:, h::HEADS]
                    n = BLOCKS - 1
                    if k == 0:
                        last, keep, take = last[:, 0:n], keep[:, 0:n], take[:, 1:]
                    else:
                        last, keep, take = last[:, 1:][:, ::-1], keep[:, 1:][:, ::-1], take[:, 0:n][:, ::-1]
                    ins = dve.tensor_tensor_scan(take, keep, last, NEG, ALU.add, ALU.max)
                ins.then_inc(x_pe, 1)
                dve.wait_ge(x_turn, NG + 2 * k + 2)
                then(dve.tensor_copy(carry_c[:], ps_e[:, 256 + k:257 + k]))
                sweep(data, pen, carry_c[:], out)
            for n in range(NG):
                part = slice(n * GB * P, min((n + 1) * GB, GROUPS) * P)
                dve.scalar_tensor_tensor(row[:, part], top[:, part], g.sorted[:], row[:, part], ALU.mult,
                                         ALU.add).then_inc(x_dve, 1)
            for n in range(NG):
                m = min(GB, GROUPS - n * GB)
                dve.wait_ge(x_back, n + 1)
                where = g.score[:].rearrange("p (b c) h -> p c b h", b=BLOCKS)[:, n * GB:n * GB + m]
                dve.tensor_copy(where, ps_r[:, n % 4, 0:m * P].rearrange("p (c b h) -> p c b h", c=m, b=BLOCKS)
                                ).then_inc(x_out, 1)


def stage_values(nc, g):
    with ExitStack() as ctx:
        def sb(name, shape, dt=F32):
            return ctx.enter_context(nc.sbuf_tensor(name, shape, dt))

        idx = sb("idx5", [P, TURN, CHUNKS], I32)
        val = sb("val", [P, TURN, CHUNKS, HEADS, DH])
        hot = sb("hot5", [P, 2, CHUNKS, P])
        msg = sb("msg5", [P, 2, CHUNKS, D + HEADS])
        ps_a = ctx.enter_context(nc.psum_tensor("ps_a5", [P, 2, 512], F32))
        v_ahead = ctx.enter_context(nc.semaphore("v_ahead"))
        v_idx = [ctx.enter_context(nc.semaphore(f"v_idx{u}")) for u in range(TURN)]
        v_ask = ctx.enter_context(nc.semaphore("v_ask"))
        val_landed = [ctx.enter_context(nc.semaphore(f"v_val{u}")) for u in range(TURN)]
        v_land = ctx.enter_context(nc.semaphore("v_land"))
        v_p = ctx.enter_context(nc.semaphore("v_p"))
        v_msg = ctx.enter_context(nc.semaphore("v_msg"))
        v_sum = ctx.enter_context(nc.semaphore("v_sum"))
        v_acc = ctx.enter_context(nc.semaphore("v_acc"))
        v_clear = ctx.enter_context(nc.semaphore("v_clear"))
        block = ctx.enter_context(nc.Block())

        @block.sync
        def _(sp):
            def senders(s, u):
                sp.dma_start(idx[:, u, :], g.src_t[:, bass.ds(s * CHUNKS, CHUNKS)]).then_inc(v_idx[u], 16)

            for u in range(TURN):
                senders(u, u)
            sp.dma_start(g.w_o[:], g.Wo.rearrange("(k p) n -> p k n", p=P)).then_inc(v_ahead, 16)
            sp.dma_start(g.w_1[:], g.W1.rearrange("(k p) n -> p k n", p=P)).then_inc(v_ahead, 16)
            sp.dma_start(g.w_2[:], g.W2.rearrange("(k p) n -> p k n", p=P)).then_inc(v_ahead, 16)
            for tile, b, n in ((g.b_o, g.bo, D), (g.b_2, g.b2, D), (g.alpha_s, g.alpha, 1), (g.beta_s, g.beta, 1)):
                sp.dma_start(tile[:], b.rearrange("(a d) -> a d", a=1).broadcast_to([P, n])).then_inc(v_ahead, 16)
            sp.dma_start(g.ln2_gain[:], g.ln2_g).then_inc(v_ahead, 16)
            sp.dma_start(g.ln2_shift[:], g.ln2_b).then_inc(v_ahead, 16)
            sp.dma_start(g.b1_s[:], g.b1).then_inc(v_ahead, 16)
            with sp.Fori(1, SUPERS // TURN) as t:
                for u in range(TURN):
                    sp.wait_ge(v_land, (t - 1) * TURN + u + 1)
                    senders(t * TURN + u, u)
            sp.wait_ge(v_ahead, 16 * 10)

        @block.gpsimd
        def _(pool):
            pool.sem_inc(v_msg, TURN)

            def gather(u, count):
                pool.wait_ge(v_idx[u], count)
                pool.sem_inc(v_ask, 1)
                for c in range(CHUNKS):
                    pool.indirect_dma_start(
                        out=val[:, u, c, :, :].rearrange("p a b -> p (a b)"), out_offset=None, in_=g.v_rows,
                        in_offset=bass.IndirectOffsetOnAxis(ap=idx[:, u, c:c + 1], axis=0),
                    ).then_inc(val_landed[u], 16)

            def landed(u, count):
                pool.wait_ge(val_landed[u], count)
                pool.sem_inc(v_land, 1)

            for u in range(TURN):
                gather(u, 16)
                if u > 0:
                    landed(u - 1, 16 * CHUNKS)
            with pool.Fori(1, SUPERS // TURN) as t:
                for u in range(TURN):
                    steps = pool.value_load(g.starts[0:1, bass.ds(t * TURN + u, 1)], min_val=TURN,
                                            max_val=TABLE + TURN)
                    pool.wait_ge(v_msg, steps)
                    pool.sem_inc(v_ask, 1)
                    gather(u, (t + 1) * 16)
                    landed((u - 1) % TURN, t * (16 * CHUNKS) if u == 0 else (t + 1) * (16 * CHUNKS))
            landed(TURN - 1, 16 * CHUNKS * (SUPERS // TURN))

        @block.tensor
        def _(pe):
            turns = pe.value_load(g.turns[0:1, 0:1], min_val=0, max_val=MAX_TURNS)
            pe.wait_ge(v_clear, 1)
            with pe.Fori(0, turns) as t:
                for u in range(TURN):
                    i = t * TURN + u
                    pe.wait_ge(v_msg, i + 1 + TURN)
                    pe.wait_ge(v_acc, i + 1)
                    for c in range(CHUNKS):
                        mm = pe.matmul(ps_a[:, u % 2, 0:D + HEADS], hot[:, u % 2, c, :], msg[:, u % 2, c, :],
                                       start=(c == 0), stop=(c == CHUNKS - 1))
                    mm.then_inc(v_sum, 1)

        @block.vector
        def _(dve):
            dve.sem_inc(v_sum, 2)
            dve.sem_inc(v_acc, 1)
            dve.memset(ps_a[:], 0.0).then_inc(v_clear, 1)
            dve.wait_ge(v_clear, 1)
            turns = dve.value_load(g.turns[0:1, 0:1], min_val=0, max_val=MAX_TURNS)

            def add_sums(i, u, w):
                dve.wait_ge(v_sum, i + 2)
                dve.wait_ge(v_acc, i + 1)
                dve.tensor_tensor(g.acc[:, bass.ds(w, 1), :], g.acc[:, bass.ds(w, 1), :],
                                  ps_a[:, (u + 1) % 2:(u + 1) % 2 + 1, 0:D + HEADS], ALU.add).then_inc(v_acc, 1)

            with dve.Fori(0, turns) as t:
                for u in range(TURN):
                    i = t * TURN + u
                    sc, w = step_of(nc, dve, g.code, i)
                    if u == 0:
                        _sc, w_before = step_of(nc, dve, g.code_before, i)
                    m = msg[:, u % 2]
                    dve.wait_ge(v_sum, i + 1)
                    dve.tensor_copy(m[:, :, D:], g.score[:, bass.ds(sc * CHUNKS, CHUNKS), :]).then_inc(v_p, 1)
                    one_hots(dve, g, hot[:, u % 2], sc, w)
                    dve.wait_ge(v_p, i + 1)
                    dve.wait_ge(v_land, sc + 1)
                    slot = nc.s_assert_within(dve.snap(sc % TURN), 0, TURN - 1,
                                              skip_runtime_bounds_check_because="a remainder of TURN")
                    rows = val[:, bass.ds(slot, 1)].rearrange("p a c h d -> p (a c) h d")
                    p = m[:, :, D:].rearrange("p c (h d) -> p c h d", d=1).broadcast_to([P, CHUNKS, HEADS, DH])
                    dve.tensor_tensor(m[:, :, 0:D].rearrange("p c (h d) -> p c h d", h=HEADS), rows, p,
                                      ALU.mult).then_inc(v_msg, 1)
                    add_sums(i, u, w_before)
                    w_before = w
            _sc, w_before = step_of(nc, dve, g.code_before, turns * TURN)
            add_sums(turns * TURN, TURN, w_before)


def stage_output(nc, g):
    FT = FF // P
    HALF = FT // 2
    with ExitStack() as ctx:
        def sb(name, shape, dt=F32):
            return ctx.enter_context(nc.sbuf_tensor(name, shape, dt))

        den = sb("den", [P, HEADS])
        att = sb("att", [P, D])
        att_t = sb("att_t", [P, 2, P])
        t_o = sb("t_o", [P, D])
        x2 = sb("x2", [P, 2, D])
        stats = sb("stats6", [P, 2, 6])
        mv = sb("mv6", [P, 2, 2])
        dev = sb("dev6", [P, 2])
        rstd = sb("rstd6", [P, 2])
        eps = sb("eps6", [P, 1])
        xn = sb("xn6", [P, D])
        xn_t = sb("xn_t6", [P, 2, P])
        gel = sb("gel", [P, FT, P])
        y = sb("y6", [P, D])
        res = sb("res", [P, 2, D])
        spare = sb("spare6", [P, 1])
        ps_a = ctx.enter_context(nc.psum_tensor("ps_a6", [P, 512], F32))
        ps_o = ctx.enter_context(nc.psum_tensor("ps_o", [P, 512], F32))
        ps_n = ctx.enter_context(nc.psum_tensor("ps_n6", [P, 512], F32))
        ps_f = ctx.enter_context(nc.psum_tensor("ps_f", [P, FT, P], F32))
        ps_y = ctx.enter_context(nc.psum_tensor("ps_y", [P, 512], F32))
        o_st = [ctx.enter_context(nc.semaphore(f"o_st{u}")) for u in range(2)]
        o_att = ctx.enter_context(nc.semaphore("o_att"))
        o_turn = ctx.enter_context(nc.semaphore("o_turn"))
        o_attt = ctx.enter_context(nc.semaphore("o_attt"))
        o_o = ctx.enter_context(nc.semaphore("o_o"))
        o_xn = ctx.enter_context(nc.semaphore("o_xn"))
        o_turn2 = ctx.enter_context(nc.semaphore("o_turn2"))
        o_xnt = ctx.enter_context(nc.semaphore("o_xnt"))
        o_ff = ctx.enter_context(nc.semaphore("o_ff"))
        o_gel = ctx.enter_context(nc.semaphore("o_gel"))
        o_y = ctx.enter_context(nc.semaphore("o_y"))
        o_read = ctx.enter_context(nc.semaphore("o_read"))
        o_res = ctx.enter_context(nc.semaphore("o_res"))
        o_stat = [ctx.enter_context(nc.semaphore(f"o_stat{n}")) for n in range(2)]
        o_dev = [ctx.enter_context(nc.semaphore(f"o_dev{n}")) for n in range(2)]
        o_eps = ctx.enter_context(nc.semaphore("o_eps"))
        o_den = ctx.enter_context(nc.semaphore("o_den"))
        o_first = ctx.enter_context(nc.semaphore("o_first"))
        o_last = ctx.enter_context(nc.semaphore("o_last"))
        block = ctx.enter_context(nc.Block())

        @block.sync
        def _(sp):
            with sp.Fori(0, WINDOWS // 2) as t:
                for u in range(2):
                    w = t * 2 + u
                    sp.wait_ge(o_res, w + 1)
                    sp.dma_start(g.out[bass.ds(w * P, P), :], res[:, u, :]).then_inc(o_st[u], 16)
            for u in range(2):
                sp.wait_ge(o_st[u], 16 * (WINDOWS // 2 + 1))

        @block.scalar
        def _(act):
            def attention_out(w):
                act.wait_ge(o_turn, w + 1)
                act.activation(att_t[:].rearrange("p a b -> p (a b)"), ps_a[:, 0:D], ACT.Copy).then_inc(o_attt, 1)

            def normed_out(w):
                act.wait_ge(o_turn2, w + 1)
                for k in range(2):
                    ins = act.activation(xn_t[:, k, :], ps_n[:, k * P:(k + 1) * P], ACT.Identity,
                                         bias=g.ln2_shift[:, k:k + 1], scale=g.ln2_gain[:, k:k + 1])
                ins.then_inc(o_xnt, 1)

            def gelu(w, half):
                act.wait_ge(o_ff, w * 2 + half + 1)
                for f in range(half * HALF, (half + 1) * HALF):
                    ins = act.activation(gel[:, f, :], ps_f[:, f, :], ACT.Gelu, bias=g.b1_s[:, f:f + 1])
                ins.then_inc(o_gel, 1)

            def deviation(n, w):
                act.wait_ge(o_stat[n], w + 1)
                act.activation(dev[:, n:n + 1], mv[:, n, 1:2], ACT.Sqrt, bias=eps[:]).then_inc(o_dev[n], 1)

            act.wait_ge(o_eps, 1)
            attention_out(0)
            deviation(0, 0)
            normed_out(0)
            with act.Fori(0, WINDOWS) as w:
                attention_out(w + 1)
                gelu(w, 0)
                gelu(w, 1)
                deviation(0, w + 1)
                normed_out(w + 1)
                deviation(1, w)

        @block.tensor
        def _(pe):
            def turn_attention(w):
                pe.wait_ge(o_att, w + 1)
                for k in range(2):
                    mm = pe.transpose(ps_a[:, k * P:(k + 1) * P], att[:, k * P:(k + 1) * P], g.ident[:])
                mm.then_inc(o_turn, 1)

            def project(w):
                pe.wait_ge(o_attt, w + 1)
                for k in range(2):
                    mm = pe.matmul(ps_o[:, 0:D], att_t[:, k, :], g.w_o[:, k, :], start=(k == 0), stop=(k == 1))
                mm.then_inc(o_o, 1)

            def turn_normed(w):
                pe.wait_ge(o_xn, w + 1)
                for k in range(2):
                    mm = pe.transpose(ps_n[:, k * P:(k + 1) * P], xn[:, k * P:(k + 1) * P], g.ident[:])
                mm.then_inc(o_turn2, 1)

            def hidden(half):
                for f in range(half * HALF, (half + 1) * HALF):
                    for k in range(2):
                        mm = pe.matmul(ps_f[:, f, :], g.w_1[:, k, f * P:(f + 1) * P], xn_t[:, k, :],
                                       start=(k == 0), stop=(k == 1), skip_group_check=True)
                mm.then_inc(o_ff, 1)

            def output(fs):
                for f in fs:
                    mm = pe.matmul(ps_y[:, 0:D], gel[:, f, :], g.w_2[:, f, :], start=(f == 0), stop=(f == FT - 1),
                                   skip_group_check=True)
                return mm

            turn_attention(0)
            project(0)
            turn_normed(0)
            with pe.Fori(0, WINDOWS) as w:
                turn_attention(w + 1)
                pe.wait_ge(o_xnt, w + 1)
                hidden(0)
                hidden(1)
                project(w + 1)
                pe.wait_ge(o_read, w + 1)
                pe.wait_ge(o_gel, w * 2 + 1)
                output(range(HALF))
                pe.wait_ge(o_gel, w * 2 + 2)
                output(range(HALF, FT - 2))
                turn_normed(w + 1)
                output(range(FT - 2, FT)).then_inc(o_y, 1)

        @block.vector
        def _(dve):
            dve.sem_inc(o_read, 1)
            for u in range(2):
                dve.sem_inc(o_st[u], 16)
            dve.memset(eps[:], EPS).then_inc(o_eps, 1)
            FIRST, LAST = 4, 3

            def norm(n, w, of, to, then):
                then(dve.bn_stats(stats[:, n, :], of))
                dve.memset(spare[:], 0.0)
                dve.bn_aggr(mv[:, n, :], stats[:, n, :]).then_inc(o_stat[n], 1)
                dve.wait_ge(o_dev[n], w + 1)
                then(dve.reciprocal(rstd[:, n:n + 1], dev[:, n:n + 1]))
                return dve.tensor_scalar(to, of, mv[:, n, 0:1], rstd[:, n:n + 1], ALU.subtract, ALU.mult)

            def divide(w):
                now = g.acc[:, bass.ds(w, 1), :].rearrange("p a d -> p (a d)")
                dve.tensor_scalar(den[:], now[:, D:], TINY, None, ALU.max).then_inc(o_den, 1)
                dve.wait_ge(o_den, w * 2 + 1)
                dve.reciprocal(den[:], den[:]).then_inc(o_den, 1)
                dve.wait_ge(o_den, w * 2 + 2)
                dve.tensor_tensor(att[:].rearrange("p (h d) -> p h d", h=HEADS),
                                  now[:, 0:D].rearrange("p (h d) -> p h d", h=HEADS),
                                  den[:].rearrange("p (h d) -> p h d", d=1).broadcast_to([P, HEADS, DH]),
                                  ALU.mult).then_inc(o_att, 1)

            def attention(w, u):
                link = [w * FIRST]

                def then(ins):
                    link[0] = link[0] + 1
                    ins.then_inc(o_first, 1)
                    dve.wait_ge(o_first, link[0])

                x1 = g.x1[:, bass.ds(w, 1), :].rearrange("p a d -> p (a d)")
                dve.wait_ge(o_o, w + 1)
                then(dve.tensor_tensor(t_o[:], ps_o[:, 0:D], g.b_o[:], ALU.add))
                then(dve.scalar_tensor_tensor(x2[:, u, :], t_o[:], g.alpha_s[:], x1, ALU.mult, ALU.add))
                norm(0, w, x2[:, u, :], xn[:], then).then_inc(o_xn, 1)
                dve.tensor_tensor(x2[:, u, :], x2[:, u, :], x1, ALU.add)

            divide(0)
            attention(0, 0)
            divide(1)
            with dve.Fori(0, WINDOWS // 2) as t:
                for u in range(2):
                    w = t * 2 + u
                    link = [w * LAST]

                    def then(ins):
                        link[0] = link[0] + 1
                        ins.then_inc(o_last, 1)
                        dve.wait_ge(o_last, link[0])

                    attention(w + 1, (u + 1) % 2)
                    divide(w + 2)
                    dve.wait_ge(o_y, w + 1)
                    dve.tensor_tensor(y[:], ps_y[:, 0:D], g.b_2[:], ALU.add).then_inc(o_read, 1)
                    dve.wait_ge(o_read, w + 2)
                    then(dve.scalar_tensor_tensor(y[:], y[:], g.beta_s[:], x2[:, u, :], ALU.mult, ALU.add))
                    dve.wait_ge(o_st[u], t * 16 + 16)
                    ins = norm(1, w, y[:], res[:, u, :], then)
                    ins.then_inc(o_res, 1)


def build(nc, g):
    g.k_rows = nc.dram_tensor("k_rows", (NODES_PAD, D), F32).ap()
    g.v_rows = nc.dram_tensor("v_rows", (NODES_PAD, D), F32).ap()
    with ExitStack() as ctx:
        def sb(name, shape, dt=F32, within=ctx):
            return within.enter_context(nc.sbuf_tensor(name, shape, dt))

        g.ident = sb("ident", [P, P])
        g.ones = sb("ones", [P, P])
        g.iota_node = sb("iota_node", [P, (WINDOWS + 1) * P])
        codes = sb("codes", [1, TABLE + 1], I32)
        g.codes = codes
        g.code, g.code_before = codes[:, 1:TABLE + 1], codes[:, 0:TABLE]
        g.turns = sb("turns", [1, 1], I32)
        g.starts = sb("starts", [1, SUPERS], I32)
        g.apart_steps = sb("apart_steps", [1, 1], I32)
        g.sorted = sb("sorted", [P, 1])
        g.unsorted = sb("unsorted", [P, 1])
        g.src_i = sb("src_i", [P, COLS], I32)
        g.ew = sb("ew", [P, COLS])
        g.rec = sb("rec", [P, COLS, 4])
        g.acc = sb("acc", [P, WINDOWS + 2, D + HEADS])
        g.w1 = sb("w1", [P, 2 * NH])
        g.w2 = sb("w2", [2 * NH, 2, NPATH * MUL])
        g.lin = sb("lin", [P, 2, P])
        stage_tables(nc, g)
        stage_messages(nc, g)
        g.x1 = sb("x1", [P, WINDOWS + 1, D])
        g.score = sb("score", [P, COLS, HEADS])
        with ExitStack() as queries:
            g.q3 = sb("q3", [P, WINDOWS + 1, 3, D], BF16, within=queries)
            stage_project(nc, g)
            stage_scores(nc, g)
        with ExitStack() as runs:
            g.dst_r = sb("dst_r", [P, BLOCK_EDGES + 2], I32, within=runs)
            stage_apart(nc, g)
            stage_softmax(nc, g)
        g.w_o = sb("w_o", [P, 2, D])
        g.w_1 = sb("w_1", [P, 2, FF])
        g.w_2 = sb("w_2", [P, FF // P, D])
        g.b_o = sb("b_o", [P, D])
        g.b1_s = sb("b_1", [P, FF // P])
        g.b_2 = sb("b_2", [P, D])
        g.ln2_gain = sb("ln2_gain", [P, 2])
        g.ln2_shift = sb("ln2_shift", [P, 2])
        g.alpha_s = sb("alpha", [P, 1])
        g.beta_s = sb("beta", [P, 1])
        stage_values(nc, g)
        stage_output(nc, g)


def by_edge(a, fill):
    a = np.asarray(a)
    full = np.full((EDGES_PAD,) + a.shape[1:], fill, a.dtype)
    full[:EDGES] = a
    return np.ascontiguousarray(np.moveaxis(full.reshape((COLS, P) + a.shape[1:]), 0, 1))


def by_feature(a):
    a = np.asarray(a)
    full = np.zeros((a.shape[1], EDGES_PAD), a.dtype)
    full[:, :EDGES] = a.T
    return full


def by_half(a):
    rows = by_feature(a)
    return np.ascontiguousarray(rows.reshape(len(rows), SUPERS, 2, SUPER // 2).transpose(2, 0, 1, 3)
                                .reshape(2 * len(rows), EDGES_PAD // 2))


def kernel(**inputs):
    import concourse.bacc as bacc
    from concourse.bass_utils import run_bass_kernel_spmd

    order = np.concatenate([np.arange(MUL)] + [MUL + 3 * np.arange(MUL) + j for j in range(3)])
    a = {n: np.asarray(v) for n, v in inputs.items()}
    x = np.zeros((NODES_PAD + 2 * P, D), a["x"].dtype)
    x[:NODES] = a["x"][:, order]
    dst_row = np.full((EDGES_PAD + 2,), -1, a["dst"].dtype)
    dst_row[1:EDGES + 1] = a["dst"]
    l1 = {n[len("L1_gnn_"):]: v for n, v in a.items() if n.startswith("L1_gnn_")}
    columns = lambda v: np.ascontiguousarray(v.reshape(-1, P).T)
    laid = {
        "src_t": by_edge(a["src"], 0), "dst_t": by_edge(a["dst"], -1), "dst_row": dst_row,
        "vec_t": by_edge(a["edge_attr_3"], 0), "ew_t": by_edge(a["edge_weight"], 0),
        "emb_t": by_half(a["edge_attr_8"]), "ef_t": by_feature(a["edge_attr_64"]),
        "x_rows": x,
        "fc_w1": a["L0_gnn_fc_w1"], "fc_w2": a["L0_gnn_fc_w2"],
        "lin_w0": a["L0_gnn_lin_w0"], "lin_w1": a["L0_gnn_lin_w1"],
        "Wq": l1["Wq"][order], "Wk": l1["Wk"][order], "Wv": l1["Wv"][order],
        "bq": l1["bq"], "bk": l1["bk"], "bv": l1["bv"], "We": l1["We"], "be": l1["be"],
        "Wo": l1["Wo"][:, order], "bo": l1["bo"][order],
        "ln1_g": columns(l1["ln1_g"][order]), "ln1_b": columns(l1["ln1_b"][order]),
        "ln2_g": columns(l1["ln2_g"][order]), "ln2_b": columns(l1["ln2_b"][order]),
        "W1": l1["W1"][order], "b1": columns(l1["b1"]), "W2": l1["W2"][:, order], "b2": l1["b2"][order],
        "alpha": l1["alpha"], "beta": l1["beta"],
    }
    nc = bacc.Bacc("TRN2", target_bir_lowering=False, num_devices=1)
    dram = {name: nc.dram_tensor("in_" + name, v.shape, mybir.dt.from_np(v.dtype), kind="ExternalInput").ap()
            for name, v in laid.items()}
    g = Held()
    g.src_t = dram["src_t"]
    g.dst_t = dram["dst_t"]
    g.dst_row = dram["dst_row"]
    g.vec_t = dram["vec_t"]
    g.ew_t = dram["ew_t"]
    g.emb_t = dram["emb_t"]
    g.ef_t = dram["ef_t"]
    g.x_rows = dram["x_rows"]
    g.fc_w1 = dram["fc_w1"]
    g.fc_w2 = dram["fc_w2"]
    g.lin_w0 = dram["lin_w0"]
    g.lin_w1 = dram["lin_w1"]
    g.Wq = dram["Wq"]
    g.Wk = dram["Wk"]
    g.Wv = dram["Wv"]
    g.bq = dram["bq"]
    g.bk = dram["bk"]
    g.bv = dram["bv"]
    g.We = dram["We"]
    g.be = dram["be"]
    g.Wo = dram["Wo"]
    g.bo = dram["bo"]
    g.ln1_g = dram["ln1_g"]
    g.ln1_b = dram["ln1_b"]
    g.ln2_g = dram["ln2_g"]
    g.ln2_b = dram["ln2_b"]
    g.W1 = dram["W1"]
    g.b1 = dram["b1"]
    g.W2 = dram["W2"]
    g.b2 = dram["b2"]
    g.alpha = dram["alpha"]
    g.beta = dram["beta"]
    arrays = {"in_" + name: np.ascontiguousarray(v) for name, v in laid.items()}
    g.w_qkv, g.b_qkv = (g.Wq, g.Wk, g.Wv), (g.bq, g.bk, g.bv)
    g.out = nc.dram_tensor("out", (NODES_PAD, D), F32, kind="ExternalOutput").ap()
    build(nc, g)
    r = run_bass_kernel_spmd(nc, [arrays], core_ids=[0])
    got = r.results[0]["out"][:NODES]
    back = np.empty_like(got)
    back[:, order] = got
    return back
```
